# Optimizing a Trainium2 kernel written in Bass

```python
import numpy as np
import jax
import jax.numpy as jnp

def _softmax(x, axis=-1):
    return jax.nn.softmax(x, axis=axis)

def _gelu(x):
    return jax.nn.gelu(x, approximate=True)

def _silu(x):
    return jax.nn.silu(x)

def _sigmoid(x):
    return jax.nn.sigmoid(x)

def _layernorm(x, axis=-1, eps=1e-05):
    m = jnp.mean(x, axis=axis, keepdims=True)
    v = jnp.var(x, axis=axis, keepdims=True)
    return (x - m) / jnp.sqrt(v + eps)

def _scatter_add(tgt, idx, src, axis=0):
    return tgt.at[idx].add(src)

def _segment_sum(src, seg, n):
    return jax.ops.segment_sum(src, seg, n)
kernel_name = 'mk_seq_postln_d4_jaxref_r8_1f6f91'

def setup_inputs(seed: int=0):
    np.random.seed(seed)
    _w = jnp.asarray

    def _L0_attn_setup():
        import jax, jax.numpy as jnp
        import numpy as np
        EMBED_DIM = 128
        NUM_HEADS = 16
        HEAD_DIM = EMBED_DIM // NUM_HEADS

        def _sinusoid_pos_emb(seq_len, dim):
            pos = jnp.arange(seq_len, dtype=jnp.float32)
            idx = jnp.arange(dim // 2, dtype=jnp.float32)
            inv_freq = 1.0 / 10000.0 ** (2.0 * idx / dim)
            ang = pos[:, None] * inv_freq[None, :]
            return jnp.concatenate([jnp.sin(ang), jnp.cos(ang)], axis=-1)

        def _relative_shift(x):
            b, h, s, _ = x.shape
            x = jnp.pad(x, ((0, 0), (0, 0), (0, 0), (1, 0)))
            x = x.reshape(b, h, s + 1, s)
            return x[:, :, 1:, :].reshape(b, h, s, s)
        key = jax.random.key(seed)
        ks = jax.random.split(key, 12)
        D = EMBED_DIM
        sc = 1.0 / np.sqrt(D)
        inp = {'x': jax.random.normal(ks[0], (2, 256, D), dtype=jnp.float32)}
        for i, name in enumerate(['Wq', 'Wk', 'Wv', 'Wp', 'Wo']):
            inp[name] = jax.random.normal(ks[1 + i], (D, D), dtype=jnp.float32) * sc
            inp['b' + name[1].lower()] = jnp.zeros((D,), dtype=jnp.float32)
        inp['u'] = jax.random.normal(ks[6], (1, NUM_HEADS, 1, HEAD_DIM), dtype=jnp.float32) * 0.05
        inp['v'] = jax.random.normal(ks[7], (1, NUM_HEADS, 1, HEAD_DIM), dtype=jnp.float32) * 0.05
        return inp
    _L0_attn_in = _L0_attn_setup()

    def _L0_ffn_setup():
        import jax, jax.numpy as jnp
        import numpy as np
        DIM = 128

        def _reference_tuple_inner(x, W_r, W_k, W_v, mu_r, mu_k):
            B, T, C = x.shape
            x_prev = jnp.concatenate([jnp.zeros((B, 1, C), x.dtype), x[:, :-1, :]], axis=1)
            xr = mu_r * x + (1.0 - mu_r) * x_prev
            xk = mu_k * x + (1.0 - mu_k) * x_prev
            r = jax.nn.sigmoid(jnp.einsum('btc,dc->btd', xr, W_r))
            k = jnp.einsum('btc,dc->btd', xk, W_k)
            k_act = jnp.square(jax.nn.relu(k))
            out = r * jnp.einsum('btc,dc->btd', k_act, W_v)
            new_state = x[:, -1, :]
            return (out, new_state)
        key = jax.random.key(seed)
        ks = jax.random.split(key, 6)
        B, T, C = (8, 256, DIM)
        x = jax.random.normal(ks[0], (B, T, C), dtype=jnp.float32)
        s = 1.0 / np.sqrt(C)
        W_r = jax.random.uniform(ks[1], (C, C), jnp.float32, -s, s)
        W_k = jax.random.uniform(ks[2], (C, C), jnp.float32, -s, s)
        W_v = jax.random.uniform(ks[3], (C, C), jnp.float32, -s, s)
        mu_r = jax.random.uniform(ks[4], (C,), jnp.float32)
        mu_k = jax.random.uniform(ks[5], (C,), jnp.float32)
        return {'x': x, 'W_r': W_r, 'W_k': W_k, 'W_v': W_v, 'mu_r': mu_r, 'mu_k': mu_k}
    _L0_ffn_in = _L0_ffn_setup()

    def _L1_attn_setup():
        import jax, jax.numpy as jnp
        import numpy as np
        B, S, D_IN, D_Q, D_V, H = (2, 256, 128, 128, 128, 16)
        HD_Q, HD_V = (D_Q // H, D_V // H)
        SCALE = float(D_Q) ** 0.5
        key = jax.random.key(seed)
        k1, k2, k3, k4, k5 = jax.random.split(key, 5)
        return {'x': jax.random.normal(k1, (B, S, D_IN), dtype=jnp.float32), 'w_q': jax.random.normal(k2, (D_IN, D_Q), dtype=jnp.float32), 'w_k': jax.random.normal(k3, (D_IN, D_Q), dtype=jnp.float32), 'w_v': jax.random.normal(k4, (D_IN, D_V), dtype=jnp.float32), 'W_o': jax.random.normal(k5, (D_IN, D_V), dtype=jnp.float32)}
    _L1_attn_in = _L1_attn_setup()

    def _L1_ffn_setup():
        import jax, jax.numpy as jnp
        import numpy as np
        key = jax.random.key(seed)
        ks = jax.random.split(key, 5)
        B, Sq, M, E, H = (4, 256, 128, 8, 512)
        x = jax.random.normal(ks[0], (B, Sq, M), dtype=jnp.float32)
        wg = jax.random.normal(ks[1], (M, E), dtype=jnp.float32) * (1.0 / np.sqrt(M))
        w1 = jax.random.normal(ks[2], (E, M, H), dtype=jnp.float32) * (1.0 / np.sqrt(M))
        b1 = jnp.zeros((E, H), dtype=jnp.float32)
        w2 = jax.random.normal(ks[3], (E, H, M), dtype=jnp.float32) * (1.0 / np.sqrt(H))
        b2 = jnp.zeros((E, M), dtype=jnp.float32)
        return {'x': x, 'wg': wg, 'w1': w1, 'b1': b1, 'w2': w2, 'b2': b2}
    _L1_ffn_in = _L1_ffn_setup()

    def _L2_attn_setup():
        import jax, jax.numpy as jnp
        import numpy as np
        import math
        D_MODEL = 128
        key = jax.random.key(seed)
        ks = jax.random.split(key, 7)
        B, S, D = (4, 512, D_MODEL)
        s = 0.02
        return {'hidden_states': jax.random.normal(ks[0], (B, S, D), jnp.float32), 'Wq': jax.random.normal(ks[1], (D, D), jnp.float32) * s, 'bq': jnp.zeros((D,), jnp.float32), 'Wk': jax.random.normal(ks[2], (D, D), jnp.float32) * s, 'bk': jnp.zeros((D,), jnp.float32), 'Wv': jax.random.normal(ks[3], (D, D), jnp.float32) * s, 'bv': jnp.zeros((D,), jnp.float32)}
    _L2_attn_in = _L2_attn_setup()

    def _L2_ffn_setup():
        import jax, jax.numpy as jnp
        import numpy as np
        DIM = 128
        DEPTH = 6
        HEADS = 16
        DIM_HEAD = 64
        WINDOW = 32
        INNER = HEADS * DIM_HEAD
        DIM_INNER = int(DIM * 4 * 2 / 3)
        QK_SCALE = 8.0

        def shift_tokens(t):
            a, s = jnp.split(t, 2, -1)
            s = jnp.pad(s, ((0, 0), (1, 0), (0, 0)))[:, :-1]
            return jnp.concatenate([a, s], -1)

        def l2norm(t):
            return t / jnp.maximum(jnp.linalg.norm(t, axis=-1, keepdims=True), 1e-12)

        def rotate_half(x):
            x1, x2 = jnp.split(x, 2, -1)
            return jnp.concatenate([-x2, x1], -1)

        def rotary_tables(n):
            half = jnp.arange(0, DIM_HEAD, 2, dtype=jnp.float32)
            inv_freq = 1.0 / 10000.0 ** (half / DIM_HEAD)
            t = jnp.arange(n, dtype=jnp.float32)
            freqs = t[:, None] * inv_freq[None, :]
            freqs = jnp.concatenate([freqs, freqs], -1)
            base_scale = (half + 0.4 * DIM_HEAD) / (1.4 * DIM_HEAD)
            power = (t - n // 2) / (WINDOW // 2)
            scale = base_scale[None, :] ** power[:, None]
            scale = jnp.concatenate([scale, scale], -1)
            return (freqs, scale)

        def local_attention(q, k, v):
            b, h, n, d = q.shape
            w = WINDOW
            nw = n // w
            bq = q.reshape(b, h, nw, w, d)
            bk = k.reshape(b, h, nw, w, d)
            bv = v.reshape(b, h, nw, w, d)

            def look(t):
                p = jnp.pad(t, ((0, 0), (0, 0), (1, 0), (0, 0), (0, 0)))
                return jnp.concatenate([p[:, :, :nw], p[:, :, 1:]], axis=3)
            bk2, bv2 = (look(bk), look(bv))
            seq = jnp.arange(n).reshape(nw, w)
            seq_p = jnp.pad(seq, ((1, 0), (0, 0)), constant_values=-1)
            jt = jnp.concatenate([seq_p[:nw], seq_p[1:]], axis=1)
            it = seq[:, :, None]
            jb = jt[:, None, :]
            mask = (it < jb) | (it > jb + w) | (jb == -1)
            sim = jnp.einsum('bhwie,bhwje->bhwij', bq, bk2) * QK_SCALE
            sim = jnp.where(mask, -jnp.finfo(sim.dtype).max, sim)
            attn = jax.nn.softmax(sim, -1)
            out = jnp.einsum('bhwij,bhwje->bhwie', attn, bv2)
            return out.reshape(b, h, n, d)

        def attn_layer(x, Wqkv, qs, ksc, Wo):
            b, n, _ = x.shape
            qkv = x @ Wqkv
            q, k, v = jnp.split(qkv, 3, -1)
            sh = lambda t: t.reshape(b, n, HEADS, DIM_HEAD).transpose(0, 2, 1, 3)
            q, k, v = (sh(q), sh(k), sh(v))
            q = l2norm(q) * qs
            k = l2norm(k) * ksc
            freqs, scale = rotary_tables(n)
            cos, sin = (jnp.cos(freqs), jnp.sin(freqs))
            q = q * cos * scale + rotate_half(q) * sin * scale
            inv = 1.0 / scale
            k = k * cos * inv + rotate_half(k) * sin * inv
            out = local_attention(q, k, v)
            out = out.transpose(0, 2, 1, 3).reshape(b, n, INNER)
            return out @ Wo

        def ffn_layer(x, g, bln, W1, b1, W2, b2):
            mu = x.mean(-1, keepdims=True)
            var = ((x - mu) ** 2).mean(-1, keepdims=True)
            xn = (x - mu) / jnp.sqrt(var + 1e-05) * g + bln
            hg = xn @ W1 + b1
            a, gate = jnp.split(hg, 2, -1)
            return a * jax.nn.gelu(gate, approximate=False) @ W2 + b2
        key = jax.random.key(seed)
        ks = jax.random.split(key, 8)
        B, N = (2, 256)
        init = lambda k, shape: jax.random.normal(k, shape, jnp.float32) * 0.02
        return {'x': jax.random.normal(ks[0], (B, N, DIM), jnp.float32), 'Wqkv': init(ks[1], (DEPTH, DIM, 3 * INNER)), 'q_scale': jnp.ones((DEPTH, DIM_HEAD), jnp.float32), 'k_scale': jnp.ones((DEPTH, DIM_HEAD), jnp.float32), 'Wo': init(ks[2], (DEPTH, INNER, DIM)), 'ln_g': jnp.ones((DEPTH, DIM), jnp.float32), 'ln_b': jnp.zeros((DEPTH, DIM), jnp.float32), 'W1': init(ks[3], (DEPTH, DIM, 2 * DIM_INNER)), 'b1': jnp.zeros((DEPTH, 2 * DIM_INNER), jnp.float32), 'W2': init(ks[4], (DEPTH, DIM_INNER, DIM)), 'b2': jnp.zeros((DEPTH, DIM), jnp.float32)}
    _L2_ffn_in = _L2_ffn_setup()

    def _L3_attn_setup():
        import jax, jax.numpy as jnp
        import numpy as np
        from jax import lax
        DIM = 128
        HEADS = 16
        HEAD_DIM = DIM // HEADS
        BLOCK = 128
        DECAY = 0.9
        SPIKE_TH = 0.5
        K_WINNERS = 4
        HIDDEN = 4 * DIM
        EPS = 1e-05

        def _rmsnorm(x, w):
            norm = lax.rsqrt(jnp.mean(x * x, axis=-1, keepdims=True) + EPS)
            return w * x * norm

        def _spike_kwta(k):
            k = jnp.where(k > SPIKE_TH, k, 0.0)
            thr = lax.top_k(k, K_WINNERS)[0][..., -1:]
            return jnp.where(k >= thr, k, 0.0)

        def _mix(h, Wr, Wk, Wv, Wo):
            B, T, _ = h.shape
            N = T // BLOCK
            r = jax.nn.sigmoid((h @ Wr).reshape(B, T, HEADS, HEAD_DIM))
            k = _spike_kwta((h @ Wk).reshape(B, T, HEADS, HEAD_DIM))
            v = (h @ Wv).reshape(B, T, HEADS, HEAD_DIM)

            def chunks(a):
                return a.reshape(B, N, BLOCK, HEADS, HEAD_DIM).transpose(1, 0, 2, 3, 4)
            rc_all, kc_all, vc_all = (chunks(r), chunks(k), chunks(v))
            t_idx = jnp.arange(BLOCK, dtype=h.dtype)
            w_in = (DECAY ** (t_idx + 1.0))[None, :, None, None]
            w_out = (DECAY ** (BLOCK - 1.0 - t_idx))[None, :, None, None]
            lm = t_idx[:, None] - t_idx[None, :]
            mask = jnp.where(lm >= 0, DECAY ** lm, 0.0)
            w_L = DECAY ** BLOCK

            def step(S, inp):
                rc, kc, vc = inp
                inter = jnp.einsum('blhd,bhde->blhe', rc * w_in, S)
                A = jnp.einsum('blhd,bmhd->bhlm', rc, kc) * mask
                intra = jnp.einsum('bhlm,bmhe->blhe', A, vc)
                S_new = w_L * S + jnp.einsum('blhd,blhe->bhde', kc * w_out, vc)
                return (S_new, inter + intra)
            S0 = jnp.zeros((B, HEADS, HEAD_DIM, HEAD_DIM), h.dtype)
            _, y = lax.scan(step, S0, (rc_all, kc_all, vc_all))
            y = y.transpose(1, 0, 2, 3, 4).reshape(B, T, DIM)
            return y @ Wo
        key = jax.random.key(seed)
        ks = jax.random.split(key, 9)
        s = 0.02
        return {'x': jax.random.normal(ks[0], (2, 128, DIM), jnp.float32), 'norm1_w': jnp.ones((DIM,), jnp.float32), 'Wr': jax.random.normal(ks[1], (DIM, DIM), jnp.float32) * s, 'Wk': jax.random.normal(ks[2], (DIM, DIM), jnp.float32) * s + 0.5, 'Wv': jax.random.normal(ks[3], (DIM, DIM), jnp.float32) * s, 'Wo': jax.random.normal(ks[4], (DIM, DIM), jnp.float32) * s, 'norm2_w': jnp.ones((DIM,), jnp.float32), 'w1': jax.random.normal(ks[5], (DIM, HIDDEN), jnp.float32) * s, 'w2': jax.random.normal(ks[6], (DIM, HIDDEN), jnp.float32) * s, 'w3': jax.random.normal(ks[7], (HIDDEN, DIM), jnp.float32) * s}
    _L3_attn_in = _L3_attn_setup()

    def _L3_ffn_setup():
        import jax, jax.numpy as jnp
        import numpy as np
        DIM = 128

        def _reference_tuple_inner(x, W_r, W_k, W_v, mu_r, mu_k):
            B, T, C = x.shape
            x_prev = jnp.concatenate([jnp.zeros((B, 1, C), x.dtype), x[:, :-1, :]], axis=1)
            xr = mu_r * x + (1.0 - mu_r) * x_prev
            xk = mu_k * x + (1.0 - mu_k) * x_prev
            r = jax.nn.sigmoid(jnp.einsum('btc,dc->btd', xr, W_r))
            k = jnp.einsum('btc,dc->btd', xk, W_k)
            k_act = jnp.square(jax.nn.relu(k))
            out = r * jnp.einsum('btc,dc->btd', k_act, W_v)
            new_state = x[:, -1, :]
            return (out, new_state)
        key = jax.random.key(seed)
        ks = jax.random.split(key, 6)
        B, T, C = (8, 256, DIM)
        x = jax.random.normal(ks[0], (B, T, C), dtype=jnp.float32)
        s = 1.0 / np.sqrt(C)
        W_r = jax.random.uniform(ks[1], (C, C), jnp.float32, -s, s)
        W_k = jax.random.uniform(ks[2], (C, C), jnp.float32, -s, s)
        W_v = jax.random.uniform(ks[3], (C, C), jnp.float32, -s, s)
        mu_r = jax.random.uniform(ks[4], (C,), jnp.float32)
        mu_k = jax.random.uniform(ks[5], (C,), jnp.float32)
        return {'x': x, 'W_r': W_r, 'W_k': W_k, 'W_v': W_v, 'mu_r': mu_r, 'mu_k': mu_k}
    _L3_ffn_in = _L3_ffn_setup()
    _d = {'L0_attn_x': _L0_attn_in['x'], 'L0_attn_Wq': _L0_attn_in['Wq'], 'L0_attn_bq': _L0_attn_in['bq'], 'L0_attn_Wk': _L0_attn_in['Wk'], 'L0_attn_bk': _L0_attn_in['bk'], 'L0_attn_Wv': _L0_attn_in['Wv'], 'L0_attn_bv': _L0_attn_in['bv'], 'L0_attn_Wp': _L0_attn_in['Wp'], 'L0_attn_bp': _L0_attn_in['bp'], 'L0_attn_Wo': _L0_attn_in['Wo'], 'L0_attn_bo': _L0_attn_in['bo'], 'L0_attn_u': _L0_attn_in['u'], 'L0_attn_v': _L0_attn_in['v'], 'L0_ffn_W_r': _L0_ffn_in['W_r'], 'L0_ffn_W_k': _L0_ffn_in['W_k'], 'L0_ffn_W_v': _L0_ffn_in['W_v'], 'L0_ffn_mu_r': _L0_ffn_in['mu_r'], 'L0_ffn_mu_k': _L0_ffn_in['mu_k'], 'L1_attn_w_q': _L1_attn_in['w_q'], 'L1_attn_w_k': _L1_attn_in['w_k'], 'L1_attn_w_v': _L1_attn_in['w_v'], 'L1_attn_W_o': _L1_attn_in['W_o'], 'L1_ffn_wg': _L1_ffn_in['wg'], 'L1_ffn_w1': _L1_ffn_in['w1'], 'L1_ffn_b1': _L1_ffn_in['b1'], 'L1_ffn_w2': _L1_ffn_in['w2'], 'L1_ffn_b2': _L1_ffn_in['b2'], 'L2_attn_Wq': _L2_attn_in['Wq'], 'L2_attn_bq': _L2_attn_in['bq'], 'L2_attn_Wk': _L2_attn_in['Wk'], 'L2_attn_bk': _L2_attn_in['bk'], 'L2_attn_Wv': _L2_attn_in['Wv'], 'L2_attn_bv': _L2_attn_in['bv'], 'L2_ffn_Wqkv': _L2_ffn_in['Wqkv'], 'L2_ffn_q_scale': _L2_ffn_in['q_scale'], 'L2_ffn_k_scale': _L2_ffn_in['k_scale'], 'L2_ffn_Wo': _L2_ffn_in['Wo'], 'L2_ffn_ln_g': _L2_ffn_in['ln_g'], 'L2_ffn_ln_b': _L2_ffn_in['ln_b'], 'L2_ffn_W1': _L2_ffn_in['W1'], 'L2_ffn_b1': _L2_ffn_in['b1'], 'L2_ffn_W2': _L2_ffn_in['W2'], 'L2_ffn_b2': _L2_ffn_in['b2'], 'L3_attn_norm1_w': _L3_attn_in['norm1_w'], 'L3_attn_Wr': _L3_attn_in['Wr'], 'L3_attn_Wk': _L3_attn_in['Wk'], 'L3_attn_Wv': _L3_attn_in['Wv'], 'L3_attn_Wo': _L3_attn_in['Wo'], 'L3_attn_norm2_w': _L3_attn_in['norm2_w'], 'L3_attn_w1': _L3_attn_in['w1'], 'L3_attn_w2': _L3_attn_in['w2'], 'L3_attn_w3': _L3_attn_in['w3'], 'L3_ffn_W_r': _L3_ffn_in['W_r'], 'L3_ffn_W_k': _L3_ffn_in['W_k'], 'L3_ffn_W_v': _L3_ffn_in['W_v'], 'L3_ffn_mu_r': _L3_ffn_in['mu_r'], 'L3_ffn_mu_k': _L3_ffn_in['mu_k']}
    _x0 = _d['L0_attn_x']
    _d['L0_attn_x'] = jax.random.normal(jax.random.fold_in(jax.random.key(seed), 1), (8, 512, 128), dtype=_x0.dtype)
    del _x0
    return _d

def reference(L0_attn_x, L0_attn_Wq, L0_attn_bq, L0_attn_Wk, L0_attn_bk, L0_attn_Wv, L0_attn_bv, L0_attn_Wp, L0_attn_bp, L0_attn_Wo, L0_attn_bo, L0_attn_u, L0_attn_v, L0_ffn_W_r, L0_ffn_W_k, L0_ffn_W_v, L0_ffn_mu_r, L0_ffn_mu_k, L1_attn_w_q, L1_attn_w_k, L1_attn_w_v, L1_attn_W_o, L1_ffn_wg, L1_ffn_w1, L1_ffn_b1, L1_ffn_w2, L1_ffn_b2, L2_attn_Wq, L2_attn_bq, L2_attn_Wk, L2_attn_bk, L2_attn_Wv, L2_attn_bv, L2_ffn_Wqkv, L2_ffn_q_scale, L2_ffn_k_scale, L2_ffn_Wo, L2_ffn_ln_g, L2_ffn_ln_b, L2_ffn_W1, L2_ffn_b1, L2_ffn_W2, L2_ffn_b2, L3_attn_norm1_w, L3_attn_Wr, L3_attn_Wk, L3_attn_Wv, L3_attn_Wo, L3_attn_norm2_w, L3_attn_w1, L3_attn_w2, L3_attn_w3, L3_ffn_W_r, L3_ffn_W_k, L3_ffn_W_v, L3_ffn_mu_r, L3_ffn_mu_k):

    def _L0_attn_ref(x, Wq, bq, Wk, bk, Wv, bv, Wp, bp, Wo, bo, u, v):
        import jax, jax.numpy as jnp
        import numpy as np
        EMBED_DIM = 128
        NUM_HEADS = 16
        HEAD_DIM = EMBED_DIM // NUM_HEADS

        def _sinusoid_pos_emb(seq_len, dim):
            pos = jnp.arange(seq_len, dtype=jnp.float32)
            idx = jnp.arange(dim // 2, dtype=jnp.float32)
            inv_freq = 1.0 / 10000.0 ** (2.0 * idx / dim)
            ang = pos[:, None] * inv_freq[None, :]
            return jnp.concatenate([jnp.sin(ang), jnp.cos(ang)], axis=-1)

        def _relative_shift(x):
            b, h, s, _ = x.shape
            x = jnp.pad(x, ((0, 0), (0, 0), (0, 0), (1, 0)))
            x = x.reshape(b, h, s + 1, s)
            return x[:, :, 1:, :].reshape(b, h, s, s)
        B, S, D = x.shape
        H, P = (NUM_HEADS, HEAD_DIM)

        def heads(t):
            return t.reshape(B, S, H, P).transpose(0, 2, 1, 3)
        q = heads(x @ Wq + bq)
        k = heads(x @ Wk + bk)
        val = heads(x @ Wv + bv)
        pos = _sinusoid_pos_emb(S, D) @ Wp + bp
        pos = pos.reshape(S, H, P).transpose(1, 0, 2)
        content_score = jnp.einsum('bhsp,bhtp->bhst', q + u, k)
        pos_score = jnp.einsum('bhsp,htp->bhst', q + v, pos)
        pos_score = _relative_shift(pos_score)
        score = (content_score + pos_score) / jnp.sqrt(jnp.float32(P))
        weights = jax.nn.softmax(score, axis=-1)
        out = jnp.einsum('bhst,bhtp->bhsp', weights, val)
        out = out.transpose(0, 2, 1, 3).reshape(B, S, D)
        return out @ Wo + bo

    def _L0_ffn_ref(x, W_r, W_k, W_v, mu_r, mu_k):
        import jax, jax.numpy as jnp
        import numpy as np
        DIM = 128

        def _reference_tuple_inner(x, W_r, W_k, W_v, mu_r, mu_k):
            B, T, C = x.shape
            x_prev = jnp.concatenate([jnp.zeros((B, 1, C), x.dtype), x[:, :-1, :]], axis=1)
            xr = mu_r * x + (1.0 - mu_r) * x_prev
            xk = mu_k * x + (1.0 - mu_k) * x_prev
            r = jax.nn.sigmoid(jnp.einsum('btc,dc->btd', xr, W_r))
            k = jnp.einsum('btc,dc->btd', xk, W_k)
            k_act = jnp.square(jax.nn.relu(k))
            out = r * jnp.einsum('btc,dc->btd', k_act, W_v)
            new_state = x[:, -1, :]
            return (out, new_state)
        return _reference_tuple_inner(x, W_r, W_k, W_v, mu_r, mu_k)[0]

    def _L1_attn_ref(x, w_q, w_k, w_v, W_o):
        import jax, jax.numpy as jnp
        import numpy as np
        B, S, D_IN, D_Q, D_V, H = (2, 256, 128, 128, 128, 16)
        HD_Q, HD_V = (D_Q // H, D_V // H)
        SCALE = float(D_Q) ** 0.5
        b, s, _ = x.shape
        q = x @ w_q
        k = x @ w_k
        v = x @ w_v
        Q = q.reshape(b, s, H, HD_Q).transpose(0, 2, 1, 3)
        K = k.reshape(b, s, H, HD_Q).transpose(0, 2, 1, 3)
        V = v.reshape(b, s, H, HD_V).transpose(0, 2, 1, 3)
        scores = jnp.einsum('bhqd,bhkd->bhqk', Q, K)
        attn = jax.nn.softmax(scores / SCALE, axis=0)
        vals = jnp.einsum('bhqk,bhkd->bhqd', attn, V)
        vals = vals.transpose(0, 2, 1, 3).reshape(b, s, D_V)
        return vals @ W_o

    def _L1_ffn_ref(x, wg, w1, b1, w2, b2):
        import jax, jax.numpy as jnp
        import numpy as np
        B, Sq, M = x.shape
        E = wg.shape[1]
        S = B * Sq
        C = S // E
        xt = x.reshape(S, M)
        gates = jax.nn.softmax(xt @ wg, axis=-1)
        expert_idx = jnp.argmax(gates, axis=-1)
        mask1 = jax.nn.one_hot(expert_idx, E, dtype=xt.dtype)
        locations = jnp.cumsum(mask1, axis=0) - 1.0
        pos = jnp.sum(locations * mask1, axis=1).astype(jnp.int32)
        keep = (pos < C).astype(xt.dtype)
        gate_val = jnp.sum(gates * mask1, axis=1) * keep
        slot = expert_idx.astype(jnp.int32) * C + jnp.clip(pos, 0, C - 1)
        disp = jnp.zeros((E * C, M), dtype=xt.dtype).at[slot].add(xt * keep[:, None])
        disp = disp.reshape(E, C, M)
        h = jax.nn.relu(jnp.einsum('ecm,emh->ech', disp, w1) + b1[:, None, :])
        eo = jnp.einsum('ech,ehm->ecm', h, w2) + b2[:, None, :]
        out = eo.reshape(E * C, M)[slot] * gate_val[:, None]
        return out.reshape(B, Sq, M)

    def _L2_attn_ref(hidden_states, Wq, bq, Wk, bk, Wv, bv):
        import jax, jax.numpy as jnp
        import numpy as np
        import math
        D_MODEL = 128
        D = hidden_states.shape[-1]
        scale = 1.0 / math.sqrt(D)
        q = hidden_states @ Wq.T + bq
        k = hidden_states @ Wk.T + bk
        v = hidden_states @ Wv.T + bv
        q = jax.nn.softmax(q, axis=-1)
        k = jax.nn.softmax(k, axis=-2) * scale
        v = jax.nn.softmax(v, axis=-2)
        attn = jnp.einsum('bqd,bkd->bqk', q, k)
        out = jnp.einsum('bqk,bkd->bqd', attn, v)
        return out

    def _L2_ffn_ref(x, Wqkv, q_scale, k_scale, Wo, ln_g, ln_b, W1, b1, W2, b2):
        import jax, jax.numpy as jnp
        import numpy as np
        DIM = 128
        DEPTH = 6
        HEADS = 16
        DIM_HEAD = 64
        WINDOW = 32
        INNER = HEADS * DIM_HEAD
        DIM_INNER = int(DIM * 4 * 2 / 3)
        QK_SCALE = 8.0

        def shift_tokens(t):
            a, s = jnp.split(t, 2, -1)
            s = jnp.pad(s, ((0, 0), (1, 0), (0, 0)))[:, :-1]
            return jnp.concatenate([a, s], -1)

        def l2norm(t):
            return t / jnp.maximum(jnp.linalg.norm(t, axis=-1, keepdims=True), 1e-12)

        def rotate_half(x):
            x1, x2 = jnp.split(x, 2, -1)
            return jnp.concatenate([-x2, x1], -1)

        def rotary_tables(n):
            half = jnp.arange(0, DIM_HEAD, 2, dtype=jnp.float32)
            inv_freq = 1.0 / 10000.0 ** (half / DIM_HEAD)
            t = jnp.arange(n, dtype=jnp.float32)
            freqs = t[:, None] * inv_freq[None, :]
            freqs = jnp.concatenate([freqs, freqs], -1)
            base_scale = (half + 0.4 * DIM_HEAD) / (1.4 * DIM_HEAD)
            power = (t - n // 2) / (WINDOW // 2)
            scale = base_scale[None, :] ** power[:, None]
            scale = jnp.concatenate([scale, scale], -1)
            return (freqs, scale)

        def local_attention(q, k, v):
            b, h, n, d = q.shape
            w = WINDOW
            nw = n // w
            bq = q.reshape(b, h, nw, w, d)
            bk = k.reshape(b, h, nw, w, d)
            bv = v.reshape(b, h, nw, w, d)

            def look(t):
                p = jnp.pad(t, ((0, 0), (0, 0), (1, 0), (0, 0), (0, 0)))
                return jnp.concatenate([p[:, :, :nw], p[:, :, 1:]], axis=3)
            bk2, bv2 = (look(bk), look(bv))
            seq = jnp.arange(n).reshape(nw, w)
            seq_p = jnp.pad(seq, ((1, 0), (0, 0)), constant_values=-1)
            jt = jnp.concatenate([seq_p[:nw], seq_p[1:]], axis=1)
            it = seq[:, :, None]
            jb = jt[:, None, :]
            mask = (it < jb) | (it > jb + w) | (jb == -1)
            sim = jnp.einsum('bhwie,bhwje->bhwij', bq, bk2) * QK_SCALE
            sim = jnp.where(mask, -jnp.finfo(sim.dtype).max, sim)
            attn = jax.nn.softmax(sim, -1)
            out = jnp.einsum('bhwij,bhwje->bhwie', attn, bv2)
            return out.reshape(b, h, n, d)

        def attn_layer(x, Wqkv, qs, ksc, Wo):
            b, n, _ = x.shape
            qkv = x @ Wqkv
            q, k, v = jnp.split(qkv, 3, -1)
            sh = lambda t: t.reshape(b, n, HEADS, DIM_HEAD).transpose(0, 2, 1, 3)
            q, k, v = (sh(q), sh(k), sh(v))
            q = l2norm(q) * qs
            k = l2norm(k) * ksc
            freqs, scale = rotary_tables(n)
            cos, sin = (jnp.cos(freqs), jnp.sin(freqs))
            q = q * cos * scale + rotate_half(q) * sin * scale
            inv = 1.0 / scale
            k = k * cos * inv + rotate_half(k) * sin * inv
            out = local_attention(q, k, v)
            out = out.transpose(0, 2, 1, 3).reshape(b, n, INNER)
            return out @ Wo

        def ffn_layer(x, g, bln, W1, b1, W2, b2):
            mu = x.mean(-1, keepdims=True)
            var = ((x - mu) ** 2).mean(-1, keepdims=True)
            xn = (x - mu) / jnp.sqrt(var + 1e-05) * g + bln
            hg = xn @ W1 + b1
            a, gate = jnp.split(hg, 2, -1)
            return a * jax.nn.gelu(gate, approximate=False) @ W2 + b2
        for i in range(DEPTH):
            x = attn_layer(shift_tokens(x), Wqkv[i], q_scale[i], k_scale[i], Wo[i]) + x
            x = ffn_layer(shift_tokens(x), ln_g[i], ln_b[i], W1[i], b1[i], W2[i], b2[i]) + x
        return x

    def _L3_attn_ref(x, norm1_w, Wr, Wk, Wv, Wo, norm2_w, w1, w2, w3):
        import jax, jax.numpy as jnp
        import numpy as np
        from jax import lax
        DIM = 128
        HEADS = 16
        HEAD_DIM = DIM // HEADS
        BLOCK = 128
        DECAY = 0.9
        SPIKE_TH = 0.5
        K_WINNERS = 4
        HIDDEN = 4 * DIM
        EPS = 1e-05

        def _rmsnorm(x, w):
            norm = lax.rsqrt(jnp.mean(x * x, axis=-1, keepdims=True) + EPS)
            return w * x * norm

        def _spike_kwta(k):
            k = jnp.where(k > SPIKE_TH, k, 0.0)
            thr = lax.top_k(k, K_WINNERS)[0][..., -1:]
            return jnp.where(k >= thr, k, 0.0)

        def _mix(h, Wr, Wk, Wv, Wo):
            B, T, _ = h.shape
            N = T // BLOCK
            r = jax.nn.sigmoid((h @ Wr).reshape(B, T, HEADS, HEAD_DIM))
            k = _spike_kwta((h @ Wk).reshape(B, T, HEADS, HEAD_DIM))
            v = (h @ Wv).reshape(B, T, HEADS, HEAD_DIM)

            def chunks(a):
                return a.reshape(B, N, BLOCK, HEADS, HEAD_DIM).transpose(1, 0, 2, 3, 4)
            rc_all, kc_all, vc_all = (chunks(r), chunks(k), chunks(v))
            t_idx = jnp.arange(BLOCK, dtype=h.dtype)
            w_in = (DECAY ** (t_idx + 1.0))[None, :, None, None]
            w_out = (DECAY ** (BLOCK - 1.0 - t_idx))[None, :, None, None]
            lm = t_idx[:, None] - t_idx[None, :]
            mask = jnp.where(lm >= 0, DECAY ** lm, 0.0)
            w_L = DECAY ** BLOCK

            def step(S, inp):
                rc, kc, vc = inp
                inter = jnp.einsum('blhd,bhde->blhe', rc * w_in, S)
                A = jnp.einsum('blhd,bmhd->bhlm', rc, kc) * mask
                intra = jnp.einsum('bhlm,bmhe->blhe', A, vc)
                S_new = w_L * S + jnp.einsum('blhd,blhe->bhde', kc * w_out, vc)
                return (S_new, inter + intra)
            S0 = jnp.zeros((B, HEADS, HEAD_DIM, HEAD_DIM), h.dtype)
            _, y = lax.scan(step, S0, (rc_all, kc_all, vc_all))
            y = y.transpose(1, 0, 2, 3, 4).reshape(B, T, DIM)
            return y @ Wo
        x = x + _mix(_rmsnorm(x, norm1_w), Wr, Wk, Wv, Wo)
        h = _rmsnorm(x, norm2_w)
        x = x + jax.nn.silu(h @ w1) * (h @ w2) @ w3
        return x

    def _L3_ffn_ref(x, W_r, W_k, W_v, mu_r, mu_k):
        import jax, jax.numpy as jnp
        import numpy as np
        DIM = 128

        def _reference_tuple_inner(x, W_r, W_k, W_v, mu_r, mu_k):
            B, T, C = x.shape
            x_prev = jnp.concatenate([jnp.zeros((B, 1, C), x.dtype), x[:, :-1, :]], axis=1)
            xr = mu_r * x + (1.0 - mu_r) * x_prev
            xk = mu_k * x + (1.0 - mu_k) * x_prev
            r = jax.nn.sigmoid(jnp.einsum('btc,dc->btd', xr, W_r))
            k = jnp.einsum('btc,dc->btd', xk, W_k)
            k_act = jnp.square(jax.nn.relu(k))
            out = r * jnp.einsum('btc,dc->btd', k_act, W_v)
            new_state = x[:, -1, :]
            return (out, new_state)
        return _reference_tuple_inner(x, W_r, W_k, W_v, mu_r, mu_k)[0]
    x = L0_attn_x
    x = _layernorm(x + _L0_attn_ref(x, L0_attn_Wq, L0_attn_bq, L0_attn_Wk, L0_attn_bk, L0_attn_Wv, L0_attn_bv, L0_attn_Wp, L0_attn_bp, L0_attn_Wo, L0_attn_bo, L0_attn_u, L0_attn_v), axis=-1)
    x = _layernorm(x + _L0_ffn_ref(x, L0_ffn_W_r, L0_ffn_W_k, L0_ffn_W_v, L0_ffn_mu_r, L0_ffn_mu_k), axis=-1)
    x = _layernorm(x + _L1_attn_ref(x, L1_attn_w_q, L1_attn_w_k, L1_attn_w_v, L1_attn_W_o), axis=-1)
    x = _layernorm(x + _L1_ffn_ref(x, L1_ffn_wg, L1_ffn_w1, L1_ffn_b1, L1_ffn_w2, L1_ffn_b2), axis=-1)
    x = _layernorm(x + _L2_attn_ref(x, L2_attn_Wq, L2_attn_bq, L2_attn_Wk, L2_attn_bk, L2_attn_Wv, L2_attn_bv), axis=-1)
    x = _layernorm(x + _L2_ffn_ref(x, L2_ffn_Wqkv, L2_ffn_q_scale, L2_ffn_k_scale, L2_ffn_Wo, L2_ffn_ln_g, L2_ffn_ln_b, L2_ffn_W1, L2_ffn_b1, L2_ffn_W2, L2_ffn_b2), axis=-1)
    x = _layernorm(x + _L3_attn_ref(x, L3_attn_norm1_w, L3_attn_Wr, L3_attn_Wk, L3_attn_Wv, L3_attn_Wo, L3_attn_norm2_w, L3_attn_w1, L3_attn_w2, L3_attn_w3), axis=-1)
    x = _layernorm(x + _L3_ffn_ref(x, L3_ffn_W_r, L3_ffn_W_k, L3_ffn_W_v, L3_ffn_mu_r, L3_ffn_mu_k), axis=-1)
    return x

_drawn_inputs = setup_inputs


def setup_inputs(seed=0):
    import zlib

    import numpy as np

    out = dict(_drawn_inputs(seed))
    spreads = {'L0_attn_bq': (0.0, 0.1),
     'L0_attn_bk': (0.0, 0.8),
     'L0_attn_bv': (0.0, 0.1),
     'L0_attn_bp': (0.0, 0.279),
     'L0_attn_bo': (0.0, 0.1),
     'L1_ffn_b1': (0.0, 0.407),
     'L1_ffn_b2': (0.0, 0.289),
     'L2_attn_bq': (0.0, 0.8),
     'L2_attn_bk': (0.0, 0.8),
     'L2_attn_bv': (0.0, 0.8),
     'L2_ffn_q_scale': (1.0, 0.6),
     'L2_ffn_k_scale': (1.0, 0.6),
     'L2_ffn_ln_g': (1.0, 0.6),
     'L2_ffn_ln_b': (0.0, 0.8),
     'L2_ffn_b1': (0.0, 0.8),
     'L2_ffn_b2': (0.0, 0.1),
     'L3_attn_norm1_w': (1.0, 0.2),
     'L3_attn_norm2_w': (1.0, 0.6)}
    factors = {'L0_attn_v': 4.607,
     'L2_attn_Wq': 8.0,
     'L2_attn_Wk': 8.0,
     'L2_attn_Wv': 8.0,
     'L2_ffn_W1': 3.645,
     'L2_ffn_W2': 3.593,
     'L3_attn_Wr': 3.191,
     'L3_attn_w1': 8.0,
     'L3_attn_w2': 8.0,
     'L3_attn_w3': 8.0,
     'L3_ffn_mu_r': 7.454}
    for name, (base, spread) in spreads.items():
        noise = np.random.default_rng([zlib.crc32(name.encode()), seed]).standard_normal(out[name].shape)
        drawn = base * np.exp(spread * noise) if base else spread * noise
        out[name] = jnp.asarray(drawn.astype(out[name].dtype))
    for name, factor in factors.items():
        out[name] = (out[name] * factor).astype(out[name].dtype)
    return out
```

```python
import numpy as np

import concourse.bass as bass
from concourse import mybir

F32 = mybir.dt.float32
ALU = mybir.AluOpType
ACT = mybir.ActivationFunctionType
AX = mybir.AxisListType
ts, ds = bass.ts, bass.ds

P = 128
B, S = 8, 512
T = B * S
NT = T // P
TB = S // P
H = 16
HD = P // H
EPS = 1e-5


class Model:
    pass


def places(nc, tag):
    def sb(name, shape, dt=F32):
        return nc.alloc_sbuf_tensor(f"{tag}_{name}", shape, dt)

    def ps(name, shape, dt=F32):
        return nc.alloc_psum_tensor(f"{tag}_{name}_psum", shape, dt)

    def sem(name):
        return nc.alloc_semaphore(f"{tag}_{name}")
    return sb, ps, sem


LN_EXP = "natural_log_exp_and_others"


def layer_norm(nc, m, tag, src=None, dst=None):
    src, dst = src or m.zt, dst or m.xt
    with nc.cleanup_on_exit():
        sb, ps, sem = places(nc, tag)
        mean_ps = [ps(f"mean{u}", [P, S]) for u in range(2)]
        var_ps = [ps(f"var{u}", [P, S]) for u in range(2)]
        cent = [sb(f"cent{u}", [P, S]) for u in range(2)]
        sq = [sb(f"sq{u}", [P, S]) for u in range(2)]
        ln = [sb(f"ln{u}", [P, S]) for u in range(2)]
        rstd = [sb(f"rstd{u}", [P, S]) for u in range(2)]
        mean_ready, cent_ready, sq_ready, var_ready, ln_ready, rstd_ready, x_ready = (
            sem(n) for n in ("mean_ready", "cent_ready", "sq_ready", "var_ready", "ln_ready", "rstd_ready", "x_ready"))
        with nc.Block() as block:
            @block.tensor
            def _(pe):
                with pe.Fori(0, B // 2) as pair:
                    b = 2 * pair
                    for u in range(2):
                        pe.wait_ge(cent_ready, b)
                        nc.tensor.matmul(mean_ps[u][:], m.mean_w[:], src[:, ts(b + u, S)],
                                         start=True, stop=True).then_inc(mean_ready, 1)
                    for u in range(2):
                        pe.wait_ge(sq_ready, b + u + 1)
                        pe.wait_ge(ln_ready, b)
                        nc.tensor.matmul(var_ps[u][:], m.mean_w[:], sq[u][:],
                                         start=True, stop=True).then_inc(var_ready, 1)

            @block.scalar
            def _(act):
                nc.scalar.preload_act_table_set(LN_EXP)
                with act.Fori(0, B // 2) as pair:
                    b = 2 * pair
                    for u in range(2):
                        act.wait_ge(cent_ready, b + u + 1)
                        act.wait_ge(var_ready, b)
                        nc.scalar.activation(sq[u][:], cent[u][:], ACT.Square).then_inc(sq_ready, 1)
                    for u in range(2):
                        act.wait_ge(var_ready, b + u + 1)
                        nc.scalar.activation(ln[u][:], var_ps[u][:], ACT.Ln, bias=m.eps[:]).then_inc(ln_ready, 1)
                    for u in range(2):
                        act.wait_ge(ln_ready, b + u + 1)
                        act.wait_ge(x_ready, b)
                        nc.scalar.activation(rstd[u][:], ln[u][:], ACT.Exp, scale=-0.5).then_inc(rstd_ready, 1)

            @block.vector
            def _(dve):
                with dve.Fori(0, B // 2) as pair:
                    b = 2 * pair
                    for u in range(2):
                        dve.wait_ge(mean_ready, b + u + 1)
                        dve.wait_ge(x_ready, b)
                        nc.vector.tensor_tensor(cent[u][:], src[:, ts(b + u, S)], mean_ps[u][:],
                                                ALU.subtract).then_inc(cent_ready, 1)
                    for u in range(2):
                        dve.wait_ge(rstd_ready, b + u + 1)
                        dve.wait_ge(cent_ready, b + u + 1)
                        nc.vector.tensor_tensor(dst[:, ts(b + u, S)], cent[u][:], rstd[u][:],
                                                ALU.mult).then_inc(x_ready, 1)


def channel_mix(nc, m, tag, w_rT, w_kT, w_vT, mu_r, mu_k):
    with nc.cleanup_on_exit():
        sb, ps, sem = places(nc, tag)
        wr, wk, wv = (sb(n, [P, P]) for n in ("wr", "wk", "wv"))
        mu = sb("mu", [P, 2])
        onemu = sb("onemu", [P, 2])
        prev = [[sb(f"prev{i}{u}", [P, S]) for u in range(2)] for i in range(2)]
        mix = [[sb(f"mix{i}{u}", [P, S]) for u in range(2)] for i in range(2)]
        gate, kk, ksq, rv = ([sb(f"{n}{u}", [P, S]) for u in range(2)] for n in ("gate", "kk", "ksq", "rv"))
        r_ps, k_ps, v_ps = ([ps(f"{n}{u}", [P, S]) for u in range(2)] for n in ("r", "k", "v"))
        loaded, onemu_ready, edge_ready, prev_ready, mix_ready, r_ready, k_ready, gate_ready, relu_ready, \
            ksq_ready, v_ready, rv_ready, z_ready = (sem(n) for n in (
                "loaded", "onemu_ready", "edge_ready", "prev_ready", "mix_ready", "r_ready", "k_ready", "gate_ready",
                "relu_ready", "ksq_ready", "v_ready", "rv_ready", "z_ready"))
        with nc.Block() as block:
            @block.sync
            def _(sp):
                sp.dma_start(mu[:, 0:1], mu_r).then_inc(loaded, 16)
                sp.dma_start(mu[:, 1:2], mu_k).then_inc(loaded, 16)
                for dst, src in ((wr, w_rT), (wk, w_kT), (wv, w_vT)):
                    sp.dma_start(dst[:], src).then_inc(loaded, 16)

            @block.gpsimd
            def _(pool):
                for i in range(2):
                    for u in range(2):
                        nc.gpsimd.memset(prev[i][u][:, 0:1], 0.0).then_inc(edge_ready, 1)

            @block.scalar
            def _(act):
                nc.scalar.preload_act_table(ACT.Sigmoid)
                with act.Fori(0, B // 2) as pair:
                    b = 2 * pair
                    for u in range(2):
                        act.wait_ge(mix_ready, 2 * b)
                        act.wait_ge(onemu_ready, 1)
                        for i in range(2):
                            nc.scalar.activation(prev[i][u][:, 1:S], m.xt[:, ds((b + u) * S, S - 1)], ACT.Copy,
                                                 scale=onemu[:, i:i + 1]).then_inc(prev_ready, 1)
                    for u in range(2):
                        act.wait_ge(r_ready, b + u + 1)
                        act.wait_ge(rv_ready, b)
                        nc.scalar.activation(gate[u][:], r_ps[u][:], ACT.Sigmoid).then_inc(gate_ready, 1)
                        act.wait_ge(k_ready, b + u + 1)
                        act.wait_ge(ksq_ready, b)
                        nc.scalar.activation(kk[u][:], k_ps[u][:], ACT.Relu).then_inc(relu_ready, 1)
                    for u in range(2):
                        act.wait_ge(relu_ready, b + u + 1)
                        act.wait_ge(v_ready, b)
                        nc.scalar.activation(ksq[u][:], kk[u][:], ACT.Square).then_inc(ksq_ready, 1)

            @block.vector
            def _(dve):
                dve.wait_ge(loaded, 5 * 16)
                nc.vector.tensor_scalar(onemu[:], mu[:], -1.0, 1.0, ALU.mult, ALU.add).then_inc(onemu_ready, 1)
                dve.wait_ge(edge_ready, 4)
                with dve.Fori(0, B // 2) as pair:
                    b = 2 * pair
                    for u in range(2):
                        for i, used in ((0, r_ready), (1, k_ready)):
                            dve.wait_ge(prev_ready, 2 * (b + u) + i + 1)
                            dve.wait_ge(used, b)
                            nc.vector.scalar_tensor_tensor(out=mix[i][u][:], in0=m.xt[:, ts(b + u, S)],
                                                           scalar=mu[:, i:i + 1], in1=prev[i][u][:],
                                                           op0=ALU.mult, op1=ALU.add).then_inc(mix_ready, 1)
                    for u in range(2):
                        dve.wait_ge(v_ready, b + u + 1)
                        dve.wait_ge(gate_ready, b + u + 1)
                        dve.wait_ge(z_ready, b)
                        nc.vector.tensor_tensor(rv[u][:], v_ps[u][:], gate[u][:], ALU.mult).then_inc(rv_ready, 1)
                    for u in range(2):
                        dve.wait_ge(rv_ready, b + u + 1)
                        nc.vector.tensor_tensor(m.zt[:, ts(b + u, S)], rv[u][:], m.xt[:, ts(b + u, S)],
                                                ALU.add).then_inc(z_ready, 1)

            @block.tensor
            def _(pe):
                pe.wait_ge(loaded, 5 * 16)
                with pe.Fori(0, B // 2) as pair:
                    b = 2 * pair
                    for u in range(2):
                        pe.wait_ge(mix_ready, 2 * (b + u) + 1)
                        pe.wait_ge(gate_ready, b)
                        nc.tensor.matmul(r_ps[u][:], wr[:], mix[0][u][:], start=True, stop=True).then_inc(r_ready, 1)
                        pe.wait_ge(mix_ready, 2 * (b + u) + 2)
                        pe.wait_ge(relu_ready, b)
                        nc.tensor.matmul(k_ps[u][:], wk[:], mix[1][u][:], start=True, stop=True).then_inc(k_ready, 1)
                    for u in range(2):
                        pe.wait_ge(ksq_ready, b + u + 1)
                        pe.wait_ge(rv_ready, b)
                        nc.tensor.matmul(v_ps[u][:], wv[:], ksq[u][:], start=True, stop=True).then_inc(v_ready, 1)


def linear_attention(nc, m, tag, w_qT, w_kT, w_vT, bq_rows, bk_col, bv_col):
    scale = float(P) ** -0.5
    with nc.cleanup_on_exit():
        sb, ps, sem = places(nc, tag)
        wq, wk, wv = (sb(n, [P, P]) for n in ("wq", "wk", "wv"))
        bq = sb("bq", [P, P])
        bkv = sb("bkv", [P, 2])
        xb = sb("xb", [P, S])
        q, qd, qe, qn = (sb(n, [P, TB, P]) for n in ("q", "qd", "qe", "qn"))
        qmax, qsum, qrec = (sb(n, [P, TB]) for n in ("qmax", "qsum", "qrec"))
        kve = [sb(f"kve{i}", [P, S]) for i in range(2)]
        kvn = [sb(f"kvn{i}", [P, S]) for i in range(2)]
        kvmax, kvbias, kvsum, kvrec = (sb(n, [P, 2]) for n in ("kvmax", "kvbias", "kvsum", "kvrec"))
        kvt = [sb(f"kvt{i}", [P, TB, P]) for i in range(2)]
        qt = sb("qt", [P, S])
        kv = sb("kv", [P, P])
        q_ps = ps("qps", [P, TB, P])
        kv_ps = [ps(f"kvps{i}", [P, S]) for i in range(2)]
        t_ps = [ps(f"tps{i}", [P, TB, P]) for i in range(3)]
        c_ps = ps("cps", [P, P])
        o_ps = ps("ops", [P, S])
        loaded, xb_ready, q_ready, kv_ready, qb_ready, qmax_ready, qd_ready, qe_ready, qsum_ready, qrec_ready, qn_ready, \
            kvmax_ready, kvtop_ready, kvbias_ready, kve_ready, kvrec_ready, kvn_ready, t_ready, kvt_ready, qt_ready, c_ready, \
            kvc_ready, o_ready, z_ready = (sem(n) for n in (
                "loaded", "xb_ready", "q_ready", "kv_ready", "qb_ready", "qmax_ready", "qd_ready", "qe_ready",
                "qsum_ready", "qrec_ready", "qn_ready", "kvmax_ready", "kvtop_ready", "kvbias_ready", "kve_ready",
                "kvrec_ready", "kvn_ready", "t_ready", "kvt_ready", "qt_ready", "c_ready", "kvc_ready", "o_ready", "z_ready"))
        with nc.Block() as block:
            @block.sync
            def _(sp):
                for dst, src in ((wq[:], w_qT), (wk[:], w_kT), (wv[:], w_vT), (bq[:], bq_rows),
                                 (bkv[:, 0:1], bk_col), (bkv[:, 1:2], bv_col)):
                    sp.dma_start(dst, src).then_inc(loaded, 16)

            @block.tensor
            def _(pe):
                pe.wait_ge(loaded, 6 * 16)
                with pe.Fori(0, B) as b:
                    pe.wait_ge(xb_ready, b + 1)
                    pe.wait_ge(qb_ready, b)
                    for t in range(TB):
                        last = nc.tensor.matmul(q_ps[:, t, :], xb[:, t * P:(t + 1) * P], wq[:], start=True, stop=True)
                    last.then_inc(q_ready, 1)
                    for i, w in enumerate((wk, wv)):
                        pe.wait_ge(kve_ready, 2 * b)
                        nc.tensor.matmul(kv_ps[i][:], w[:], xb[:], start=True, stop=True).then_inc(kv_ready, 1)
                    for i in range(2):
                        pe.wait_ge(kvn_ready, 2 * b + i + 1)
                        for t in range(TB):
                            last = nc.tensor.transpose(t_ps[i][:, t, :], kvn[i][:, t * P:(t + 1) * P], m.ident[:])
                        last.then_inc(t_ready, 1)
                    pe.wait_ge(qn_ready, b + 1)
                    for t in range(TB):
                        last = nc.tensor.transpose(t_ps[2][:, t, :], qn[:, t, :], m.ident[:])
                    last.then_inc(t_ready, 1)
                    pe.wait_ge(kvt_ready, 2 * b + 2)
                    pe.wait_ge(kvc_ready, b)
                    for t in range(TB):
                        last = nc.tensor.matmul(c_ps[:], kvt[0][:, t, :], kvt[1][:, t, :],
                                                start=(t == 0), stop=(t == TB - 1))
                    last.then_inc(c_ready, 1)
                    pe.wait_ge(kvc_ready, b + 1)
                    pe.wait_ge(qt_ready, b + 1)
                    pe.wait_ge(z_ready, b)
                    nc.tensor.matmul(o_ps[:], kv[:], qt[:], start=True, stop=True).then_inc(o_ready, 1)

            @block.scalar
            def _(act):
                with act.Fori(0, B) as b:
                    act.wait_ge(qd_ready, b + 1)
                    act.wait_ge(qn_ready, b)
                    nc.scalar.activation(qe[:], qd[:], ACT.Exp).then_inc(qe_ready, 1)
                    for i in range(2):
                        act.wait_ge(kvbias_ready, b + 1)
                        act.wait_ge(kvn_ready, 2 * b)
                        nc.scalar.activation(kve[i][:], kv_ps[i][:], ACT.Exp, bias=kvbias[:, i:i + 1],
                                             accum_out=kvsum[:, i:i + 1]).then_inc(kve_ready, 1)
                    for i in range(2):
                        act.wait_ge(t_ready, 3 * b + i + 1)
                        act.wait_ge(c_ready, b)
                        nc.scalar.activation(kvt[i][:], t_ps[i][:], ACT.Copy).then_inc(kvt_ready, 1)
                    act.wait_ge(t_ready, 3 * b + 3)
                    act.wait_ge(o_ready, b)
                    nc.scalar.activation(qt[:], t_ps[2][:].rearrange("p t q -> p (t q)"), ACT.Copy).then_inc(qt_ready, 1)

            @block.vector
            def _(dve):
                dve.wait_ge(loaded, 6 * 16)
                with dve.Fori(0, B) as b:
                    dve.wait_ge(kv_ready, 2 * b)
                    nc.vector.tensor_copy(xb[:], m.xt[:, ts(b, S)]).then_inc(xb_ready, 1)
                    dve.wait_ge(q_ready, b + 1)
                    nc.vector.tensor_tensor(q[:], q_ps[:], bq[:].rearrange("p (t q) -> p t q", t=1).broadcast_to([P, TB, P]),
                                            ALU.add).then_inc(qb_ready, 1)
                    dve.wait_ge(qb_ready, b + 1)
                    nc.vector.tensor_reduce(qmax[:], q[:], AX.X, ALU.max).then_inc(qmax_ready, 1)
                    dve.wait_ge(qmax_ready, b + 1)
                    nc.vector.tensor_tensor(qd[:], q[:], qmax[:].rearrange("p (t q) -> p t q", q=1).broadcast_to([P, TB, P]),
                                            ALU.subtract).then_inc(qd_ready, 1)
                    for i in range(2):
                        dve.wait_ge(kv_ready, 2 * b + i + 1)
                        nc.vector.tensor_reduce(kvmax[:, i:i + 1], kv_ps[i][:], AX.X, ALU.max).then_inc(kvmax_ready, 1)
                    dve.wait_ge(kvmax_ready, 2 * b + 2)
                    nc.vector.tensor_tensor(kvbias[:], kvmax[:], bkv[:], ALU.add).then_inc(kvtop_ready, 1)
                    dve.wait_ge(kvtop_ready, b + 1)
                    nc.vector.tensor_tensor(kvbias[:], bkv[:], kvbias[:], ALU.subtract).then_inc(kvbias_ready, 1)
                    dve.wait_ge(qe_ready, b + 1)
                    nc.vector.tensor_reduce(qsum[:], qe[:], AX.X, ALU.add).then_inc(qsum_ready, 1)
                    dve.wait_ge(qsum_ready, b + 1)
                    nc.vector.reciprocal(qrec[:], qsum[:]).then_inc(qrec_ready, 1)
                    dve.wait_ge(qrec_ready, b + 1)
                    nc.vector.tensor_tensor(qn[:], qe[:], qrec[:].rearrange("p (t q) -> p t q", q=1).broadcast_to([P, TB, P]),
                                            ALU.mult).then_inc(qn_ready, 1)
                    dve.wait_ge(kve_ready, 2 * b + 2)
                    nc.vector.reciprocal(kvrec[:], kvsum[:]).then_inc(kvrec_ready, 1)
                    dve.wait_ge(kvrec_ready, b + 1)
                    for i in range(2):
                        nc.vector.tensor_scalar(kvn[i][:], kve[i][:], kvrec[:, i:i + 1], (scale, 1.0)[i],
                                                ALU.mult, ALU.mult).then_inc(kvn_ready, 1)
                    dve.wait_ge(c_ready, b + 1)
                    dve.wait_ge(o_ready, b)
                    nc.vector.tensor_copy(kv[:], c_ps[:]).then_inc(kvc_ready, 1)
                    dve.wait_ge(o_ready, b + 1)
                    nc.vector.tensor_tensor(m.zt[:, ts(b, S)], o_ps[:], m.xt[:, ts(b, S)], ALU.add).then_inc(z_ready, 1)


def attention_out(nc, m, tag, w_o, bias_in, bias_out):
    with nc.cleanup_on_exit():
        sb, ps, sem = places(nc, tag)
        w = sb("w", [P, P])
        bias = sb("bias", [P, 2])
        ot = [sb(f"ot{u}", [P, S]) for u in range(2)]
        t_ps = [ps(f"t{u}", [P, S]) for u in range(2)]
        z_ps = [ps(f"z{u}", [P, S]) for u in range(2)]
        loaded, t_ready, ot_ready, zp_ready, z_ready = (
            sem(n) for n in ("loaded", "t_ready", "ot_ready", "zp_ready", "z_ready"))
        with nc.Block() as block:
            @block.sync
            def _(sp):
                sp.dma_start(w[:], w_o).then_inc(loaded, 16)
                sp.dma_start(bias[:, 0:1], bias_in).then_inc(loaded, 16)
                sp.dma_start(bias[:, 1:2], bias_out).then_inc(loaded, 16)

            @block.tensor
            def _(pe):
                pe.wait_ge(loaded, 3 * 16)

                def turn(b):
                    if b >= 2:
                        pe.wait_ge(ot_ready, b - 1)
                    for t in range(TB):
                        n = b * TB + t
                        last = nc.tensor.transpose(t_ps[b % 2][:, t * P:(t + 1) * P], m.zt[:, n * P:(n + 1) * P], m.ident[:])
                    last.then_inc(t_ready, 1)

                turn(0)
                for b in range(B):
                    if b + 1 < B:
                        turn(b + 1)
                    pe.wait_ge(ot_ready, b + 1)
                    if b >= 2:
                        pe.wait_ge(z_ready, b - 1)
                    nc.tensor.matmul(z_ps[b % 2][:], w[:], ot[b % 2][:], start=True, stop=True).then_inc(zp_ready, 1)

            @block.scalar
            def _(act):
                act.wait_ge(loaded, 3 * 16)
                for b in range(B):
                    act.wait_ge(t_ready, b + 1)
                    if b >= 2:
                        act.wait_ge(zp_ready, b - 1)
                    nc.scalar.activation(ot[b % 2][:], t_ps[b % 2][:], ACT.Identity, bias=bias[:, 0:1]).then_inc(ot_ready, 1)

            @block.vector
            def _(dve):
                for b in range(B):
                    dve.wait_ge(zp_ready, b + 1)
                    nc.vector.scalar_tensor_tensor(out=m.zt[:, b * S:(b + 1) * S], in0=z_ps[b % 2][:], scalar=bias[:, 1:2],
                                                   in1=m.xt[:, b * S:(b + 1) * S], op0=ALU.add, op1=ALU.add).then_inc(z_ready, 1)


def project(nc, m, tag, feat, weights, w_v, vt):
    with nc.cleanup_on_exit():
        sb, ps, sem = places(nc, tag)
        w = [sb(f"w{i}", [P, P]) for i in range(len(weights))]
        wv = sb("wv", [P, P])
        f_ps = [[ps(f"f{i}{u}", [P, S]) for u in range(2)] for i in range(len(weights))]
        v_ps = [ps(f"v{u}", [P, TB, P]) for u in range(2)]
        loaded = sem("loaded")
        f_ready = [sem(f"f_ready{i}") for i in range(len(weights))]
        f_used = [sem(f"f_used{i}") for i in range(len(weights))]
        v_ready, v_used = sem("v_ready"), sem("v_used")
        with nc.Block() as block:
            @block.sync
            def _(sp):
                for dst, src in zip(w, weights):
                    sp.dma_start(dst[:], src).then_inc(loaded, 16)
                sp.dma_start(wv[:], w_v).then_inc(loaded, 16)

            @block.tensor
            def _(pe):
                pe.wait_ge(loaded, 16 * (len(weights) + 1))
                for b in range(B):
                    for i in range(len(weights)):
                        if b >= 2:
                            pe.wait_ge(f_used[i], (b - 1) * sum(j == i for j, _, _ in feat))
                        nc.tensor.matmul(f_ps[i][b % 2][:], w[i][:], m.xt[:, b * S:(b + 1) * S],
                                         start=True, stop=True).then_inc(f_ready[i], 1)
                    if b >= 2:
                        pe.wait_ge(v_used, b - 1)
                    for t in range(TB):
                        n = b * TB + t
                        last = nc.tensor.matmul(v_ps[b % 2][:, t, :], m.xt[:, n * P:(n + 1) * P], wv[:], start=True, stop=True)
                    last.then_inc(v_ready, 1)

            @block.vector
            def _(dve):
                for b in range(B):
                    for i, bias, dst in feat:
                        dve.wait_ge(f_ready[i], b + 1)
                        nc.vector.tensor_scalar(dst[:, b * S:(b + 1) * S], f_ps[i][b % 2][:], bias, None,
                                                ALU.add).then_inc(f_used[i], 1)

            @block.scalar
            def _(act):
                for b in range(B):
                    act.wait_ge(v_ready, b + 1)
                    nc.scalar.activation(vt[:, b * TB:(b + 1) * TB, :], v_ps[b % 2][:], ACT.Copy).then_inc(v_used, 1)


def batch_softmax_attention(nc, m, tag, w_q, w_k, w_v, w_o, zero_col):
    inv_scale = 1.0 / float(P) ** 0.5
    with nc.cleanup_on_exit():
        sb, ps, sem = places(nc, tag)
        qt, kt = sb("qt", [P, T]), sb("kt", [P, T])
        vt = sb("vt", [P, NT, P])
        zero = sb("zero", [P, 1])
        z_ld = sem("z_ld")
        with nc.Block() as block:
            @block.vector
            def _(dve):
                nc.vector.memset(zero[:], 0.0).then_inc(z_ld, 1)
        project(nc, m, tag + "p", [(0, zero[:, 0:1], qt), (1, zero[:, 0:1], kt)], [w_q, w_k], w_v, vt)
        qm = sb("qm", [P, 2 * T])
        diff = [sb(f"diff{u}", [P, B, P]) for u in range(2)]
        top = [sb(f"top{u}", [P, P]) for u in range(2)]
        ex, prob = ([sb(f"{n}{u}", [P, B, P]) for u in range(TB)] for n in ("ex", "prob"))
        total, lnt, rec = ([sb(f"{n}{u}", [P, P]) for u in range(TB)] for n in ("total", "lnt", "rec"))
        s_ps = [ps(f"s{u}", [P, B, P]) for u in range(2)]
        o_ps = [ps(f"o{u}", [P, B, HD]) for u in range(2)]
        names = ("qm_ready", "s_ready", "top_ready", "diff_ready", "ex_ready", "total_ready", "ln_ready",
                 "rec_ready", "prob_ready", "pv_ready", "o_used")
        qm_ready, s_ready, top_ready, diff_ready, ex_ready, total_ready, ln_ready, rec_ready, prob_ready, \
            pv_ready, o_used = (sem(n) for n in names)
        o_view = m.zt[:].rearrange("p (b c) -> p b c", b=B)
        units = H * TB * TB
        with nc.Block() as block:
            @block.tensor
            def _(pe):
                def scores(n, k, h, q):
                    pe.wait_ge(qm_ready, h + 1)
                    if not isinstance(n, int) or n >= 2:
                        pe.wait_ge(diff_ready, n - 1)
                    for b in range(B):
                        last = nc.tensor.matmul(s_ps[k % 2][:, b, :], kt[:, (b * TB + k) * P:(b * TB + k + 1) * P],
                                                qm[:, ds((h % 2) * T + q * P + b * S, P)], start=True, stop=True)
                    last.then_inc(s_ready, 1)

                def values(n, k, h, f):
                    pe.wait_ge(prob_ready, TB + n + 1)
                    if k == 0:
                        pe.wait_ge(o_used, f + 2)
                    for b in range(B):
                        last = nc.tensor.matmul(o_ps[0][:, b, :], prob[k][:, b, :],
                                                vt[:, b * TB + k, ds(h * HD, HD)], start=(k == 0 and b == 0),
                                                stop=(k == TB - 1), skip_group_check=True)
                    last.then_inc(pv_ready, 1)

                def step(f, h, h1, q, q1):
                    for k in range(TB):
                        if k < 1:
                            scores(TB * f + k + 3, k + 3, h, q)
                        elif h1 is not None:
                            scores(TB * f + k + 3, k - 1, h1, q1)
                        values(TB * f + k, k, h, f)

                pe.sem_inc(pv_ready, TB)
                for k in range(3):
                    scores(k, k, 0, 0)
                with pe.Fori(0, H * TB - 1) as f:
                    step(f, f // TB, (f + 1) // TB, f % TB, (f + 1) % TB)
                step(H * TB - 1, H - 1, None, TB - 1, None)

            @block.vector
            def _(dve):
                def head(h, par):
                    nc.vector.tensor_scalar(qm[:, ds(par * T, T)], qt[:], m.hm[:, ds(h, 1)], None, ALU.mult).then_inc(qm_ready, 1)

                def diff_of(n, k):
                    dve.wait_ge(s_ready, n + 1)
                    if not isinstance(n, int) or n >= 2:
                        dve.wait_ge(diff_ready, n - 1)
                    nc.vector.tensor_reduce(top[k % 2][:], s_ps[k % 2][:].rearrange("p b q -> p q b"), AX.X,
                                            ALU.max).then_inc(top_ready, 1)
                    dve.wait_ge(top_ready, n + 1)
                    if not isinstance(n, int) or n >= 2:
                        dve.wait_ge(ex_ready, n - 1)
                    nc.vector.tensor_tensor(diff[k % 2][:], s_ps[k % 2][:],
                                            top[k % 2][:].rearrange("p (b q) -> p b q", b=1).broadcast_to([P, B, P]),
                                            ALU.subtract).then_inc(diff_ready, 1)

                def total_of(n, k):
                    dve.wait_ge(ex_ready, n + 1)
                    if not isinstance(n, int):
                        dve.wait_ge(prob_ready, n + 1)
                    nc.vector.tensor_reduce(total[k][:], ex[k][:].rearrange("p b q -> p q b"), AX.X,
                                            ALU.add).then_inc(total_ready, 1)

                def store(f, slot):
                    dve.wait_ge(pv_ready, TB * f + TB)
                    dve.wait_ge(o_used, f + 1)
                    nc.vector.tensor_scalar(o_view[:, :, ds((slot % TB) * P + (slot // TB) * HD, HD)], o_ps[0][:], 1.0, None,
                                            ALU.mult).then_inc(o_used, 1)

                def step(f, last):
                    for k in range(TB):
                        if not (last and k == TB - 1):
                            diff_of(4 * f + k + 1, (k + 1) % TB)
                        if k == 1:
                            store(f, (f + H * TB - 1) % (H * TB))
                        total_of(4 * f + k, k)

                nc.vector.memset(o_ps[0][:], 0.0).then_inc(o_used, 1)
                head(0, 0)
                diff_of(0, 0)
                with dve.Fori(0, H - 1) as h:
                    dve.wait_ge(s_ready, h * TB * TB)
                    dve.wait_ge(qm_ready, h + 1)
                    head(h + 1, (h + 1) % 2)
                    with dve.Fori(0, TB) as q:
                        step(h * TB + q, False)
                with dve.Fori(0, TB - 1) as q:
                    step((H - 1) * TB + q, False)
                step(H * TB - 1, True)
                store(H * TB, H * TB - 1)

            @block.scalar
            def _(act):
                def exps(n, k):
                    act.wait_ge(diff_ready, n + 1)
                    act.wait_ge(prob_ready, n + 1)
                    nc.scalar.activation(ex[k][:], diff[k % 2][:], ACT.Exp, scale=inv_scale).then_inc(ex_ready, 1)

                def recip(n, k):
                    act.wait_ge(total_ready, n + 1)
                    act.wait_ge(prob_ready, n + 1)
                    nc.scalar.activation(lnt[k][:], total[k][:], ACT.Ln).then_inc(ln_ready, 1)
                    act.wait_ge(ln_ready, n + 1)
                    nc.scalar.activation(rec[k][:], lnt[k][:], ACT.Exp, scale=-1.0).then_inc(rec_ready, 1)

                nc.scalar.preload_act_table_set(LN_EXP)
                exps(0, 0)
                with act.Fori(0, units // TB - 1) as f:
                    for k in range(TB):
                        exps(4 * f + k + 1, (k + 1) % TB)
                        recip(4 * f + k, k)
                for k in range(TB):
                    n = units - TB + k
                    if k < TB - 1:
                        exps(n + 1, k + 1)
                    recip(n, k)

            @block.gpsimd
            def _(pool):
                pool.sem_inc(prob_ready, TB)
                with pool.Fori(0, units // TB) as f:
                    for u in range(TB):
                        pool.wait_ge(rec_ready, TB * f + u + 1)
                        pool.wait_ge(pv_ready, TB * f + u + 1)
                        nc.gpsimd.tensor_tensor(prob[u][:], ex[u][:],
                                                rec[u][:].rearrange("p (b q) -> p b q", b=1).broadcast_to([P, B, P]),
                                                ALU.mult).then_inc(prob_ready, 1)
    attention_out(nc, m, tag + "o", w_o, zero_col, zero_col)


def relative_attention(nc, m, tag, a, scratch):
    inv_scale = 1.0 / float(HD) ** 0.5
    heads = B * H
    with nc.cleanup_on_exit():
        sb, ps, sem = places(nc, tag)
        qu, qv, kt = (sb(n, [P, T]) for n in ("qu", "qv", "kt"))
        vt = sb("vt", [P, NT, P])
        wp, feat = sb("wp", [P, P]), sb("feat", [P, S])
        cols = sb("cols", [P, 5])
        bqu, bqv = sb("bqu", [P, 1]), sb("bqv", [P, 1])
        pos = sb("pos", [P, S])
        loaded, bias_ready, pos_made, pos_ready = (sem(n) for n in ("loaded", "bias_ready", "pos_made", "pos_ready"))
        rows = [scratch[u].rearrange("(t p c) -> p t c", p=P, c=S + 1) for u in range(2)]
        back = [scratch[u][S:S * (S + 1)].rearrange("(t p c) -> p t c", p=P, c=S) for u in range(2)]
        with nc.cleanup_on_exit():
            pos_ps = ps("pos_ps", [P, S])
            with nc.Block() as block:
                @block.sync
                def _(sp):
                    for dst, src in ((wp[:], a["Wp"]), (feat[:], a["feat"]), *((cols[:, i:i + 1], a[n]) for i, n in
                                     enumerate(("bq", "bk", "bp", "u", "v")))):
                        sp.dma_start(dst, src).then_inc(loaded, 16)

                @block.tensor
                def _(pe):
                    pe.wait_ge(loaded, 7 * 16)
                    nc.tensor.matmul(pos_ps[:], wp[:], feat[:], start=True, stop=True).then_inc(pos_made, 1)

                @block.vector
                def _(dve):
                    dve.wait_ge(loaded, 7 * 16)
                    nc.vector.tensor_tensor(bqu[:], cols[:, 0:1], cols[:, 3:4], ALU.add).then_inc(bias_ready, 1)
                    nc.vector.tensor_tensor(bqv[:], cols[:, 0:1], cols[:, 4:5], ALU.add).then_inc(bias_ready, 1)
                    dve.wait_ge(pos_made, 1)
                    nc.vector.tensor_scalar(pos[:], pos_ps[:], cols[:, 2:3], None, ALU.add).then_inc(pos_ready, 1)
        with nc.cleanup_on_exit():
            project(nc, m, tag + "p", [(0, bqu[:], qu), (0, bqv[:], qv), (1, cols[:, 1:2], kt)], [a["Wq"], a["Wk"]], a["Wv"], vt)

        quh, qvh = ([sb(f"{n}{u}", [P, S]) for u in range(2)] for n in ("quh", "qvh"))
        pc = [sb(f"pc{u}", [P, TB, S + 1]) for u in range(2)]
        rel = [sb(f"rel{u}", [P, TB, S]) for u in range(2)]
        s, ex, et = ([sb(f"{n}{u}", [P, S]) for u in range(2)] for n in ("s", "ex", "et"))
        top, ntop, total = (sb(n, [P, 2, TB]) for n in ("top", "ntop", "total"))
        rec = sb("rec", [P, 2, TB])
        p_ps, c_ps, t_ps = ([ps(f"{n}ps{u}", [P, S]) for u in range(2)] for n in ("p", "c", "t"))
        o_ps = [ps(f"o{u}", [P, TB, HD]) for u in range(2)]
        names = ("quh_ready", "qvh_ready", "p_ready", "pc_ready", "out_done", "rel_ready0", "rel_ready1", "c_ready", "s_ready",
                 "ntop_ready", "ex_ready", "t_ready", "et_ready", "pv_ready", "rec_ready", "o_ready", "edge_ready")
        quh_ready, qvh_ready, p_ready, pc_ready, out_done, rel_ready0, rel_ready1, c_ready, s_ready, ntop_ready, \
            ex_ready, t_ready, et_ready, pv_ready, rec_ready, o_ready, edge_ready = (sem(n) for n in names)
        rel_ready = (rel_ready0, rel_ready1)
        o_view = m.zt[:].rearrange("p (n f) -> p n f", f=P)
        static = lambda n: isinstance(n, int)
        with nc.Block() as block:
            @block.gpsimd
            def _(pool):
                for u in range(2):
                    nc.gpsimd.memset(pc[u][:, :, 0:1], 0.0).then_inc(edge_ready, 1)

            @block.sync
            def _(sp):
                def shift(g, u):
                    if static(g):
                        copied, read, out, added = TB * g + TB, 8 * (g - u), 16 * g + 16, TB * g - TB
                    else:
                        copied, read, out, added = (sp.snap(sp.to_reg(v)) for v in (TB * g + TB, 8 * (g - u), 16 * g + 16, TB * g - TB))
                    sp.wait_ge(edge_ready, 2)
                    sp.wait_ge(pc_ready, copied)
                    if not static(g) or g >= 2:
                        sp.wait_ge(rel_ready[u], read)
                    sp.dma_start(rows[u], pc[u][:]).then_inc(out_done, 16)
                    sp.wait_ge(out_done, out)
                    if not static(g) or g >= 2:
                        sp.wait_ge(s_ready, added)
                    sp.dma_start(rel[u][:], back[u]).then_inc(rel_ready[u], 16)

                shift(0, 0)
                shift(1, 1)
                with sp.Fori(1, heads // 2) as pair:
                    for u in range(2):
                        shift(2 * pair + u, u)
                for u in range(2):
                    sp.wait_ge(rel_ready[u], 8 * heads)

            @block.tensor
            def _(pe):
                def position(g, u, t):
                    pe.wait_ge(qvh_ready, g + 1)
                    if not (static(g) and TB * g + t < 2):
                        pe.wait_ge(pc_ready, TB * g + t - 1)
                    nc.tensor.matmul(p_ps[t % 2][:], qvh[u][:, t * P:(t + 1) * P], pos[:], start=True, stop=True).then_inc(p_ready, 1)

                def content(g, u, t, b):
                    pe.wait_ge(quh_ready, g + 1)
                    if not (static(g) and TB * g + t < 2):
                        pe.wait_ge(s_ready, TB * g + t - 1)
                    nc.tensor.matmul(c_ps[t % 2][:], quh[u][:, t * P:(t + 1) * P], kt[:, ds(b * S, S)],
                                     start=True, stop=True).then_inc(c_ready, 1)

                def turn(g, t):
                    pe.wait_ge(ex_ready, TB * g + t + 1)
                    if not (static(g) and TB * g + t < 2):
                        pe.wait_ge(et_ready, TB * g + t - 1)
                    for k in range(TB):
                        last = nc.tensor.transpose(t_ps[t % 2][:, k * P:(k + 1) * P], ex[t % 2][:, k * P:(k + 1) * P], m.ident[:])
                    last.then_inc(t_ready, 1)

                def values(g, u, t, b, h):
                    pe.wait_ge(et_ready, TB * g + t + 1)
                    if t == 0 and not (static(g) and g < 2):
                        pe.wait_ge(o_ready, g - 1)
                    for k in range(TB):
                        last = nc.tensor.matmul(o_ps[u][:, t, :], et[t % 2][:, k * P:(k + 1) * P],
                                                vt[:, ds(b * TB + k, 1), ds(h * HD, HD)], start=(k == 0), stop=(k == TB - 1))
                    last.then_inc(pv_ready, 1)

                def head(g, u, at, at1, ahead):
                    for t in range(TB):
                        if ahead:
                            position(g + 2, u, t)
                        if t < 2:
                            content(g, u, t + 2, at[0])
                        elif at1:
                            content(g + 1, 1 - u, t - 2, at1[0])
                        if t < 3:
                            turn(g, t + 1)
                        elif at1:
                            turn(g + 1, 0)
                        values(g, u, t, *at)

                for g in range(2):
                    for t in range(TB):
                        position(g, g, t)
                content(0, 0, 0, 0)
                content(0, 0, 1, 0)
                turn(0, 0)
                for g in range(2):
                    head(g, g, (0, g), (0, g + 1), True)
                with pe.Fori(1, heads // 2 - 1) as pair:
                    for u in range(2):
                        g = 2 * pair + u
                        head(g, u, (g // H, g % H), ((g + 1) // H, (g + 1) % H), True)
                head(heads - 2, 0, (B - 1, H - 2), (B - 1, H - 1), False)
                head(heads - 1, 1, (B - 1, H - 1), None, False)

            @block.scalar
            def _(act):
                def copy(g, u, t):
                    act.wait_ge(p_ready, TB * g + t + 1)
                    if t == 0 and not (static(g) and g < 2):
                        act.wait_ge(out_done, 16 * (g - 1))
                    nc.scalar.activation(pc[u][:, t, 1:], p_ps[t % 2][:], ACT.Copy).then_inc(pc_ready, 1)

                def exps(g, u, t):
                    act.wait_ge(ntop_ready, TB * g + t + 1)
                    if not (static(g) and TB * g + t < 2):
                        act.wait_ge(t_ready, TB * g + t - 1)
                    if t == 0 and not (static(g) and g < 2):
                        act.wait_ge(rec_ready, g - 1)
                    nc.scalar.activation(ex[t % 2][:], s[t % 2][:], ACT.Exp, scale=inv_scale, bias=ntop[:, u, t:t + 1],
                                         accum_out=total[:, u, t:t + 1]).then_inc(ex_ready, 1)

                def head(g, u, ahead, last):
                    for t in range(TB):
                        if ahead:
                            copy(g + 2, u, t)
                        if t < 3:
                            exps(g, u, t + 1)
                        elif not last:
                            exps(g + 1, 1 - u, 0)

                nc.scalar.preload_act_table(ACT.Exp)
                for g in range(2):
                    for t in range(TB):
                        copy(g, g, t)
                exps(0, 0, 0)
                with act.Fori(0, heads // 2 - 1) as pair:
                    for u in range(2):
                        head(2 * pair + u, u, True, False)
                head(heads - 2, 0, False, False)
                head(heads - 1, 1, False, True)

            @block.vector
            def _(dve):
                def mask(dst, src, b, h, ready):
                    nc.vector.tensor_scalar(dst, src[:, ds(b * S, S)], m.hm[:, ds(h, 1)], None, ALU.mult).then_inc(ready, 1)

                def score(g, u, t):
                    dve.wait_ge(c_ready, TB * g + t + 1)
                    dve.wait_ge(rel_ready[u], 8 * (g - u) + 16)
                    if not (static(g) and TB * g + t < 2):
                        dve.wait_ge(ex_ready, TB * g + t - 1)
                    dve.nop(nofuse=True)
                    nc.vector.tensor_tensor_reduce(s[t % 2][:], c_ps[t % 2][:], rel[u][:, t, :], 1.0, -3.0e38, ALU.add, ALU.max,
                                                   top[:, u, t:t + 1]).then_inc(s_ready, 1)
                    dve.wait_ge(s_ready, TB * g + t + 1)
                    nc.vector.tensor_scalar(ntop[:, u, t:t + 1], top[:, u, t:t + 1], -inv_scale, None, ALU.mult).then_inc(ntop_ready, 1)

                def copy(g, t):
                    dve.wait_ge(t_ready, TB * g + t + 1)
                    if not (static(g) and TB * g + t < 2):
                        dve.wait_ge(pv_ready, TB * g + t - 1)
                    nc.vector.tensor_copy(et[t % 2][:], t_ps[t % 2][:]).then_inc(et_ready, 1)

                def store(g, u, b, h):
                    dve.wait_ge(pv_ready, TB * g + TB)
                    dve.wait_ge(rec_ready, g + 1)
                    nc.vector.tensor_tensor(o_view[:, ds(b * TB, TB), ds(h * HD, HD)], o_ps[u][:],
                                            rec[:, u, :].rearrange("p (t c) -> p t c", c=1).broadcast_to([P, TB, HD]),
                                            ALU.mult).then_inc(o_ready, 1)

                def head(g, u, at, at1, at3, last):
                    if at1:
                        if not (static(g) and g == 0):
                            dve.wait_ge(c_ready, TB * g)
                        mask(quh[1 - u][:], qu, *at1, quh_ready)
                    if at3:
                        dve.wait_ge(p_ready, TB * (g + 2))
                        mask(qvh[1 - u][:], qv, *at3, qvh_ready)
                    for t in range(TB):
                        if t < 3:
                            score(g, u, t + 1)
                        elif not last:
                            score(g + 1, 1 - u, 0)
                        copy(g, t)
                    dve.wait_ge(ex_ready, TB * g + TB)
                    if not (static(g) and g < 2):
                        dve.wait_ge(o_ready, g - 1)
                    nc.vector.reciprocal(rec[:, u, :], total[:, u, :]).then_inc(rec_ready, 1)
                    store(g, u, *at)

                mask(qvh[0][:], qv, 0, 0, qvh_ready)
                mask(qvh[1][:], qv, 0, 1, qvh_ready)
                mask(quh[0][:], qu, 0, 0, quh_ready)
                dve.wait_ge(p_ready, TB)
                mask(qvh[0][:], qv, 0, 2, qvh_ready)
                score(0, 0, 0)
                for g in range(2):
                    head(g, g, (0, g), (0, g + 1), (0, g + 3), False)
                with dve.Fori(1, heads // 2 - 1) as pair:
                    for u in range(2):
                        g = 2 * pair + u
                        head(g, u, (g // H, g % H), ((g + 1) // H, (g + 1) % H), (((g + 3) // H) % B, (g + 3) % H), False)
                head(heads - 2, 0, (B - 1, H - 2), (B - 1, H - 1), None, False)
                head(heads - 1, 1, (B - 1, H - 1), None, None, True)


E = 8
FF = 512
CAP = T // E


def experts(nc, m, tag, a):
    C = FF // P
    with nc.cleanup_on_exit():
        sb, ps, sem = places(nc, tag)
        y = sb("y", [P, NT, P])
        gates = sb("gates", [P, NT, E])
        with nc.cleanup_on_exit():
            wg, b2 = sb("wg", [P, E]), sb("b2", [E, P])
            before, ones = sb("before", [P, P]), sb("ones", [P, P])
            first = sb("first", [P, E])
            lg, d, ex, hit, rank, pick, tot, run, place, kept = (sb(n, [P, NT, E]) for n in (
                "lg", "d", "ex", "hit", "rank", "pick", "tot", "run", "place", "kept"))
            top, total, gate, best = (sb(n, [P, NT]) for n in ("top", "total", "gate", "best"))
            unit = sb("unit", [P, NT])
            gt = sb("gt", [E, T])
            l_ps, n_ps, s_ps = ps("l", [P, NT, E]), ps("n", [P, NT, E]), ps("s", [P, NT, E])
            g_ps = [ps(f"g{u}", [E, S]) for u in range(2)]
            y_ps = [ps(f"y{u}", [P, TB, P]) for u in range(2)]
            loaded, l_ready, step, ex_ready, pick_ready, n_ready, s_ready, gates_ready, g_ready, gt_ready, yp_ready, y_ready = (
                sem(n) for n in ("loaded", "l_ready", "step", "ex_ready", "pick_ready", "n_ready", "s_ready",
                                 "gates_ready", "g_ready", "gt_ready", "yp_ready", "y_ready"))
            ones_ready = sem("ones_ready")
            wide = lambda ap: ap.rearrange("p (t e) -> p t e", e=1).broadcast_to([P, NT, E])
            with nc.Block() as block:
                @block.sync
                def _(sp):
                    for dst, src in ((wg, a["wg"]), (b2, a["b2"]), (before, a["before"]), (first, a["first"])):
                        sp.dma_start(dst[:], src).then_inc(loaded, 16)

                @block.tensor
                def _(pe):
                    pe.wait_ge(loaded, 4 * 16)
                    for n in range(NT):
                        last = nc.tensor.matmul(l_ps[:, n, :], m.xt[:, n * P:(n + 1) * P], wg[:], start=True, stop=True)
                    last.then_inc(l_ready, 1)
                    pe.wait_ge(ones_ready, 1)
                    pe.wait_ge(pick_ready, 1)
                    nc.tensor.matmul(n_ps[:], before[:], pick[:], start=True, stop=True).then_inc(n_ready, 1)
                    nc.tensor.matmul(s_ps[:], ones[:], pick[:], start=True, stop=True).then_inc(s_ready, 1)
                    pe.wait_ge(gates_ready, 1)
                    for b in range(B):
                        if b >= 2:
                            pe.wait_ge(gt_ready, b - 1)
                            pe.wait_ge(y_ready, b - 1)
                        for t in range(TB):
                            last = nc.tensor.transpose(g_ps[b % 2][:, t * P:(t + 1) * P], gates[:, b * TB + t, :], m.ident[:])
                        last.then_inc(g_ready, 1)
                        pe.wait_ge(gt_ready, b + 1)
                        for t in range(TB):
                            n = b * TB + t
                            last = nc.tensor.matmul(y_ps[b % 2][:, t, :], gt[:, n * P:(n + 1) * P], b2[:], start=True, stop=True)
                        last.then_inc(yp_ready, 1)

                @block.scalar
                def _(act):
                    act.wait_ge(step, 2)
                    nc.scalar.activation(ex[:], d[:], ACT.Exp).then_inc(ex_ready, 1)
                    for b in range(B):
                        act.wait_ge(yp_ready, b + 1)
                        nc.scalar.activation(y[:, b * TB:(b + 1) * TB, :], y_ps[b % 2][:], ACT.Copy).then_inc(y_ready, 1)

                @block.vector
                def _(dve):
                    done = [0]

                    def then(ins):
                        done[0] += 1
                        ins.then_inc(step, 1)
                        dve.wait_ge(step, done[0])

                    nc.vector.memset(unit[:], 1.0)
                    dve.wait_ge(l_ready, 1)
                    then(nc.vector.tensor_reduce(top[:], l_ps[:], AX.X, ALU.max))
                    then(nc.vector.tensor_tensor(d[:], l_ps[:], wide(top[:]), ALU.subtract))
                    then(nc.vector.tensor_scalar(hit[:], d[:], 0.0, None, ALU.is_ge))
                    dve.wait_ge(loaded, 4 * 16)
                    then(nc.vector.tensor_tensor(rank[:], hit[:], first[:].rearrange("p (t e) -> p t e", t=1).broadcast_to([P, NT, E]),
                                                 ALU.mult))
                    then(nc.vector.tensor_reduce(best[:], rank[:], AX.X, ALU.max))
                    nc.vector.tensor_tensor(pick[:], rank[:], wide(best[:]), ALU.is_equal).then_inc(pick_ready, 1)
                    dve.wait_ge(ex_ready, 1)
                    then(nc.vector.tensor_reduce(total[:], ex[:], AX.X, ALU.add))
                    then(nc.vector.reciprocal(gate[:], total[:]))
                    dve.wait_ge(s_ready, 1)
                    then(nc.vector.tensor_copy(tot[:], s_ps[:]))
                    for e in range(E):
                        last = nc.vector.tensor_tensor_scan(run[:, :, e], unit[:], tot[:, :, e], 0.0, ALU.mult, ALU.add)
                    then(last)
                    dve.wait_ge(n_ready, 1)
                    then(nc.vector.tensor_tensor(place[:], n_ps[:], run[:], ALU.add))
                    then(nc.vector.tensor_tensor(lg[:], place[:], tot[:], ALU.subtract))
                    then(nc.vector.tensor_scalar(kept[:], lg[:], float(CAP), None, ALU.is_le))
                    then(nc.vector.tensor_tensor(hit[:], kept[:], pick[:], ALU.mult))
                    nc.vector.tensor_tensor(gates[:], hit[:], wide(gate[:]), ALU.mult).then_inc(gates_ready, 1)
                    for b in range(B):
                        dve.wait_ge(g_ready, b + 1)
                        nc.vector.tensor_copy(gt[:, b * S:(b + 1) * S], g_ps[b % 2][:]).then_inc(gt_ready, 1)

                @block.gpsimd
                def _(pool):
                    nc.gpsimd.memset(ones[:], 1.0).then_inc(ones_ready, 1)

        with nc.cleanup_on_exit():
            w1 = [sb(f"w1{u}", [P, FF]) for u in range(2)]
            w2 = [sb(f"w2{u}", [P, C, P]) for u in range(2)]
            b1 = [sb(f"b1{u}", [P, C]) for u in range(2)]
            h = [sb(f"h{c}", [P, S]) for c in range(C)]
            h_ps = [ps(f"h_ps{c}", [P, S]) for c in range(C)]
            e_ps = [ps(f"e{u}", [P, TB, P]) for u in range(2)]
            ld0, ld1, hp_ready, h_act, h_dve, e_ready, y_ready = (
                sem(n) for n in ("ld0", "ld1", "hp_ready", "h_act", "h_dve", "e_ready", "y2_ready"))
            loaded = (ld0, ld1)
            with nc.Block() as block:
                @block.sync
                def _(sp):
                    with sp.Fori(0, E // 2) as i:
                        for u in range(2):
                            e = 2 * i + u
                            used, read = sp.snap(sp.to_reg(B * (e - u))), e
                            sp.wait_ge(e_ready, used)
                            sp.dma_start(w1[u][:], a["w1"][ds(e, 1)].rearrange("e m h -> (e m) h")).then_inc(loaded[u], 16)
                            sp.dma_start(w2[u][:], a["w2"][ds(e, 1)].rearrange("e (c p) m -> p (e c) m", p=P)).then_inc(loaded[u], 16)
                            sp.dma_start(b1[u][:], a["b1"][:, ds(e * C, C)]).then_inc(loaded[u], 16)

                @block.tensor
                def _(pe):
                    with pe.Fori(0, E // 2) as i:
                        for u in range(2):
                            with pe.Fori(0, B // 2) as pair:
                                for v in range(2):
                                    n = (2 * i + u) * B + 2 * pair + v
                                    pe.wait_ge(loaded[u], 48 * i + 48)
                                    pe.wait_ge(h_act, 2 * n)
                                    pe.wait_ge(h_dve, 2 * n)
                                    for c in range(C):
                                        nc.tensor.matmul(h_ps[c][:], w1[u][:, c * P:(c + 1) * P], m.xt[:, ds((2 * pair + v) * S, S)],
                                                         start=True, stop=True).then_inc(hp_ready, 1)
                                    pe.wait_ge(y_ready, TB * 2 * ((2 * i + u) * (B // 2) + pair))
                                    for t in range(TB):
                                        for c in range(C):
                                            if t == 0:
                                                pe.wait_ge(h_act if c % 2 == 0 else h_dve, 2 * n + c // 2 + 1)
                                            last = nc.tensor.matmul(e_ps[v][:, t, :], h[c][:, t * P:(t + 1) * P], w2[u][:, c, :],
                                                                    start=(c == 0), stop=(c == C - 1))
                                    last.then_inc(e_ready, 1)

                @block.scalar
                def _(act):
                    with act.Fori(0, E // 2) as i:
                        for u in range(2):
                            with act.Fori(0, B) as b:
                                n = (2 * i + u) * B + b
                                for c in (0, 2):
                                    act.wait_ge(hp_ready, C * n + c + 1)
                                    act.wait_ge(e_ready, n)
                                    nc.scalar.activation(h[c][:], h_ps[c][:], ACT.Relu, bias=b1[u][:, c:c + 1]).then_inc(h_act, 1)

                @block.vector
                def _(dve):
                    with dve.Fori(0, E // 2) as i:
                        for u in range(2):
                            with dve.Fori(0, B // 2) as pair:
                                for v in range(2):
                                    e, b = 2 * i + u, 2 * pair + v
                                    n = e * B + b
                                    for c in (1, 3):
                                        dve.wait_ge(hp_ready, C * n + c + 1)
                                        dve.wait_ge(e_ready, n)
                                        nc.vector.tensor_scalar(h[c][:], h_ps[c][:], b1[u][:, c:c + 1], 0.0,
                                                                ALU.add, ALU.max).then_inc(h_dve, 1)
                                    dve.wait_ge(e_ready, n + 1)
                                    dve.wait_ge(y_ready, TB * n)
                                    for t in range(TB):
                                        row = y[:, ds(b * TB + t, 1), :].rearrange("p a f -> p (a f)")
                                        nc.vector.scalar_tensor_tensor(
                                            out=row, in0=e_ps[v][:, t, :],
                                            scalar=gates[:, ds(b * TB + t, 1), ds(e, 1)].rearrange("p a f -> p (a f)"),
                                            in1=row, op0=ALU.mult, op1=ALU.add).then_inc(y_ready, 1)
        rows_out(nc, m, tag + "o", y)


def rows_out(nc, m, tag, y):
    with nc.cleanup_on_exit():
        sb, ps, sem = places(nc, tag)
        t_ps = [ps(f"t{u}", [P, S]) for u in range(2)]
        t_ready, z_ready = sem("t_ready"), sem("z_ready")
        with nc.Block() as block:
            @block.tensor
            def _(pe):
                for b in range(B):
                    if b >= 2:
                        pe.wait_ge(z_ready, b - 1)
                    for t in range(TB):
                        last = nc.tensor.transpose(t_ps[b % 2][:, t * P:(t + 1) * P], y[:, b * TB + t, :], m.ident[:])
                    last.then_inc(t_ready, 1)

            @block.vector
            def _(dve):
                for b in range(B):
                    dve.wait_ge(t_ready, b + 1)
                    nc.vector.tensor_tensor(m.zt[:, b * S:(b + 1) * S], t_ps[b % 2][:], m.xt[:, b * S:(b + 1) * S],
                                            ALU.add).then_inc(z_ready, 1)


DECAY = 0.9
SPIKE, WINNERS = 0.5, 4


def rms_norm(nc, m, tag, w_col):
    with nc.cleanup_on_exit():
        sb, ps, sem = places(nc, tag)
        w = sb("w", [P, 1])
        sq, ln, rstd = ([sb(f"{n}{u}", [P, S]) for u in range(2)] for n in ("sq", "ln", "rstd"))
        var_ps = [ps(f"var{u}", [P, S]) for u in range(2)]
        loaded, sq_ready, var_ready, ln_ready, rstd_ready, z_ready = (
            sem(n) for n in ("loaded", "sq_ready", "var_ready", "ln_ready", "rstd_ready", "z_ready"))
        with nc.Block() as block:
            @block.sync
            def _(sp):
                sp.dma_start(w[:], w_col).then_inc(loaded, 16)

            @block.tensor
            def _(pe):
                for b in range(B):
                    pe.wait_ge(sq_ready, b + 1)
                    if b >= 2:
                        pe.wait_ge(ln_ready, b - 1)
                    nc.tensor.matmul(var_ps[b % 2][:], m.mean_w[:], sq[b % 2][:], start=True, stop=True).then_inc(var_ready, 1)

            @block.scalar
            def _(act):
                nc.scalar.preload_act_table_set(LN_EXP)
                for b in range(B + 1):
                    if b < B:
                        if b >= 2:
                            act.wait_ge(var_ready, b - 1)
                        nc.scalar.activation(sq[b % 2][:], m.xt[:, b * S:(b + 1) * S], ACT.Square).then_inc(sq_ready, 1)
                    if b >= 1:
                        act.wait_ge(var_ready, b)
                        if b >= 3:
                            act.wait_ge(rstd_ready, b - 2)
                        nc.scalar.activation(ln[(b - 1) % 2][:], var_ps[(b - 1) % 2][:], ACT.Ln, bias=m.eps[:]).then_inc(ln_ready, 1)
                        act.wait_ge(ln_ready, b)
                        if b >= 3:
                            act.wait_ge(z_ready, b - 2)
                        nc.scalar.activation(rstd[(b - 1) % 2][:], ln[(b - 1) % 2][:], ACT.Exp, scale=-0.5).then_inc(rstd_ready, 1)

            @block.vector
            def _(dve):
                dve.wait_ge(loaded, 16)
                for b in range(B):
                    dve.wait_ge(rstd_ready, b + 1)
                    nc.vector.scalar_tensor_tensor(out=m.zt[:, b * S:(b + 1) * S], in0=m.xt[:, b * S:(b + 1) * S], scalar=w[:],
                                                   in1=rstd[b % 2][:], op0=ALU.mult, op1=ALU.mult).then_inc(z_ready, 1)


def spiking_mix(nc, m, tag, a):
    with nc.cleanup_on_exit():
        sb, ps, sem = places(nc, tag)
        wr, wk, wv = (sb(n, [P, P]) for n in ("wr", "wk", "wv"))
        w_in = sb("w_in", [P, P])
        w_out = sb("w_out", [P, 1])
        dmask = sb("dmask", [P, P])
        hblock = sb("hblock", [P, P])
        hb = sb("hb", [P, S])
        rt = sb("rt", [P, TB, P])
        rin = sb("rin", [P, TB, P])
        kraw, k0, cnt, kw, kout, v = (sb(n, [P, TB, P]) for n in ("kraw", "k0", "cnt", "kw", "kout", "v"))
        more = [sb(f"more{u}", [P, H, HD, HD]) for u in range(2)]
        kt = sb("kt", [P, TB, P])
        rm = [sb(f"rm{u}", [P, H, P]) for u in range(2)]
        am = [sb(f"am{u}", [P, H, P]) for u in range(2)]
        state, su = sb("state", [P, P]), sb("su", [P, P])
        r_ps, t_ps, y_ps, u_ps = ps("r", [P, S]), ps("t", [P, TB, P]), ps("y", [P, P]), ps("u", [P, P])
        k_ps, v_ps = ps("k", [P, TB, P]), ps("v", [P, TB, P])
        a_ps = [ps(f"a{u}", [P, 4, P]) for u in range(2)]
        names = ("loaded", "hb_ready", "r_ready", "k_ready", "v_ready", "rt_ready", "kraw_ready", "vs_ready", "k0_ready", "more_ready",
                 "cnt_ready", "kw_ready", "kout_ready", "rin_ready", "kt_made", "kt_ready", "rm_ready", "a_ready", "am_ready",
                 "u_ready", "su_ready", "state_ready", "y_ready", "ys_ready")
        loaded, hb_ready, r_ready, k_ready, v_ready, rt_ready, kraw_ready, vs_ready, k0_ready, more_ready, cnt_ready, kw_ready, \
            kout_ready, rin_ready, kt_made, kt_ready, rm_ready, a_ready, am_ready, u_ready, su_ready, state_ready, y_ready, \
            ys_ready = (sem(n) for n in names)
        z_view = m.zt[:].rearrange("p (n f) -> p n f", f=P)
        NL = 7
        with nc.Block() as block:
            @block.sync
            def _(sp):
                for dst, src in ((wr, a["Wr"]), (wk, a["Wk"]), (wv, a["Wv"]), (w_in, a["w_in"]), (w_out, a["w_out"]),
                                 (dmask, a["dmask"]), (hblock, a["hblock"])):
                    sp.dma_start(dst[:], src).then_inc(loaded, 16)

            @block.tensor
            def _(pe):
                pe.wait_ge(loaded, NL * 16)
                with pe.Fori(0, B) as b:
                    pe.wait_ge(hb_ready, b + 1)
                    pe.wait_ge(rt_ready, b)
                    nc.tensor.matmul(r_ps[:], wr[:], hb[:], start=True, stop=True).then_inc(r_ready, 1)
                    pe.wait_ge(kraw_ready, b)
                    for t in range(TB):
                        last = nc.tensor.matmul(k_ps[:, t, :], hb[:, t * P:(t + 1) * P], wk[:], start=True, stop=True)
                    last.then_inc(k_ready, 1)
                    pe.wait_ge(vs_ready, b)
                    for t in range(TB):
                        last = nc.tensor.matmul(v_ps[:, t, :], hb[:, t * P:(t + 1) * P], wv[:], start=True, stop=True)
                    last.then_inc(v_ready, 1)
                    pe.wait_ge(kw_ready, b + 1)
                    pe.wait_ge(kt_ready, b)
                    for t in range(TB):
                        last = nc.tensor.transpose(t_ps[:, t, :], kw[:, t, :], m.ident[:])
                    last.then_inc(kt_made, 1)
                    pe.wait_ge(kt_ready, b + 1)
                    pe.wait_ge(vs_ready, b + 1)
                    pe.wait_ge(kout_ready, b + 1)
                    pe.wait_ge(rin_ready, b + 1)
                    for c in range(TB):
                        n = TB * b + c
                        pe.wait_ge(rm_ready, n + 1)
                        for g in range(4):
                            if g < 2:
                                pe.wait_ge(am_ready, 4 * n)
                            else:
                                pe.wait_ge(am_ready, 4 * n + g - 1)
                            nc.tensor.matmul(a_ps[g % 2][:], kt[:, c, :], rm[c % 2][:, 4 * g:4 * g + 4, :],
                                             start=True, stop=True).then_inc(a_ready, 1)
                        if c + 1 < TB:
                            pe.wait_ge(su_ready, (TB - 1) * b + c)
                            nc.tensor.matmul(u_ps[:], kout[:, c, :], v[:, c, :], start=True, stop=True).then_inc(u_ready, 1)
                        pe.wait_ge(ys_ready, n)
                        if c > 0:
                            pe.wait_ge(state_ready, (TB - 1) * b + c)
                            nc.tensor.matmul(y_ps[:], rin[:, c, :], state[:], start=True, stop=False, skip_group_check=True)
                        for h in range(H):
                            if h % 4 == 0:
                                pe.wait_ge(am_ready, 4 * n + h // 4 + 1)
                            last = nc.tensor.matmul(y_ps[:, h * HD:(h + 1) * HD], am[c % 2][:, h, :], v[:, c, h * HD:(h + 1) * HD],
                                                    start=(c == 0 and h == 0), stop=(h == H - 1), skip_group_check=True)
                        last.then_inc(y_ready, 1)

            @block.scalar
            def _(act):
                nc.scalar.preload_act_table(ACT.Sigmoid)
                with act.Fori(0, B) as b:
                    act.wait_ge(k_ready, b + 1)
                    act.wait_ge(kout_ready, b)
                    nc.scalar.activation(kraw[:], k_ps[:], ACT.Copy).then_inc(kraw_ready, 1)
                    act.wait_ge(r_ready, b + 1)
                    act.wait_ge(rm_ready, TB * b)
                    act.wait_ge(rin_ready, b)
                    nc.scalar.activation(rt[:].rearrange("p t q -> p (t q)"), r_ps[:], ACT.Sigmoid).then_inc(rt_ready, 1)
                    act.wait_ge(v_ready, b + 1)
                    act.wait_ge(y_ready, TB * b)
                    nc.scalar.activation(v[:], v_ps[:], ACT.Copy).then_inc(vs_ready, 1)
                    act.wait_ge(kt_made, b + 1)
                    act.wait_ge(a_ready, 4 * TB * b)
                    nc.scalar.activation(kt[:], t_ps[:], ACT.Copy).then_inc(kt_ready, 1)

            @block.gpsimd
            def _(pool):
                with pool.Fori(0, B) as b:
                    pool.wait_ge(rt_ready, b + 1)
                    for c in range(TB):
                        if c < 2:
                            pool.wait_ge(a_ready, 4 * TB * b)
                        else:
                            pool.wait_ge(a_ready, 4 * (TB * b + c - 1))
                        nc.gpsimd.tensor_tensor(rm[c % 2][:], rt[:, c, :].rearrange("p (h l) -> p h l", h=1).broadcast_to([P, H, P]),
                                                m.hm[:].rearrange("p (h l) -> p h l", l=1).broadcast_to([P, H, P]),
                                                ALU.mult).then_inc(rm_ready, 1)

            @block.vector
            def _(dve):
                dve.wait_ge(loaded, NL * 16)
                with dve.Fori(0, B) as b:
                    dve.wait_ge(v_ready, b)
                    dve.nop(nofuse=True)
                    nc.vector.tensor_copy(hb[:], m.zt[:, ts(b, S)]).then_inc(hb_ready, 1)
                    dve.wait_ge(kraw_ready, b + 1)
                    nc.vector.scalar_tensor_tensor(out=k0[:], in0=kraw[:], scalar=SPIKE, in1=kraw[:], op0=ALU.is_gt,
                                                   op1=ALU.mult).then_inc(k0_ready, 1)
                    dve.wait_ge(k0_ready, b + 1)
                    for t in range(TB):
                        k4 = k0[:, t, :].rearrange("p (h a c) -> p h a c", h=H, a=1)
                        k4t = k0[:, t, :].rearrange("p (h c a) -> p h c a", h=H, a=1)
                        if t >= 2:
                            dve.wait_ge(cnt_ready, TB * b + t - 1)
                        nc.vector.tensor_tensor(more[t % 2][:], k4.broadcast_to([P, H, HD, HD]), k4t.broadcast_to([P, H, HD, HD]),
                                                ALU.is_gt).then_inc(more_ready, 1)
                        dve.wait_ge(more_ready, TB * b + t + 1)
                        nc.vector.tensor_reduce(cnt[:, t, :], more[t % 2][:].rearrange("p h i j -> p (h i) j"), AX.X,
                                                ALU.add).then_inc(cnt_ready, 1)
                    dve.wait_ge(cnt_ready, TB * b + TB)
                    nc.vector.scalar_tensor_tensor(out=kw[:], in0=cnt[:], scalar=float(WINNERS) - 0.5, in1=k0[:],
                                                   op0=ALU.is_lt, op1=ALU.mult).then_inc(kw_ready, 1)
                    dve.wait_ge(kw_ready, b + 1)
                    nc.vector.tensor_scalar(kout[:], kw[:], w_out[:], None, ALU.mult).then_inc(kout_ready, 1)
                    dve.wait_ge(rt_ready, b + 1)
                    nc.vector.tensor_tensor(rin[:], rt[:], w_in[:].rearrange("p (t l) -> p t l", t=1).broadcast_to([P, TB, P]),
                                            ALU.mult).then_inc(rin_ready, 1)
                    for c in range(TB):
                        n = TB * b + c
                        for g in range(4):
                            dve.wait_ge(a_ready, 4 * n + g + 1)
                            if c < 2:
                                dve.wait_ge(y_ready, TB * b)
                            else:
                                dve.wait_ge(y_ready, n - 1)
                            nc.vector.tensor_tensor(am[c % 2][:, 4 * g:4 * g + 4, :], a_ps[g % 2][:],
                                                    dmask[:].rearrange("p (h l) -> p h l", h=1).broadcast_to([P, 4, P]),
                                                    ALU.mult).then_inc(am_ready, 1)
                        if c + 1 < TB:
                            r = (TB - 1) * b + c
                            dve.wait_ge(u_ready, r + 1)
                            dve.wait_ge(state_ready, r)
                            nc.vector.tensor_tensor(su[:], u_ps[:], hblock[:], ALU.mult).then_inc(su_ready, 1)
                            dve.wait_ge(su_ready, r + 1)
                            dve.wait_ge(y_ready, n + (1 if c else 0))
                            if c == 0:
                                nc.vector.tensor_copy(state[:], su[:]).then_inc(state_ready, 1)
                            else:
                                nc.vector.scalar_tensor_tensor(out=state[:], in0=state[:], scalar=DECAY ** P, in1=su[:],
                                                               op0=ALU.mult, op1=ALU.add).then_inc(state_ready, 1)
                        dve.wait_ge(y_ready, n + 1)
                        dve.nop(nofuse=True)
                        nc.vector.tensor_copy(z_view[:, ds(n, 1), :].rearrange("p a f -> p (a f)"), y_ps[:]).then_inc(ys_ready, 1)


def swiglu(nc, m, tag, w1_d, w2_d, w3_d, hidden=4 * P):
    C = hidden // P
    with nc.cleanup_on_exit():
        sb, ps, sem = places(nc, tag)
        w1, w2, w3 = sb("w1", [P, hidden]), sb("w2", [P, hidden]), sb("w3", [P, C, P])
        sg, h = ([sb(f"{n}{u}", [P, S]) for u in range(2)] for n in ("sg", "h"))
        g_ps, u_ps, o_ps = ([ps(f"{n}{u}", [P, S]) for u in range(2)] for n in ("g", "u", "o"))
        loaded, g_ready, u_ready, sg_ready, h_ready, o_ready, o_done, z_ready = (
            sem(n) for n in ("loaded", "g_ready", "u_ready", "sg_ready", "h_ready", "o_ready", "o_done", "z_ready"))
        with nc.Block() as block:
            @block.sync
            def _(sp):
                sp.dma_start(w1[:], w1_d).then_inc(loaded, 16)
                sp.dma_start(w2[:], w2_d).then_inc(loaded, 16)
                sp.dma_start(w3[:], w3_d.rearrange("(c p) m -> p c m", p=P)).then_inc(loaded, 16)

            @block.tensor
            def _(pe):
                pe.wait_ge(loaded, 3 * 16)

                def up(b, c):
                    n = C * b + c
                    if not isinstance(n, int) or n >= 2:
                        pe.wait_ge(sg_ready, n - 1)
                    nc.tensor.matmul(g_ps[c % 2][:], w1[:, c * P:(c + 1) * P], m.zt[:, ts(b, S)], start=True, stop=True).then_inc(g_ready, 1)
                    if not isinstance(n, int) or n >= 2:
                        pe.wait_ge(h_ready, n - 1)
                    nc.tensor.matmul(u_ps[c % 2][:], w2[:, c * P:(c + 1) * P], m.zt[:, ts(b, S)], start=True, stop=True).then_inc(u_ready, 1)

                def batch(b, v, nxt):
                    for c in range(C):
                        if c + 1 < C:
                            up(b, c + 1)
                        elif nxt is not None:
                            up(nxt, 0)
                        pe.wait_ge(h_ready, C * b + c + 1)
                        if c == 0 and not (isinstance(b, int) and b < 2):
                            pe.wait_ge(z_ready, b - 1)
                        nc.tensor.matmul(o_ps[v][:], w3[:, c, :], h[c % 2][:], start=(c == 0), stop=(c == C - 1)).then_inc(o_ready, 1)

                up(0, 0)
                for b in range(B):
                    batch(b, b % 2, b + 1 if b + 1 < B else None)

            @block.scalar
            def _(act):
                nc.scalar.preload_act_table(ACT.Silu)
                for n in range(B * C):
                    act.wait_ge(g_ready, n + 1)
                    if n >= 2:
                        act.wait_ge(h_ready, n - 1)
                    nc.scalar.activation(sg[n % 2][:], g_ps[n % 2][:], ACT.Silu).then_inc(sg_ready, 1)

            @block.vector
            def _(dve):
                for b in range(B):
                    for c in range(C):
                        n = C * b + c
                        dve.wait_ge(sg_ready, n + 1)
                        dve.wait_ge(u_ready, n + 1)
                        if n >= 2:
                            dve.wait_ge(o_ready, n - 1)
                        nc.vector.tensor_tensor(h[c % 2][:], sg[c % 2][:], u_ps[c % 2][:], ALU.mult).then_inc(h_ready, 1)
                    dve.wait_ge(o_ready, C * b + C)
                    nc.vector.tensor_tensor(m.zt[:, b * S:(b + 1) * S], o_ps[b % 2][:], m.xt[:, b * S:(b + 1) * S],
                                            ALU.add).then_inc(z_ready, 1)


def keep_x(nc, m, tag):
    with nc.Block() as block:
        @block.vector
        def _(dve):
            nc.vector.tensor_copy(m.kept[:], m.xt[:])


def add_kept(nc, m, tag):
    with nc.Block() as block:
        @block.vector
        def _(dve):
            nc.vector.tensor_tensor(m.zt[:], m.zt[:], m.kept[:], ALU.add)


def gated_retention_layer(nc, m, tag, a):
    keep_x(nc, m, tag)
    rms_norm(nc, m, tag + "n1", a["n1"])
    spiking_mix(nc, m, tag + "m", a)
    attention_out(nc, m, tag + "o", a["Wo"], a["zero"], a["zero"])
    m.xt, m.zt = m.zt, m.xt
    rms_norm(nc, m, tag + "n2", a["n2"])
    swiglu(nc, m, tag + "s", a["w1"], a["w2"], a["w3"])
    add_kept(nc, m, tag)


DEPTH = 6
DH = 64
INNER = H * DH
W = 32
KS = W + P
FT = INNER // P
DI = 341
CH = [(0, P), (P, P), (2 * P, DI - 2 * P)]
TINY = 1e-24
LIFT = 2.0 ** 40
HIDDEN = -1e20


def windowed_layers(nc, m, tag, a):
    keep_x(nc, m, tag)
    with nc.cleanup_on_exit():
        sb, ps, sem = places(nc, tag)
        g = Model()
        g.tab = [sb(f"tab{i}", [P, S]) for i in range(4)]
        g.ltab = [sb(f"ltab{i}", [P, S]) for i in range(4)]
        g.cols = sb("cols", [P, DEPTH * 4])
        g.mask = sb("mask", [P, 2, KS])
        g.pair = sb("pair", [P, P])
        g.pair2 = sb("pair2", [P, 2])
        g.consts = sb("consts", [P, 2])
        loaded = sem("loaded")
        with nc.Block() as block:
            @block.sync
            def _(sp):
                for i in range(4):
                    sp.dma_start(g.tab[i][:], a["tables"][:, i * S:(i + 1) * S]).then_inc(loaded, 16)
                for dst, src in ((g.cols, "cols"), (g.mask, "mask"), (g.pair, "pair"), (g.pair2, "pair2"), (g.consts, "consts")):
                    sp.dma_start(dst[:], a[src]).then_inc(loaded, 16)
                sp.wait_ge(loaded, 9 * 16)
        with nc.Fori(0, DEPTH) as layer:
            with nc.cleanup_on_exit():
                windowed_attention(nc, m, tag + "a", a, g, layer)
            with nc.cleanup_on_exit():
                gated_layer(nc, m, tag + "f", a, g, layer)
    m.xt, m.zt = m.zt, m.xt
    add_kept(nc, m, tag)


def windowed_attention(nc, m, tag, a, g, layer):
    sb, ps, sem = places(nc, tag)
    wqkv = sb("wqkv", [P, 3 * INNER])
    wrot = sb("wrot", [P, 2 * INNER])
    wo = sb("wo", [P, FT, P])
    with nc.cleanup_on_exit():
        loaded = sem("loaded")
        with nc.Block() as block:
            @block.sync
            def _(sp):
                sp.dma_start(wqkv[:], a["Wqkv"][ds(layer, 1)].rearrange("l p n -> (l p) n")).then_inc(loaded, 16)
                sp.dma_start(wo[:], a["Wo"][ds(layer, 1)].rearrange("l (c p) n -> p (l c) n", p=P)).then_inc(loaded, 16)
                sp.wait_ge(loaded, 3 * 16)

            @block.scalar
            def _(act):
                act.dma_start(wrot[:], a["Wrot"][ds(layer, 1)].rearrange("l p n -> (l p) n")).then_inc(loaded, 16)

            @block.vector
            def _(dve):
                for i in range(4):
                    nc.vector.tensor_scalar(g.ltab[i][:], g.tab[i][:], g.cols[:, ds(layer * 4 + i, 1)], None, ALU.mult)

    xs = sb("xs", [P, S])
    v = sb("v", [P, TB, INNER])
    sq = [sb(f"sq{i}", [P, S]) for i in range(2)]
    rot = [[sb(f"rot{i}{j}", [P, S]) for j in range(2)] for i in range(2)]
    kraw, nk, lnk, rn = (sb(n, [P, S]) for n in ("kraw", "nk", "lnk", "rn"))
    nq, lnq = sb("nq", [P, TB, 2]), sb("lnq", [P, TB, 2])
    scq = [sb(f"scq{u}", [P, TB, 2]) for u in range(2)]
    qt = [sb(f"qt{u}", [P, S]) for u in range(2)]
    kt = [sb(f"kt{u}", [P, W + S]) for u in range(2)]
    s = [sb(f"s{u}", [P, KS]) for u in range(2)]
    ex = [sb(f"ex{u}", [P, 2 * P]) for u in range(2)]
    et = [sb(f"et{u}", [P, 2, P]) for u in range(2)]
    top, ntop, total = (sb(n, [P, 2, 2 * TB]) for n in ("top", "ntop", "total"))
    rec = sb("rec", [P, 2, 2 * TB])
    osb = [sb(f"osb{u}", [P, TB, P]) for u in range(2)]
    ot = sb("ot", [P, FT, S])
    pr_ps = [ps(f"pr{i}", [P, S]) for i in range(3)]
    n_ps = ps("n", [P, S])
    s_ps = [ps(f"s{u}", [P, S]) for u in range(2)]
    t_ps = ps("t", [P, 2, P])
    o_ps = ps("o", [P, 2 * TB, DH])
    with nc.Block() as block:
        @block.vector
        def _(dve):
            for u in range(2):
                nc.vector.memset(kt[u][:, 0:W], 0.0)
                nc.vector.memset(ex[u][:, 0:P - W], 0.0)
            nc.vector.memset(xs[P // 2:P, 0:1], 0.0)

    with nc.Fori(0, B) as b:
      with nc.cleanup_on_exit():
        names = ("xs_ready", "v_ready", "v_dve", "v_act", "pr_ready", "sq_ready", "rot_ready", "rope_ready", "nq_made", "nq_ready",
                 "lnq_ready", "sc_ready", "nk_made", "nk_ready", "lnk_ready", "rn_ready", "kt_ready", "s_ready", "masked_ready",
                 "ntop_ready", "ex_ready", "t_ready", "et_ready", "pv_ready", "rec_ready", "o_ready", "ott_ready", "ot_ready", "z_made")
        xs_ready, v_ready, v_dve, v_act, pr_ready, sq_ready, rot_ready, rope_ready, nq_made, nq_ready, lnq_ready, sc_ready, \
            nk_made, nk_ready, lnk_ready, rn_ready, kt_ready, s_ready, masked_ready, ntop_ready, ex_ready, t_ready, et_ready, \
            pv_ready, rec_ready, o_ready, ott_ready, ot_ready, z_made = (sem(n) for n in names)
        U = 2 * TB
        with nc.Block() as block:
            @block.tensor
            def _(pe):
                def product(f, i):
                    n = 4 * f + i
                    if n >= 3:
                        pe.wait_ge(rot_ready, n - 2)
                    w = wrot if i % 2 else wqkv
                    col = (i // 2) * INNER + f * P
                    nc.tensor.matmul(pr_ps[n % 3][:], w[:, col:col + P], xs[:], start=True, stop=True).then_inc(pr_ready, 1)

                def norms(f, k):
                    pe.wait_ge(sq_ready, 2 * f + k + 1)
                    if f >= 1:
                        pe.wait_ge(nk_ready, f)
                    if f >= 3:
                        pe.wait_ge(ot_ready, f - 2)
                    if k == 0:
                        for t in range(TB):
                            last = nc.tensor.matmul(n_ps[:, 2 * t:2 * t + 2], sq[0][:, t * P:(t + 1) * P], g.pair2[:],
                                                    start=True, stop=True)
                        last.then_inc(nq_made, 1)
                    else:
                        pe.wait_ge(nq_ready, f + 1)
                        nc.tensor.matmul(n_ps[:], g.pair[:], sq[1][:], start=True, stop=True).then_inc(nk_made, 1)

                def scores(f, j):
                    n, t, e = U * f + j, j // 2, j % 2
                    pe.wait_ge(rope_ready, 2 * f + 1)
                    pe.wait_ge(kt_ready, f + 1)
                    if n >= 2:
                        pe.wait_ge(masked_ready, n - 1)
                    rows = slice(e * DH, (e + 1) * DH)
                    nc.tensor.matmul(s_ps[n % 2][:, 0:KS], qt[f % 2][rows, t * P:(t + 1) * P], kt[f % 2][rows, t * P:t * P + KS],
                                     start=True, stop=True).then_inc(s_ready, 1)

                def turn(f, j):
                    n = U * f + j
                    pe.wait_ge(ex_ready, n + 1)
                    if n >= 1:
                        pe.wait_ge(et_ready, n)
                    for c in range(2):
                        last = nc.tensor.transpose(t_ps[:, c, :], ex[n % 2][:, c * P:(c + 1) * P], m.ident[:])
                    last.then_inc(t_ready, 1)

                def values(f, j):
                    n, t, e = U * f + j, j // 2, j % 2
                    pe.wait_ge(et_ready, n + 1)
                    if j == 0 and f >= 1:
                        pe.wait_ge(o_ready, f)
                    cols = slice(f * P + e * DH, f * P + (e + 1) * DH)
                    last = nc.tensor.matmul(o_ps[:, j, :], et[n % 2][:, 1, :], v[:, t, cols], start=True, stop=(t == 0))
                    if t > 0:
                        last = nc.tensor.matmul(o_ps[:, j, :], et[n % 2][P - W:P, 0, :], v[P - W:P, t - 1, cols], start=False, stop=True)
                    last.then_inc(pv_ready, 1)

                def out_turn(f):
                    pe.wait_ge(o_ready, f + 1)
                    if f >= 1:
                        pe.wait_ge(ot_ready, f)
                    pe.wait_ge(nk_ready, min(f + 3, FT))
                    for t in range(TB):
                        last = nc.tensor.transpose(n_ps[:, t * P:(t + 1) * P], osb[f % 2][:, t, :], m.ident[:])
                    last.then_inc(ott_ready, 1)

                pe.wait_ge(xs_ready, 2)
                for i in range(2 * TB):
                    if i >= 3:
                        pe.wait_ge(v_act if i % 2 else v_dve, (i - 3) // 2 + 1)
                    c = 2 * INNER + (i % 2) * S
                    nc.tensor.matmul(pr_ps[i % 3][:], xs[:, (i // 2) * P:(i // 2 + 1) * P], wqkv[:, c:c + S],
                                     start=True, stop=True).then_inc(v_ready, 1)
                pe.wait_ge(v_dve, TB)
                pe.wait_ge(v_act, TB)
                for f in range(FT + 1):
                    p, q = (f if f < FT else None), (f - 1 if f else None)
                    if q is not None:
                        scores(q, 0)
                    for j in range(U):
                        if p is not None:
                            if j < 2:
                                product(p, j)
                            elif j in (3, 4):
                                product(p, j - 1)
                            elif j == 2:
                                norms(p, 0)
                            elif j == 5:
                                norms(p, 1)
                        if j == 6 and q is not None and q >= 1:
                            out_turn(q - 1)
                        if q is not None:
                            if j + 1 < U:
                                scores(q, j + 1)
                            if j >= 1:
                                values(q, j - 1)
                            turn(q, j)
                    if q is not None:
                        values(q, U - 1)
                out_turn(FT - 1)
                pe.wait_ge(ot_ready, FT)
                pe.wait_ge(masked_ready, U * FT)
                for f in range(FT):
                    last = nc.tensor.matmul(s_ps[0][:], wo[:, f, :], ot[:, f, :], start=(f == 0), stop=(f == FT - 1))
                last.then_inc(z_made, 1)

            @block.scalar
            def _(act):
                def squares(f, k):
                    act.wait_ge(pr_ready, 4 * f + 2 * k + 1)
                    if f >= 1:
                        act.wait_ge(nk_made if k else nq_made, f)
                    nc.scalar.activation(sq[k][:], pr_ps[(4 * f + 2 * k) % 3][:], ACT.Square).then_inc(sq_ready, 1)

                def inverse_q(f):
                    act.wait_ge(nq_ready, f + 1)
                    if f >= 1:
                        act.wait_ge(sc_ready, f)
                    nc.scalar.activation(lnq[:], nq[:], ACT.Ln).then_inc(lnq_ready, 1)
                    act.wait_ge(lnq_ready, f + 1)
                    if f >= 2:
                        act.wait_ge(ntop_ready, U * (f - 1))
                        act.wait_ge(ex_ready, U * (f - 1))
                    nc.scalar.activation(scq[f % 2][:], lnq[:], ACT.Exp, scale=-0.5, bias=g.consts[:, 0:1]).then_inc(sc_ready, 1)

                def inverse_k(f):
                    act.wait_ge(nk_ready, f + 1)
                    if f >= 1:
                        act.wait_ge(rn_ready, f)
                    nc.scalar.activation(lnk[:], nk[:], ACT.Ln).then_inc(lnk_ready, 1)
                    act.wait_ge(lnk_ready, f + 1)
                    if f >= 1:
                        act.wait_ge(kt_ready, f)
                    nc.scalar.activation(rn[:], lnk[:], ACT.Exp, scale=-0.5, bias=g.consts[:, 1:2]).then_inc(rn_ready, 1)

                def exps(f, j):
                    n = U * f + j
                    act.wait_ge(ntop_ready, n + 1)
                    act.wait_ge(sc_ready, f + 1)
                    if n >= 2:
                        act.wait_ge(t_ready, n - 1)
                    if j == 0 and f >= 2:
                        act.wait_ge(rec_ready, f - 1)
                    nc.scalar.activation(ex[n % 2][:, P - W:2 * P], s[n % 2][:], ACT.Exp, scale=scq[f % 2][:, j // 2, j % 2:j % 2 + 1],
                                         bias=ntop[:, f % 2, j:j + 1], accum_out=total[:, f % 2, j:j + 1]).then_inc(ex_ready, 1)

                def out_copy(f):
                    act.wait_ge(ott_ready, f + 1)
                    nc.scalar.activation(ot[:, f, :], n_ps[:], ACT.Copy).then_inc(ot_ready, 1)

                nc.scalar.preload_act_table_set(LN_EXP)
                for i in range(0, 2 * TB, 2):
                    act.wait_ge(v_ready, i + 1)
                    nc.scalar.activation(v[:, i // 2, 0:S], pr_ps[i % 3][:], ACT.Copy).then_inc(v_act, 1)
                for f in range(FT + 1):
                    p, q = (f if f < FT else None), (f - 1 if f else None)
                    for j in range(U):
                        if p is not None:
                            if j == 0:
                                squares(p, 0)
                            elif j == 3:
                                squares(p, 1)
                            elif j == 4:
                                inverse_q(p)
                            elif j == 6:
                                inverse_k(p)
                        if q is not None:
                            exps(q, j)
                        if j == 7 and q is not None and q >= 1:
                            out_copy(q - 1)
                out_copy(FT - 1)

            @block.gpsimd
            def _(pool):
                for f in range(FT):
                    for k in range(2):
                        pool.wait_ge(rot_ready, 4 * f + 2 * k + 2)
                        if k == 0 and f >= 2:
                            pool.wait_ge(s_ready, U * (f - 1))
                        if k == 1 and f >= 1:
                            pool.wait_ge(kt_ready, f)
                        nc.gpsimd.tensor_tensor((kraw if k else qt[f % 2])[:], rot[k][0][:], rot[k][1][:], ALU.add).then_inc(rope_ready, 1)
                    pool.wait_ge(rn_ready, f + 1)
                    pool.wait_ge(rope_ready, 2 * f + 2)
                    if f >= 2:
                        pool.wait_ge(s_ready, U * (f - 1))
                    nc.gpsimd.tensor_tensor(kt[f % 2][:, W:W + S], kraw[:], rn[:], ALU.mult).then_inc(kt_ready, 1)

            @block.vector
            def _(dve):
                def rotate(f, i):
                    n = 4 * f + i
                    dve.wait_ge(pr_ready, n + 1)
                    if i % 2 == 0:
                        dve.wait_ge(sq_ready, 2 * f + i // 2 + 1)
                    if f >= 1:
                        dve.wait_ge(rope_ready, 2 * f - 1 + i // 2)
                    nc.vector.tensor_tensor(rot[i // 2][i % 2][:], pr_ps[n % 3][:], g.ltab[i][:], ALU.mult).then_inc(rot_ready, 1)

                def norm_q(f):
                    dve.wait_ge(nq_made, f + 1)
                    if f >= 1:
                        dve.wait_ge(lnq_ready, f)
                    nc.vector.tensor_scalar(nq[:].rearrange("p t e -> p (t e)"), n_ps[:, 0:2 * TB], TINY, LIFT, ALU.max,
                                            ALU.mult).then_inc(nq_ready, 1)

                def norm_k(f):
                    dve.wait_ge(nk_made, f + 1)
                    if f >= 1:
                        dve.wait_ge(lnk_ready, f)
                    nc.vector.tensor_scalar(nk[:], n_ps[:], TINY, LIFT, ALU.max, ALU.mult).then_inc(nk_ready, 1)

                def masked(f, j):
                    n = U * f + j
                    dve.wait_ge(s_ready, n + 1)
                    if n >= 2:
                        dve.wait_ge(ex_ready, n - 1)
                    nc.vector.tensor_tensor_reduce(s[n % 2][:], s_ps[n % 2][:, 0:KS], g.mask[:, min(j // 2, 1), :], 1.0, -3.0e38,
                                                   ALU.add, ALU.max, top[:, f % 2, j:j + 1]).then_inc(masked_ready, 1)
                    dve.wait_ge(masked_ready, n + 1)
                    dve.wait_ge(sc_ready, f + 1)
                    nc.vector.scalar_tensor_tensor(out=ntop[:, f % 2, j:j + 1], in0=top[:, f % 2, j:j + 1], scalar=-1.0,
                                                   in1=scq[f % 2][:, j // 2, j % 2:j % 2 + 1], op0=ALU.mult, op1=ALU.mult).then_inc(ntop_ready, 1)

                def copy(f, j):
                    n = U * f + j
                    dve.wait_ge(t_ready, n + 1)
                    if n >= 2:
                        dve.wait_ge(pv_ready, n - 1)
                    nc.vector.tensor_copy(et[n % 2][:], t_ps[:]).then_inc(et_ready, 1)

                def normed(f):
                    dve.wait_ge(ex_ready, U * f + U)
                    if f >= 2:
                        dve.wait_ge(o_ready, f - 1)
                    nc.vector.reciprocal(rec[:, f % 2, :], total[:, f % 2, :]).then_inc(rec_ready, 1)
                    dve.wait_ge(rec_ready, f + 1)
                    dve.wait_ge(pv_ready, U * f + U)
                    if f >= 2:
                        dve.wait_ge(ott_ready, f - 1)
                    nc.vector.tensor_tensor(osb[f % 2][:].rearrange("p t (e d) -> p (t e) d", e=2), o_ps[:],
                                            rec[:, f % 2, :].rearrange("p (u d) -> p u d", d=1).broadcast_to([P, U, DH]),
                                            ALU.mult).then_inc(o_ready, 1)

                half = P // 2
                nc.vector.tensor_copy(xs[0:half, :], m.xt[0:half, ts(b, S)]).then_inc(xs_ready, 1)
                nc.vector.tensor_copy(xs[half:P, 1:S], m.xt[half:P, ds(b * S, S - 1)]).then_inc(xs_ready, 1)
                for i in range(1, 2 * TB, 2):
                    dve.wait_ge(v_ready, i + 1)
                    nc.vector.tensor_copy(v[:, i // 2, S:2 * S], pr_ps[i % 3][:]).then_inc(v_dve, 1)
                for f in range(FT + 1):
                    p, q = (f if f < FT else None), (f - 1 if f else None)
                    if q is not None:
                        masked(q, 0)
                    for j in range(U):
                        if p is not None:
                            if j < 4:
                                rotate(p, j)
                            if j == 3:
                                norm_q(p)
                            elif j == 6:
                                norm_k(p)
                        if q is not None:
                            if j + 1 < U:
                                masked(q, j + 1)
                            copy(q, j)
                    if q is not None:
                        normed(q)
                dve.wait_ge(z_made, 1)
                nc.vector.tensor_tensor(m.zt[:, ts(b, S)], s_ps[0][:], m.xt[:, ts(b, S)], ALU.add)


def gated_layer(nc, m, tag, a, g, layer):
    sb, ps, sem = places(nc, tag)
    w1, w1g = sb("w1", [P, 2 * DI]), sb("w1g", [P, 2 * DI])
    w2 = sb("w2", [P, 3, P])
    b1 = sb("b1", [P, 6])
    bias = sb("bias", [P, 6])
    lnb = sb("lnb", [P, 3])
    xn = sb("xn", [P, T])
    b_ps = ps("b", [P, 6])
    half = P // 2
    with nc.cleanup_on_exit():
        w_loaded, c_loaded, bias_made, edge = sem("w_loaded"), sem("c_loaded"), sem("bias_made"), sem("edge")
        zero_ready = sem("zero_ready")
        with nc.Block() as block:
            @block.sync
            def _(sp):
                sp.dma_start(w1[:], a["W1"][ds(layer, 1)].rearrange("l p n -> (l p) n")).then_inc(w_loaded, 16)
                sp.dma_start(b1[:], a["b1"][:, ds(layer * 6, 6)]).then_inc(c_loaded, 16)
                sp.dma_start(lnb[:], a["lnb"][:, ds(layer * 3, 3)]).then_inc(c_loaded, 16)
                for c, (lo, n) in enumerate(CH):
                    sp.dma_start(w2[0:n, c, :], a["W2"][ds(layer, 1), lo:lo + n, :].rearrange("l p n -> (l p) n")).then_inc(c_loaded, 16)
                sp.wait_ge(c_loaded, 5 * 16)

            @block.gpsimd
            def _(pool):
                nc.gpsimd.memset(xn[half:P, :].rearrange("p (b s) -> p b s", b=B)[:, :, 0:1], 0.0).then_inc(edge, 1)

            @block.vector
            def _(dve):
                for i in range(B):
                    nc.vector.tensor_copy(xn[half:P, i * S + 1:(i + 1) * S], m.zt[half:P, i * S:(i + 1) * S - 1])
                nc.vector.memset(bias[:], 0.0).then_inc(zero_ready, 1)
                dve.wait_ge(w_loaded, 16)
                dve.wait_ge(c_loaded, 5 * 16)
                nc.vector.tensor_scalar(w1g[:], w1[:], lnb[:, 0:1], None, ALU.mult)
                dve.wait_ge(bias_made, 1)
                dve.wait_ge(zero_ready, 1)
                for i in range(6):
                    n = CH[i % 3][1]
                    nc.vector.tensor_tensor(bias[0:n, i:i + 1], b_ps[0:n, i:i + 1], b1[0:n, i:i + 1], ALU.add)

            @block.scalar
            def _(act):
                nc.scalar.activation(xn[0:half, :], m.zt[0:half, :], ACT.Copy)

            @block.tensor
            def _(pe):
                pe.wait_ge(w_loaded, 16)
                pe.wait_ge(c_loaded, 5 * 16)
                for i in range(6):
                    lo, n = CH[i % 3]
                    lo += (i // 3) * DI
                    last = nc.tensor.matmul(b_ps[0:n, i:i + 1], w1[:, lo:lo + n], lnb[:, 1:2], start=True, stop=True)
                last.then_inc(bias_made, 1)
    layer_norm(nc, m, tag + "n", xn, xn)
    with nc.cleanup_on_exit():
        ge, h = ([sb(f"{n}{i}", [P, S]) for i in range(3)] for n in ("ge", "h"))
        g_ps, a_ps = ([ps(f"{n}{i}", [P, S]) for i in range(3)] for n in ("g", "a"))
        o_ps = ps("o", [P, S])
        g_ready, ge_ready, a_ready, h_ready, o_ready, x_ready = (
            sem(n) for n in ("g_ready", "ge_ready", "a_ready", "h_ready", "o_ready", "x_ready"))
        with nc.Block() as block:
            @block.tensor
            def _(pe):
                def up(i, c):
                    lo, n = CH[c]
                    if i:
                        pe.wait_ge(ge_ready, 3 * (i - 1) + c + 1)
                    nc.tensor.matmul(g_ps[c][0:n, :], w1g[:, DI + lo:DI + lo + n], xn[:, i * S:(i + 1) * S],
                                     start=True, stop=True).then_inc(g_ready, 1)
                    if i:
                        pe.wait_ge(h_ready, 3 * (i - 1) + c + 1)
                    nc.tensor.matmul(a_ps[c][0:n, :], w1g[:, lo:lo + n], xn[:, i * S:(i + 1) * S],
                                     start=True, stop=True).then_inc(a_ready, 1)

                for c in range(3):
                    up(0, c)
                for i in range(B):
                    for c in range(3):
                        n = CH[c][1]
                        pe.wait_ge(h_ready, 3 * i + c + 1)
                        if c == 0 and i:
                            pe.wait_ge(x_ready, i)
                        nc.tensor.matmul(o_ps[:], w2[0:n, c, :], h[c][0:n, :], start=(c == 0), stop=(c == 2)).then_inc(o_ready, 1)
                        if i + 1 < B:
                            up(i + 1, c)

            @block.scalar
            def _(act):
                nc.scalar.preload_act_table(ACT.Gelu)
                for i in range(B):
                    for c in range(3):
                        n = CH[c][1]
                        act.wait_ge(g_ready, 3 * i + c + 1)
                        if i:
                            act.wait_ge(h_ready, 3 * (i - 1) + c + 1)
                        nc.scalar.activation(ge[c][0:n, :], g_ps[c][0:n, :], ACT.Gelu, bias=bias[0:n, 3 + c:4 + c]).then_inc(ge_ready, 1)

            @block.vector
            def _(dve):
                for i in range(B):
                    for c in range(3):
                        n = CH[c][1]
                        dve.wait_ge(ge_ready, 3 * i + c + 1)
                        dve.wait_ge(a_ready, 3 * i + c + 1)
                        if i:
                            dve.wait_ge(o_ready, 3 * (i - 1) + c + 1)
                        nc.vector.scalar_tensor_tensor(out=h[c][0:n, :], in0=a_ps[c][0:n, :], scalar=bias[0:n, c:c + 1],
                                                       in1=ge[c][0:n, :], op0=ALU.add, op1=ALU.mult).then_inc(h_ready, 1)
                    dve.wait_ge(o_ready, 3 * i + 3)
                    nc.vector.scalar_tensor_tensor(out=m.xt[:, i * S:(i + 1) * S], in0=o_ps[:], scalar=lnb[:, 2:3],
                                                   in1=m.zt[:, i * S:(i + 1) * S], op0=ALU.add, op1=ALU.add).then_inc(x_ready, 1)


def model(nc, a):
    m = Model()
    m.xt, m.zt, m.kept, m.ident, m.mean_w, m.eps, m.hm = (
        nc.alloc_sbuf_tensor(f"model_{name}", shape, F32) for name, shape in
        (("xt", [P, T]), ("zt", [P, T]), ("kept", [P, T]), ("ident", [P, P]), ("mean_w", [P, P]), ("eps", [P, 1]), ("hm", [P, H])))
    scratch = [nc.dram_tensor(f"scratch{u}", [S * (S + 1)], F32).ap() for u in range(2)]
    with nc.cleanup_on_exit():
        loaded = nc.alloc_semaphore("model_loaded")
        with nc.Block() as block:
            @block.sync
            def _(sp):
                for dst, name in ((m.xt, "x"), (m.ident, "ident"), (m.mean_w, "mean_w"), (m.eps, "eps"), (m.hm, "hm")):
                    sp.dma_start(dst[:], a[name]).then_inc(loaded, 16)
                sp.wait_ge(loaded, 5 * 16)

    def of(prefix):
        return {name[len(prefix):]: ap for name, ap in a.items() if name.startswith(prefix)}

    relative_attention(nc, m, "l0a", of("L0_attn_"), scratch)
    attention_out(nc, m, "l0o", a["L0_attn_Wo"], a["L0_attn_bv"], a["L0_attn_bo"])
    layer_norm(nc, m, "n0")
    channel_mix(nc, m, "l0f", *(a["L0_ffn_" + n] for n in ("W_r", "W_k", "W_v", "mu_r", "mu_k")))
    layer_norm(nc, m, "n1")
    batch_softmax_attention(nc, m, "l1a", *(a["L1_attn_" + n] for n in ("w_q", "w_k", "w_v", "W_o")), a["zero"])
    layer_norm(nc, m, "n2")
    experts(nc, m, "l1f", of("L1_ffn_"))
    layer_norm(nc, m, "n3")
    linear_attention(nc, m, "l2a", *(a["L2_attn_" + n] for n in ("Wq", "Wk", "Wv", "bq", "bk", "bv")))
    layer_norm(nc, m, "n4")
    windowed_layers(nc, m, "l2f", of("L2_ffn_"))
    layer_norm(nc, m, "n5")
    gated_retention_layer(nc, m, "l3a", {**of("L3_attn_"), "zero": a["zero"]})
    layer_norm(nc, m, "n6")
    channel_mix(nc, m, "l3f", *(a["L3_ffn_" + n] for n in ("W_r", "W_k", "W_v", "mu_r", "mu_k")))
    layer_norm(nc, m, "n7")
    with nc.cleanup_on_exit():
        stored = nc.alloc_semaphore("model_stored")
        with nc.Block() as block:
            @block.sync
            def _(sp):
                sp.dma_start(a["out"], m.xt[:]).then_inc(stored, 16)
                sp.wait_ge(stored, 16)


def shape_constants():
    f = np.float32
    i = np.arange(P)
    c = {"ident": np.eye(P, dtype=f), "mean_w": np.full((P, P), 1 / P, f), "eps": np.full((P, 1), EPS, f),
         "zero": np.zeros((P, 1), f), "hm": (i[:, None] // HD == np.arange(H)[None]).astype(f)}
    inv = (1.0 / 10000.0 ** (2.0 * np.arange(P // 2, dtype=f) / P)).astype(f)
    ang = np.arange(S, dtype=f)[:, None] * inv[None]
    c["L0_attn_feat"] = np.concatenate([np.sin(ang), np.cos(ang)], -1).T
    c["L1_ffn_before"] = np.triu(np.ones((P, P), f))
    c["L1_ffn_first"] = np.broadcast_to(np.arange(E, 0, -1), (P, E))
    half = np.arange(0, DH, 2, dtype=f)
    freqs = np.arange(S, dtype=f)[:, None] * (f(1) / f(10000) ** (half / f(DH))).astype(f)[None]
    freqs = np.concatenate([freqs, freqs], -1)
    base = ((half + f(0.4 * DH)) / f(1.4 * DH)).astype(f)
    power = ((np.arange(S, dtype=f) - f(S // 2)) / f(W // 2)).astype(f)
    scale = (base[None] ** power[:, None]).astype(f)
    scale = np.concatenate([scale, scale], -1)
    cos, sin = np.cos(freqs), np.sin(freqs) * np.where(np.arange(DH) < DH // 2, -1, 1).astype(f)
    c["L2_ffn_tables"] = np.concatenate([np.tile(x.T, (2, 1)) for x in (cos * scale, sin * scale, cos / scale, sin / scale)], 1)
    seen = (np.arange(KS)[None] >= i[:, None]) & (np.arange(KS)[None] <= i[:, None] + W)
    c["L2_ffn_mask"] = np.stack([np.where(seen & (np.arange(KS)[None] >= W), 0, HIDDEN), np.where(seen, 0, HIDDEN)], 1)
    c["L2_ffn_pair"] = i[:, None] // DH == i[None] // DH
    c["L2_ffn_pair2"] = i[:, None] // DH == np.arange(2)[None]
    c["L2_ffn_consts"] = np.tile([np.log(8) + np.log(LIFT) / 2, np.log(LIFT) / 2], (P, 1))
    c["L3_attn_w_in"] = np.broadcast_to(f(DECAY) ** (i + 1), (P, P))
    c["L3_attn_w_out"] = (f(DECAY) ** (P - 1 - i))[:, None]
    ahead = i[None] - i[:, None]
    c["L3_attn_dmask"] = np.where(ahead >= 0, DECAY ** np.maximum(ahead, 0), 0)
    c["L3_attn_hblock"] = i[:, None] // HD == i[None] // HD
    return {name: np.ascontiguousarray(v, dtype=f) for name, v in c.items()}


def layouts(d):
    a = {n: v for n, v in d.items()}
    a["x"] = a.pop("L0_attn_x").reshape(T, P).T
    for n in ("W_r", "W_k", "W_v"):
        for layer in ("L0_ffn_", "L3_ffn_"):
            a[layer + n] = d[layer + n].T
    for n in ("Wq", "Wk", "Wv"):
        a["L2_attn_" + n] = d["L2_attn_" + n].T
    a["L2_attn_bq"] = np.broadcast_to(d["L2_attn_bq"], (P, P))
    for n in ("bq", "bk", "bv", "bp", "bo", "u", "v"):
        a["L0_attn_" + n] = d["L0_attn_" + n].reshape(P, 1)
    for n in ("L0_ffn_mu_r", "L0_ffn_mu_k", "L3_ffn_mu_r", "L3_ffn_mu_k", "L2_attn_bk", "L2_attn_bv"):
        a[n] = d[n].reshape(P, 1)
    a["L3_attn_n1"], a["L3_attn_n2"] = a.pop("L3_attn_norm1_w").reshape(P, 1), a.pop("L3_attn_norm2_w").reshape(P, 1)
    a["L1_ffn_b1"] = d["L1_ffn_b1"].reshape(E, FF // P, P).transpose(2, 0, 1).reshape(P, E * FF // P)
    other = np.arange(DH) ^ (DH // 2)
    q_k = d["L2_ffn_Wqkv"][:, :, :2 * INNER]
    a["L2_ffn_Wrot"] = q_k.reshape(DEPTH, P, 2 * H, DH)[..., other].reshape(DEPTH, P, 2 * INNER)
    scales = (a.pop("L2_ffn_q_scale"), a.pop("L2_ffn_k_scale"))
    cols = np.stack([np.tile(v[:, o], (1, 2)) for v in scales for o in (slice(None), other)], 1)
    a["L2_ffn_cols"] = cols.transpose(2, 0, 1).reshape(P, DEPTH * 4)
    b1 = np.zeros((DEPTH, 6, P), np.float32)
    for k in range(6):
        lo, n = CH[k % 3]
        b1[:, k, :n] = d["L2_ffn_b1"][:, (k // 3) * DI + lo:(k // 3) * DI + lo + n]
    a["L2_ffn_b1"] = b1.transpose(2, 0, 1).reshape(P, DEPTH * 6)
    lnb = np.stack([a.pop("L2_ffn_" + n) for n in ("ln_g", "ln_b", "b2")], 1)
    a["L2_ffn_lnb"] = lnb.transpose(2, 0, 1).reshape(P, DEPTH * 3)
    return {n: np.ascontiguousarray(v) for n, v in a.items()}


def kernel(**inputs):
    import concourse.bacc as bacc
    from concourse.bass_utils import run_bass_kernel_spmd as run

    arrays = {**layouts({n: np.asarray(v) for n, v in inputs.items()}), **shape_constants()}
    nc = bacc.Bacc("TRN2", target_bir_lowering=False, num_devices=1)
    args = {n: nc.dram_tensor(f"in_{n}", v.shape, mybir.dt.from_np(v.dtype), kind="ExternalInput").ap()
            for n, v in arrays.items()}
    args["out"] = nc.dram_tensor("out", [P, T], F32, kind="ExternalOutput").ap()
    model(nc, args)
    result = run(nc, [{f"in_{n}": v for n, v in arrays.items()}], core_ids=[0]).results[0]["out"]
    return np.ascontiguousarray(result.T).reshape(B, S, P)
```

```python
import numpy as np

import concourse.bass as bass
from concourse import mybir

F32 = mybir.dt.float32
BF16 = mybir.dt.bfloat16
ALU = mybir.AluOpType
ACT = mybir.ActivationFunctionType
AX = mybir.AxisListType
ts, ds = bass.ts, bass.ds

P = 128
B, S = 8, 512
T = B * S
NT = T // P
TB = S // P
H = 16
HD = P // H
EPS = 1e-5


class Model:
    pass


def places(nc, tag):
    def sb(name, shape, dt=F32):
        return nc.alloc_sbuf_tensor(f"{tag}_{name}", shape, dt)

    def ps(name, shape, dt=F32):
        return nc.alloc_psum_tensor(f"{tag}_{name}_psum", shape, dt)

    def sem(name):
        return nc.alloc_semaphore(f"{tag}_{name}")
    return sb, ps, sem


LN_EXP = "natural_log_exp_and_others"


def rounds(engine, n):
    yield 0
    with engine.Fori(1, n) as i:
        yield i


def layer_norm(nc, m, tag, src=None, dst=None):
    src, dst = src or m.zt, dst or m.xt
    with nc.cleanup_on_exit():
        sb, ps, sem = places(nc, tag)
        mean_ps = [ps(f"mean{u}", [P, S]) for u in range(2)]
        var_ps = [ps(f"var{u}", [P, S]) for u in range(2)]
        cent = [sb(f"cent{u}", [P, S]) for u in range(2)]
        sq = [sb(f"sq{u}", [P, S]) for u in range(2)]
        ln = [sb(f"ln{u}", [P, S]) for u in range(2)]
        rstd = [sb(f"rstd{u}", [P, S]) for u in range(2)]
        mean_ready, cent_ready, sq_ready, var_ready, ln_ready, rstd_ready, x_ready = (
            sem(n) for n in ("mean_ready", "cent_ready", "sq_ready", "var_ready", "ln_ready", "rstd_ready", "x_ready"))
        with nc.Block() as block:
            @block.tensor
            def _(pe):
                for pair in rounds(pe, B // 2):
                    b = 2 * pair
                    for u in range(2):
                        pe.wait_ge(cent_ready, b)
                        nc.tensor.matmul(mean_ps[u][:], m.mean_w[:], src[:, ts(b + u, S)],
                                         start=True, stop=True).then_inc(mean_ready, 1)
                    for u in range(2):
                        pe.wait_ge(sq_ready, b + u + 1)
                        pe.wait_ge(ln_ready, b)
                        nc.tensor.matmul(var_ps[u][:], m.mean_w[:], sq[u][:],
                                         start=True, stop=True).then_inc(var_ready, 1)

            @block.scalar
            def _(act):
                nc.scalar.preload_act_table_set(LN_EXP)
                for pair in rounds(act, B // 2):
                    b = 2 * pair
                    for u in range(2):
                        act.wait_ge(cent_ready, b + u + 1)
                        act.wait_ge(var_ready, b)
                        nc.scalar.activation(sq[u][:], cent[u][:], ACT.Square).then_inc(sq_ready, 1)
                    for u in range(2):
                        act.wait_ge(var_ready, b + u + 1)
                        nc.scalar.activation(ln[u][:], var_ps[u][:], ACT.Ln, bias=m.eps[:]).then_inc(ln_ready, 1)
                    for u in range(2):
                        act.wait_ge(ln_ready, b + u + 1)
                        act.wait_ge(x_ready, b)
                        nc.scalar.activation(rstd[u][:], ln[u][:], ACT.Exp, scale=-0.5).then_inc(rstd_ready, 1)

            @block.vector
            def _(dve):
                for pair in rounds(dve, B // 2):
                    b = 2 * pair
                    for u in range(2):
                        dve.wait_ge(mean_ready, b + u + 1)
                        dve.wait_ge(x_ready, b)
                        nc.vector.tensor_tensor(cent[u][:], src[:, ts(b + u, S)], mean_ps[u][:],
                                                ALU.subtract).then_inc(cent_ready, 1)
                    for u in range(2):
                        dve.wait_ge(rstd_ready, b + u + 1)
                        dve.wait_ge(cent_ready, b + u + 1)
                        nc.vector.tensor_tensor(dst[:, ts(b + u, S)], cent[u][:], rstd[u][:],
                                                ALU.mult).then_inc(x_ready, 1)


def channel_mix(nc, m, tag, w_rT, w_kT, w_vT, mu_r, mu_k):
    with nc.cleanup_on_exit():
        sb, ps, sem = places(nc, tag)
        wr, wk, wv = (sb(n, [P, P]) for n in ("wr", "wk", "wv"))
        mu = sb("mu", [P, 2])
        onemu = sb("onemu", [P, 2])
        prev = [[sb(f"prev{i}{u}", [P, S]) for u in range(2)] for i in range(2)]
        mix = [[sb(f"mix{i}{u}", [P, S]) for u in range(2)] for i in range(2)]
        gate, kk, ksq, rv = ([sb(f"{n}{u}", [P, S]) for u in range(2)] for n in ("gate", "kk", "ksq", "rv"))
        r_ps, k_ps, v_ps = ([ps(f"{n}{u}", [P, S]) for u in range(2)] for n in ("r", "k", "v"))
        loaded, onemu_ready, edge_ready, prev_ready, mix_ready, r_ready, k_ready, gate_ready, relu_ready, \
            ksq_ready, v_ready, rv_ready, z_ready = (sem(n) for n in (
                "loaded", "onemu_ready", "edge_ready", "prev_ready", "mix_ready", "r_ready", "k_ready", "gate_ready",
                "relu_ready", "ksq_ready", "v_ready", "rv_ready", "z_ready"))
        with nc.Block() as block:
            @block.sync
            def _(sp):
                sp.dma_start(mu[:, 0:1], mu_r).then_inc(loaded, 16)
                sp.dma_start(mu[:, 1:2], mu_k).then_inc(loaded, 16)
                for dst, src in ((wr, w_rT), (wk, w_kT), (wv, w_vT)):
                    sp.dma_start(dst[:], src).then_inc(loaded, 16)

            @block.gpsimd
            def _(pool):
                for i in range(2):
                    for u in range(2):
                        nc.gpsimd.memset(prev[i][u][:, 0:1], 0.0).then_inc(edge_ready, 1)

            @block.scalar
            def _(act):
                nc.scalar.preload_act_table(ACT.Sigmoid)
                for pair in rounds(act, B // 2):
                    b = 2 * pair
                    for u in range(2):
                        act.wait_ge(mix_ready, 2 * b)
                        act.wait_ge(onemu_ready, 1)
                        for i in range(2):
                            nc.scalar.activation(prev[i][u][:, 1:S], m.xt[:, ds((b + u) * S, S - 1)], ACT.Copy,
                                                 scale=onemu[:, i:i + 1]).then_inc(prev_ready, 1)
                    for u in range(2):
                        act.wait_ge(r_ready, b + u + 1)
                        act.wait_ge(rv_ready, b)
                        nc.scalar.activation(gate[u][:], r_ps[u][:], ACT.Sigmoid).then_inc(gate_ready, 1)
                        act.wait_ge(k_ready, b + u + 1)
                        act.wait_ge(ksq_ready, b)
                        nc.scalar.activation(kk[u][:], k_ps[u][:], ACT.Relu).then_inc(relu_ready, 1)
                    for u in range(2):
                        act.wait_ge(relu_ready, b + u + 1)
                        act.wait_ge(v_ready, b)
                        nc.scalar.activation(ksq[u][:], kk[u][:], ACT.Square).then_inc(ksq_ready, 1)

            @block.vector
            def _(dve):
                dve.wait_ge(loaded, 5 * 16)
                nc.vector.tensor_scalar(onemu[:], mu[:], -1.0, 1.0, ALU.mult, ALU.add).then_inc(onemu_ready, 1)
                dve.wait_ge(edge_ready, 4)
                for pair in rounds(dve, B // 2):
                    b = 2 * pair
                    for u in range(2):
                        for i, used in ((0, r_ready), (1, k_ready)):
                            dve.wait_ge(prev_ready, 2 * (b + u) + i + 1)
                            dve.wait_ge(used, b)
                            nc.vector.scalar_tensor_tensor(out=mix[i][u][:], in0=m.xt[:, ts(b + u, S)],
                                                           scalar=mu[:, i:i + 1], in1=prev[i][u][:],
                                                           op0=ALU.mult, op1=ALU.add).then_inc(mix_ready, 1)
                    for u in range(2):
                        dve.wait_ge(v_ready, b + u + 1)
                        dve.wait_ge(gate_ready, b + u + 1)
                        dve.wait_ge(z_ready, b)
                        nc.vector.tensor_tensor(rv[u][:], v_ps[u][:], gate[u][:], ALU.mult).then_inc(rv_ready, 1)
                    for u in range(2):
                        dve.wait_ge(rv_ready, b + u + 1)
                        nc.vector.tensor_tensor(m.zt[:, ts(b + u, S)], rv[u][:], m.xt[:, ts(b + u, S)],
                                                ALU.add).then_inc(z_ready, 1)

            @block.tensor
            def _(pe):
                pe.wait_ge(loaded, 5 * 16)
                for pair in rounds(pe, B // 2):
                    b = 2 * pair
                    for u in range(2):
                        pe.wait_ge(mix_ready, 2 * (b + u) + 1)
                        pe.wait_ge(gate_ready, b)
                        nc.tensor.matmul(r_ps[u][:], wr[:], mix[0][u][:], start=True, stop=True).then_inc(r_ready, 1)
                        pe.wait_ge(mix_ready, 2 * (b + u) + 2)
                        pe.wait_ge(relu_ready, b)
                        nc.tensor.matmul(k_ps[u][:], wk[:], mix[1][u][:], start=True, stop=True).then_inc(k_ready, 1)
                    for u in range(2):
                        pe.wait_ge(ksq_ready, b + u + 1)
                        pe.wait_ge(rv_ready, b)
                        nc.tensor.matmul(v_ps[u][:], wv[:], ksq[u][:], start=True, stop=True).then_inc(v_ready, 1)


def linear_attention(nc, m, tag, w_qT, w_kT, w_vT, bq_rows, bk_col, bv_col):
    scale = float(P) ** -0.5
    with nc.cleanup_on_exit():
        sb, ps, sem = places(nc, tag)
        wq, wk, wv = (sb(n, [P, P]) for n in ("wq", "wk", "wv"))
        bq = sb("bq", [P, P])
        bkv = sb("bkv", [P, 2])
        xb = sb("xb", [P, S])
        q, qd, qe, qn = (sb(n, [P, TB, P]) for n in ("q", "qd", "qe", "qn"))
        qmax, qsum, qrec = (sb(n, [P, TB]) for n in ("qmax", "qsum", "qrec"))
        kve = [sb(f"kve{i}", [P, S]) for i in range(2)]
        kvn = [sb(f"kvn{i}", [P, S]) for i in range(2)]
        kvmax, kvbias, kvsum, kvrec = (sb(n, [P, 2]) for n in ("kvmax", "kvbias", "kvsum", "kvrec"))
        kvt = [sb(f"kvt{i}", [P, TB, P]) for i in range(2)]
        qt = sb("qt", [P, S])
        kv = sb("kv", [P, P])
        q_ps = ps("qps", [P, TB, P])
        kv_ps = [ps(f"kvps{i}", [P, S]) for i in range(2)]
        t_ps = [ps(f"tps{i}", [P, TB, P]) for i in range(3)]
        c_ps = ps("cps", [P, P])
        o_ps = ps("ops", [P, S])
        loaded, xb_ready, q_ready, kv_ready, qb_ready, qmax_ready, qd_ready, qe_ready, qsum_ready, qrec_ready, qn_ready, \
            kvmax_ready, kvtop_ready, kvbias_ready, kve_ready, kvrec_ready, kvn_ready, t_ready, kvt_ready, qt_ready, c_ready, \
            kvc_ready, o_ready, z_ready = (sem(n) for n in (
                "loaded", "xb_ready", "q_ready", "kv_ready", "qb_ready", "qmax_ready", "qd_ready", "qe_ready",
                "qsum_ready", "qrec_ready", "qn_ready", "kvmax_ready", "kvtop_ready", "kvbias_ready", "kve_ready",
                "kvrec_ready", "kvn_ready", "t_ready", "kvt_ready", "qt_ready", "c_ready", "kvc_ready", "o_ready", "z_ready"))
        with nc.Block() as block:
            @block.sync
            def _(sp):
                for dst, src in ((wq[:], w_qT), (wk[:], w_kT), (wv[:], w_vT), (bq[:], bq_rows),
                                 (bkv[:, 0:1], bk_col), (bkv[:, 1:2], bv_col)):
                    sp.dma_start(dst, src).then_inc(loaded, 16)

            @block.tensor
            def _(pe):
                pe.wait_ge(loaded, 6 * 16)
                for b in rounds(pe, B):
                    pe.wait_ge(xb_ready, b + 1)
                    pe.wait_ge(qb_ready, b)
                    for t in range(TB):
                        last = nc.tensor.matmul(q_ps[:, t, :], xb[:, t * P:(t + 1) * P], wq[:], start=True, stop=True)
                    last.then_inc(q_ready, 1)
                    for i, w in enumerate((wk, wv)):
                        pe.wait_ge(kve_ready, 2 * b)
                        nc.tensor.matmul(kv_ps[i][:], w[:], xb[:], start=True, stop=True).then_inc(kv_ready, 1)
                    for i in range(2):
                        pe.wait_ge(kvn_ready, 2 * b + i + 1)
                        for t in range(TB):
                            last = nc.tensor.transpose(t_ps[i][:, t, :], kvn[i][:, t * P:(t + 1) * P], m.ident[:])
                        last.then_inc(t_ready, 1)
                    pe.wait_ge(qn_ready, b + 1)
                    for t in range(TB):
                        last = nc.tensor.transpose(t_ps[2][:, t, :], qn[:, t, :], m.ident[:])
                    last.then_inc(t_ready, 1)
                    pe.wait_ge(kvt_ready, 2 * b + 2)
                    pe.wait_ge(kvc_ready, b)
                    for t in range(TB):
                        last = nc.tensor.matmul(c_ps[:], kvt[0][:, t, :], kvt[1][:, t, :],
                                                start=(t == 0), stop=(t == TB - 1))
                    last.then_inc(c_ready, 1)
                    pe.wait_ge(kvc_ready, b + 1)
                    pe.wait_ge(qt_ready, b + 1)
                    pe.wait_ge(z_ready, b)
                    nc.tensor.matmul(o_ps[:], kv[:], qt[:], start=True, stop=True).then_inc(o_ready, 1)

            @block.scalar
            def _(act):
                for b in rounds(act, B):
                    act.wait_ge(qd_ready, b + 1)
                    act.wait_ge(qn_ready, b)
                    nc.scalar.activation(qe[:], qd[:], ACT.Exp).then_inc(qe_ready, 1)
                    for i in range(2):
                        act.wait_ge(kvbias_ready, b + 1)
                        act.wait_ge(kvn_ready, 2 * b)
                        nc.scalar.activation(kve[i][:], kv_ps[i][:], ACT.Exp, bias=kvbias[:, i:i + 1],
                                             accum_out=kvsum[:, i:i + 1]).then_inc(kve_ready, 1)
                    for i in range(2):
                        act.wait_ge(t_ready, 3 * b + i + 1)
                        act.wait_ge(c_ready, b)
                        nc.scalar.activation(kvt[i][:], t_ps[i][:], ACT.Copy).then_inc(kvt_ready, 1)
                    act.wait_ge(t_ready, 3 * b + 3)
                    act.wait_ge(o_ready, b)
                    nc.scalar.activation(qt[:], t_ps[2][:].rearrange("p t q -> p (t q)"), ACT.Copy).then_inc(qt_ready, 1)

            @block.vector
            def _(dve):
                dve.wait_ge(loaded, 6 * 16)
                for b in rounds(dve, B):
                    dve.wait_ge(kv_ready, 2 * b)
                    nc.vector.tensor_copy(xb[:], m.xt[:, ts(b, S)]).then_inc(xb_ready, 1)
                    dve.wait_ge(q_ready, b + 1)
                    nc.vector.tensor_tensor(q[:], q_ps[:], bq[:].rearrange("p (t q) -> p t q", t=1).broadcast_to([P, TB, P]),
                                            ALU.add).then_inc(qb_ready, 1)
                    dve.wait_ge(qb_ready, b + 1)
                    nc.vector.tensor_reduce(qmax[:], q[:], AX.X, ALU.max).then_inc(qmax_ready, 1)
                    dve.wait_ge(qmax_ready, b + 1)
                    nc.vector.tensor_tensor(qd[:], q[:], qmax[:].rearrange("p (t q) -> p t q", q=1).broadcast_to([P, TB, P]),
                                            ALU.subtract).then_inc(qd_ready, 1)
                    for i in range(2):
                        dve.wait_ge(kv_ready, 2 * b + i + 1)
                        nc.vector.tensor_reduce(kvmax[:, i:i + 1], kv_ps[i][:], AX.X, ALU.max).then_inc(kvmax_ready, 1)
                    dve.wait_ge(kvmax_ready, 2 * b + 2)
                    nc.vector.tensor_tensor(kvbias[:], kvmax[:], bkv[:], ALU.add).then_inc(kvtop_ready, 1)
                    dve.wait_ge(kvtop_ready, b + 1)
                    nc.vector.tensor_tensor(kvbias[:], bkv[:], kvbias[:], ALU.subtract).then_inc(kvbias_ready, 1)
                    dve.wait_ge(qe_ready, b + 1)
                    nc.vector.tensor_reduce(qsum[:], qe[:], AX.X, ALU.add).then_inc(qsum_ready, 1)
                    dve.wait_ge(qsum_ready, b + 1)
                    nc.vector.reciprocal(qrec[:], qsum[:]).then_inc(qrec_ready, 1)
                    dve.wait_ge(qrec_ready, b + 1)
                    nc.vector.tensor_tensor(qn[:], qe[:], qrec[:].rearrange("p (t q) -> p t q", q=1).broadcast_to([P, TB, P]),
                                            ALU.mult).then_inc(qn_ready, 1)
                    dve.wait_ge(kve_ready, 2 * b + 2)
                    nc.vector.reciprocal(kvrec[:], kvsum[:]).then_inc(kvrec_ready, 1)
                    dve.wait_ge(kvrec_ready, b + 1)
                    for i in range(2):
                        nc.vector.tensor_scalar(kvn[i][:], kve[i][:], kvrec[:, i:i + 1], (scale, 1.0)[i],
                                                ALU.mult, ALU.mult).then_inc(kvn_ready, 1)
                    dve.wait_ge(c_ready, b + 1)
                    dve.wait_ge(o_ready, b)
                    nc.vector.tensor_copy(kv[:], c_ps[:]).then_inc(kvc_ready, 1)
                    dve.wait_ge(o_ready, b + 1)
                    nc.vector.tensor_tensor(m.zt[:, ts(b, S)], o_ps[:], m.xt[:, ts(b, S)], ALU.add).then_inc(z_ready, 1)


def attention_out(nc, m, tag, w_o, bias_in, bias_out):
    with nc.cleanup_on_exit():
        sb, ps, sem = places(nc, tag)
        w = sb("w", [P, P])
        bias = sb("bias", [P, 2])
        ot = [sb(f"ot{u}", [P, S]) for u in range(2)]
        t_ps = [ps(f"t{u}", [P, S]) for u in range(2)]
        z_ps = [ps(f"z{u}", [P, S]) for u in range(2)]
        loaded, t_ready, ot_ready, zp_ready, z_ready = (
            sem(n) for n in ("loaded", "t_ready", "ot_ready", "zp_ready", "z_ready"))
        with nc.Block() as block:
            @block.sync
            def _(sp):
                sp.dma_start(w[:], w_o).then_inc(loaded, 16)
                sp.dma_start(bias[:, 0:1], bias_in).then_inc(loaded, 16)
                sp.dma_start(bias[:, 1:2], bias_out).then_inc(loaded, 16)

            @block.tensor
            def _(pe):
                pe.wait_ge(loaded, 3 * 16)

                def turn(b):
                    if b >= 2:
                        pe.wait_ge(ot_ready, b - 1)
                    for t in range(TB):
                        n = b * TB + t
                        last = nc.tensor.transpose(t_ps[b % 2][:, t * P:(t + 1) * P], m.zt[:, n * P:(n + 1) * P], m.ident[:])
                    last.then_inc(t_ready, 1)

                turn(0)
                for b in range(B):
                    if b + 1 < B:
                        turn(b + 1)
                    pe.wait_ge(ot_ready, b + 1)
                    if b >= 2:
                        pe.wait_ge(z_ready, b - 1)
                    nc.tensor.matmul(z_ps[b % 2][:], w[:], ot[b % 2][:], start=True, stop=True).then_inc(zp_ready, 1)

            @block.scalar
            def _(act):
                act.wait_ge(loaded, 3 * 16)
                for b in range(B):
                    act.wait_ge(t_ready, b + 1)
                    if b >= 2:
                        act.wait_ge(zp_ready, b - 1)
                    nc.scalar.activation(ot[b % 2][:], t_ps[b % 2][:], ACT.Identity, bias=bias[:, 0:1]).then_inc(ot_ready, 1)

            @block.vector
            def _(dve):
                for b in range(B):
                    dve.wait_ge(zp_ready, b + 1)
                    nc.vector.scalar_tensor_tensor(out=m.zt[:, b * S:(b + 1) * S], in0=z_ps[b % 2][:], scalar=bias[:, 1:2],
                                                   in1=m.xt[:, b * S:(b + 1) * S], op0=ALU.add, op1=ALU.add).then_inc(z_ready, 1)


def project(nc, m, tag, feat, weights, w_v, vt):
    with nc.cleanup_on_exit():
        sb, ps, sem = places(nc, tag)
        w = [sb(f"w{i}", [P, P]) for i in range(len(weights))]
        wv = sb("wv", [P, P])
        f_ps = [[ps(f"f{i}{u}", [P, S]) for u in range(2)] for i in range(len(weights))]
        v_ps = [ps(f"v{u}", [P, TB, P]) for u in range(2)]
        loaded = sem("loaded")
        f_ready = [sem(f"f_ready{i}") for i in range(len(weights))]
        f_used = [sem(f"f_used{i}") for i in range(len(weights))]
        v_ready, v_used = sem("v_ready"), sem("v_used")
        with nc.Block() as block:
            @block.sync
            def _(sp):
                for dst, src in zip(w, weights):
                    sp.dma_start(dst[:], src).then_inc(loaded, 16)
                sp.dma_start(wv[:], w_v).then_inc(loaded, 16)

            @block.tensor
            def _(pe):
                pe.wait_ge(loaded, 16 * (len(weights) + 1))
                for b in range(B):
                    for i in range(len(weights)):
                        if b >= 2:
                            pe.wait_ge(f_used[i], (b - 1) * sum(j == i for j, _, _ in feat))
                        nc.tensor.matmul(f_ps[i][b % 2][:], w[i][:], m.xt[:, b * S:(b + 1) * S],
                                         start=True, stop=True).then_inc(f_ready[i], 1)
                    if b >= 2:
                        pe.wait_ge(v_used, b - 1)
                    for t in range(TB):
                        n = b * TB + t
                        last = nc.tensor.matmul(v_ps[b % 2][:, t, :], m.xt[:, n * P:(n + 1) * P], wv[:], start=True, stop=True)
                    last.then_inc(v_ready, 1)

            @block.vector
            def _(dve):
                for b in range(B):
                    for i, bias, dst in feat:
                        dve.wait_ge(f_ready[i], b + 1)
                        nc.vector.tensor_scalar(dst[:, b * S:(b + 1) * S], f_ps[i][b % 2][:], bias, None,
                                                ALU.add).then_inc(f_used[i], 1)

            @block.scalar
            def _(act):
                for b in range(B):
                    act.wait_ge(v_ready, b + 1)
                    nc.scalar.activation(vt[:, b * TB:(b + 1) * TB, :], v_ps[b % 2][:], ACT.Copy).then_inc(v_used, 1)


def batch_softmax_attention(nc, m, tag, w_q, w_k, w_v, w_o, zero_col):
    inv_scale = 1.0 / float(P) ** 0.5
    VC = 64
    with nc.cleanup_on_exit():
        sb, ps, sem = places(nc, tag)
        qt, kt = sb("qt", [P, T]), sb("kt", [P, T])
        vt = sb("vt", [P, NT, P])
        zero = sb("zero", [P, 1])
        z_ld = sem("z_ld")
        with nc.Block() as block:
            @block.vector
            def _(dve):
                nc.vector.memset(zero[:], 0.0).then_inc(z_ld, 1)
        project(nc, m, tag + "p", [(0, zero[:, 0:1], qt), (1, zero[:, 0:1], kt)], [w_q, w_k], w_v, vt)
        qm = sb("qm", [P, 2 * T])
        diff = [sb(f"diff{u}", [P, B, P]) for u in range(2)]
        top = [sb(f"top{u}", [P, P]) for u in range(2)]
        ex, prob = ([sb(f"{n}{u}", [P, B, P]) for u in range(TB)] for n in ("ex", "prob"))
        total, lnt, rec = ([sb(f"{n}{u}", [P, P]) for u in range(TB)] for n in ("total", "lnt", "rec"))
        s_ps = [ps(f"s{u}", [P, B, P]) for u in range(2)]
        o_ps = ps("o", [P, B, VC])
        names = ("qm_ready", "s_ready", "top_ready", "diff_ready", "ex_ready", "total_ready", "ln_ready",
                 "rec_ready", "prob_ready", "pv_ready", "o_used")
        qm_ready, s_ready, top_ready, diff_ready, ex_ready, total_ready, ln_ready, rec_ready, prob_ready, \
            pv_ready, o_used = (sem(n) for n in names)
        o_view = m.zt[:].rearrange("p (b c) -> p b c", b=B)
        units = H * TB * TB
        with nc.Block() as block:
            @block.tensor
            def _(pe):
                def scores(n, k, h, q):
                    pe.wait_ge(qm_ready, h + 1)
                    if not isinstance(n, int) or n >= 2:
                        pe.wait_ge(diff_ready, n - 1)
                    for b in range(B):
                        last = nc.tensor.matmul(s_ps[k % 2][:, b, :], kt[:, (b * TB + k) * P:(b * TB + k + 1) * P],
                                                qm[:, ds((h % 2) * T + q * P + b * S, P)], start=True, stop=True)
                    last.then_inc(s_ready, 1)

                def values(n, k, h, f):
                    pe.wait_ge(prob_ready, TB + n + 1)
                    if k == 0:
                        pe.wait_ge(o_used, f + 2)
                    for b in range(B):
                        last = nc.tensor.matmul(o_ps[:, b, :], prob[k][:, b, :],
                                                vt[:, b * TB + k, ds((h // (VC // HD)) * VC, VC)], start=(k == 0 and b == 0),
                                                stop=(k == TB - 1), skip_group_check=True)
                    last.then_inc(pv_ready, 1)

                def step(f, h, h1, q, q1):
                    for k in range(TB):
                        if k < 1:
                            scores(TB * f + k + 3, k + 3, h, q)
                        elif h1 is not None:
                            scores(TB * f + k + 3, k - 1, h1, q1)
                        values(TB * f + k, k, h, f)

                pe.sem_inc(pv_ready, TB)
                for k in range(3):
                    scores(k, k, 0, 0)
                with pe.Fori(0, H * TB - 1) as f:
                    step(f, f // TB, (f + 1) // TB, f % TB, (f + 1) % TB)
                step(H * TB - 1, H - 1, None, TB - 1, None)

            @block.vector
            def _(dve):
                def head(h, par):
                    nc.vector.tensor_scalar(qm[:, ds(par * T, T)], qt[:], m.hm[:, ds(h, 1)], None, ALU.mult).then_inc(qm_ready, 1)

                def diff_of(n, k):
                    dve.wait_ge(s_ready, n + 1)
                    if not isinstance(n, int) or n >= 2:
                        dve.wait_ge(diff_ready, n - 1)
                    nc.vector.tensor_reduce(top[k % 2][:], s_ps[k % 2][:].rearrange("p b q -> p q b"), AX.X,
                                            ALU.max).then_inc(top_ready, 1)
                    dve.wait_ge(top_ready, n + 1)
                    if not isinstance(n, int) or n >= 2:
                        dve.wait_ge(ex_ready, n - 1)
                    nc.vector.tensor_tensor(diff[k % 2][:], s_ps[k % 2][:],
                                            top[k % 2][:].rearrange("p (b q) -> p b q", b=1).broadcast_to([P, B, P]),
                                            ALU.subtract).then_inc(diff_ready, 1)

                def total_of(n, k):
                    dve.wait_ge(ex_ready, n + 1)
                    if not isinstance(n, int):
                        dve.wait_ge(prob_ready, n + 1)
                    nc.vector.tensor_reduce(total[k][:], ex[k][:].rearrange("p b q -> p q b"), AX.X,
                                            ALU.add).then_inc(total_ready, 1)

                def store(f, slot):
                    dve.wait_ge(pv_ready, TB * f + TB)
                    dve.wait_ge(o_used, f + 1)
                    nc.vector.tensor_scalar(o_view[:, :, ds((slot % TB) * P + (slot // TB) * HD, HD)],
                                            o_ps[:, :, ds(((slot // TB) % (VC // HD)) * HD, HD)], 1.0, None,
                                            ALU.mult).then_inc(o_used, 1)

                def step(f, last):
                    for k in range(TB):
                        if not (last and k == TB - 1):
                            diff_of(4 * f + k + 1, (k + 1) % TB)
                        if k == 1:
                            store(f, (f + H * TB - 1) % (H * TB))
                        total_of(4 * f + k, k)

                nc.vector.memset(o_ps[:], 0.0).then_inc(o_used, 1)
                head(0, 0)
                diff_of(0, 0)
                for h in rounds(dve, H - 1):
                    dve.wait_ge(s_ready, h * TB * TB)
                    dve.wait_ge(qm_ready, h + 1)
                    head(h + 1, (h + 1) % 2)
                    for q in rounds(dve, TB):
                        step(h * TB + q, False)
                with dve.Fori(0, TB - 1) as q:
                    step((H - 1) * TB + q, False)
                step(H * TB - 1, True)
                store(H * TB, H * TB - 1)

            @block.scalar
            def _(act):
                def exps(n, k):
                    act.wait_ge(diff_ready, n + 1)
                    act.wait_ge(prob_ready, n + 1)
                    nc.scalar.activation(ex[k][:], diff[k % 2][:], ACT.Exp, scale=inv_scale).then_inc(ex_ready, 1)

                def recip(n, k):
                    act.wait_ge(total_ready, n + 1)
                    act.wait_ge(prob_ready, n + 1)
                    nc.scalar.activation(lnt[k][:], total[k][:], ACT.Ln).then_inc(ln_ready, 1)
                    act.wait_ge(ln_ready, n + 1)
                    nc.scalar.activation(rec[k][:], lnt[k][:], ACT.Exp, scale=-1.0).then_inc(rec_ready, 1)

                nc.scalar.preload_act_table_set(LN_EXP)
                exps(0, 0)
                with act.Fori(0, units // TB - 1) as f:
                    for k in range(TB):
                        exps(4 * f + k + 1, (k + 1) % TB)
                        recip(4 * f + k, k)
                for k in range(TB):
                    n = units - TB + k
                    if k < TB - 1:
                        exps(n + 1, k + 1)
                    recip(n, k)

            @block.gpsimd
            def _(pool):
                pool.sem_inc(prob_ready, TB)
                with pool.Fori(0, units // TB) as f:
                    for u in range(TB):
                        pool.wait_ge(rec_ready, TB * f + u + 1)
                        pool.wait_ge(pv_ready, TB * f + u + 1)
                        nc.gpsimd.tensor_tensor(prob[u][:], ex[u][:],
                                                rec[u][:].rearrange("p (b q) -> p b q", b=1).broadcast_to([P, B, P]),
                                                ALU.mult).then_inc(prob_ready, 1)
    attention_out(nc, m, tag + "o", w_o, zero_col, zero_col)


def relative_attention(nc, m, tag, a, scratch):
    inv_scale = 1.0 / float(HD) ** 0.5
    heads = B * H
    with nc.cleanup_on_exit():
        sb, ps, sem = places(nc, tag)
        qu, qv, kt = (sb(n, [P, T]) for n in ("qu", "qv", "kt"))
        vt = sb("vt", [P, NT, P])
        wp, feat = sb("wp", [P, P]), sb("feat", [P, S])
        cols = sb("cols", [P, 5])
        bqu, bqv = sb("bqu", [P, 1]), sb("bqv", [P, 1])
        pos = sb("pos", [P, S])
        loaded, bias_ready, pos_made, pos_ready = (sem(n) for n in ("loaded", "bias_ready", "pos_made", "pos_ready"))
        rows = [scratch[u].rearrange("(t p c) -> p t c", p=P, c=S + 1) for u in range(2)]
        back = [scratch[u][S:S * (S + 1)].rearrange("(t p c) -> p t c", p=P, c=S) for u in range(2)]
        with nc.cleanup_on_exit():
            pos_ps = ps("pos_ps", [P, S])
            with nc.Block() as block:
                @block.sync
                def _(sp):
                    for dst, src in ((wp[:], a["Wp"]), (feat[:], a["feat"]), *((cols[:, i:i + 1], a[n]) for i, n in
                                     enumerate(("bq", "bk", "bp", "u", "v")))):
                        sp.dma_start(dst, src).then_inc(loaded, 16)

                @block.tensor
                def _(pe):
                    pe.wait_ge(loaded, 7 * 16)
                    nc.tensor.matmul(pos_ps[:], wp[:], feat[:], start=True, stop=True).then_inc(pos_made, 1)

                @block.vector
                def _(dve):
                    dve.wait_ge(loaded, 7 * 16)
                    nc.vector.tensor_tensor(bqu[:], cols[:, 0:1], cols[:, 3:4], ALU.add).then_inc(bias_ready, 1)
                    nc.vector.tensor_tensor(bqv[:], cols[:, 0:1], cols[:, 4:5], ALU.add).then_inc(bias_ready, 1)
                    dve.wait_ge(pos_made, 1)
                    nc.vector.tensor_scalar(pos[:], pos_ps[:], cols[:, 2:3], None, ALU.add).then_inc(pos_ready, 1)
        with nc.cleanup_on_exit():
            project(nc, m, tag + "p", [(0, bqu[:], qu), (0, bqv[:], qv), (1, cols[:, 1:2], kt)], [a["Wq"], a["Wk"]], a["Wv"], vt)

        quh, qvh = ([sb(f"{n}{u}", [P, S]) for u in range(2)] for n in ("quh", "qvh"))
        pc = [sb(f"pc{u}", [P, TB, S + 1]) for u in range(2)]
        rel = [sb(f"rel{u}", [P, TB, S]) for u in range(2)]
        s, ex, et = ([sb(f"{n}{u}", [P, S]) for u in range(2)] for n in ("s", "ex", "et"))
        top, ntop, total = (sb(n, [P, 2, TB]) for n in ("top", "ntop", "total"))
        rec = sb("rec", [P, 2, TB])
        p_ps, c_ps, t_ps = ([ps(f"{n}ps{u}", [P, S]) for u in range(2)] for n in ("p", "c", "t"))
        o_ps = [ps(f"o{u}", [P, TB, HD]) for u in range(2)]
        names = ("quh_ready", "qvh_ready", "p_ready", "pc_ready", "out_done", "rel_ready0", "rel_ready1", "c_ready", "s_ready",
                 "ntop_ready", "ex_ready", "t_ready", "et_ready", "pv_ready", "rec_ready", "o_ready", "edge_ready")
        quh_ready, qvh_ready, p_ready, pc_ready, out_done, rel_ready0, rel_ready1, c_ready, s_ready, ntop_ready, \
            ex_ready, t_ready, et_ready, pv_ready, rec_ready, o_ready, edge_ready = (sem(n) for n in names)
        rel_ready = (rel_ready0, rel_ready1)
        o_view = m.zt[:].rearrange("p (n f) -> p n f", f=P)
        static = lambda n: isinstance(n, int)
        with nc.Block() as block:
            @block.gpsimd
            def _(pool):
                for u in range(2):
                    nc.gpsimd.memset(pc[u][:, :, 0:1], 0.0).then_inc(edge_ready, 1)

            @block.sync
            def _(sp):
                def shift(g, u):
                    if static(g):
                        copied, read, out, added = TB * g + TB, 8 * (g - u), 16 * g + 16, TB * g - TB
                    else:
                        copied, read, out, added = (sp.snap(sp.to_reg(v)) for v in (TB * g + TB, 8 * (g - u), 16 * g + 16, TB * g - TB))
                    sp.wait_ge(edge_ready, 2)
                    sp.wait_ge(pc_ready, copied)
                    if not static(g) or g >= 2:
                        sp.wait_ge(rel_ready[u], read)
                    sp.dma_start(rows[u], pc[u][:]).then_inc(out_done, 16)
                    sp.wait_ge(out_done, out)
                    if not static(g) or g >= 2:
                        sp.wait_ge(s_ready, added)
                    sp.dma_start(rel[u][:], back[u]).then_inc(rel_ready[u], 16)

                shift(0, 0)
                shift(1, 1)
                with sp.Fori(1, heads // 2) as pair:
                    for u in range(2):
                        shift(2 * pair + u, u)
                for u in range(2):
                    sp.wait_ge(rel_ready[u], 8 * heads)

            @block.tensor
            def _(pe):
                def position(g, u, t):
                    pe.wait_ge(qvh_ready, g + 1)
                    if not (static(g) and TB * g + t < 2):
                        pe.wait_ge(pc_ready, TB * g + t - 1)
                    nc.tensor.matmul(p_ps[t % 2][:], qvh[u][:, t * P:(t + 1) * P], pos[:], start=True, stop=True).then_inc(p_ready, 1)

                def content(g, u, t, b):
                    pe.wait_ge(quh_ready, g + 1)
                    if not (static(g) and TB * g + t < 2):
                        pe.wait_ge(s_ready, TB * g + t - 1)
                    nc.tensor.matmul(c_ps[t % 2][:], quh[u][:, t * P:(t + 1) * P], kt[:, ds(b * S, S)],
                                     start=True, stop=True).then_inc(c_ready, 1)

                def turn(g, t):
                    pe.wait_ge(ex_ready, TB * g + t + 1)
                    if not (static(g) and TB * g + t < 2):
                        pe.wait_ge(et_ready, TB * g + t - 1)
                    for k in range(TB):
                        last = nc.tensor.transpose(t_ps[t % 2][:, k * P:(k + 1) * P], ex[t % 2][:, k * P:(k + 1) * P], m.ident[:])
                    last.then_inc(t_ready, 1)

                def values(g, u, t, b, h):
                    pe.wait_ge(et_ready, TB * g + t + 1)
                    if t == 0 and not (static(g) and g < 2):
                        pe.wait_ge(o_ready, g - 1)
                    for k in range(TB):
                        last = nc.tensor.matmul(o_ps[u][:, t, :], et[t % 2][:, k * P:(k + 1) * P],
                                                vt[:, ds(b * TB + k, 1), ds(h * HD, HD)], start=(k == 0), stop=(k == TB - 1))
                    last.then_inc(pv_ready, 1)

                def head(g, u, at, at1, ahead):
                    for t in range(TB):
                        if ahead:
                            position(g + 2, u, t)
                        if t < 2:
                            content(g, u, t + 2, at[0])
                        elif at1:
                            content(g + 1, 1 - u, t - 2, at1[0])
                        if t < 3:
                            turn(g, t + 1)
                        elif at1:
                            turn(g + 1, 0)
                        values(g, u, t, *at)

                for g in range(2):
                    for t in range(TB):
                        position(g, g, t)
                content(0, 0, 0, 0)
                content(0, 0, 1, 0)
                turn(0, 0)
                for g in range(2):
                    head(g, g, (0, g), (0, g + 1), True)
                with pe.Fori(1, heads // 2 - 1) as pair:
                    for u in range(2):
                        g = 2 * pair + u
                        head(g, u, (g // H, g % H), ((g + 1) // H, (g + 1) % H), True)
                head(heads - 2, 0, (B - 1, H - 2), (B - 1, H - 1), False)
                head(heads - 1, 1, (B - 1, H - 1), None, False)

            @block.scalar
            def _(act):
                def copy(g, u, t):
                    act.wait_ge(p_ready, TB * g + t + 1)
                    if t == 0 and not (static(g) and g < 2):
                        act.wait_ge(out_done, 16 * (g - 1))
                    nc.scalar.activation(pc[u][:, t, 1:], p_ps[t % 2][:], ACT.Copy).then_inc(pc_ready, 1)

                def exps(g, u, t):
                    act.wait_ge(ntop_ready, TB * g + t + 1)
                    if not (static(g) and TB * g + t < 2):
                        act.wait_ge(t_ready, TB * g + t - 1)
                    if t == 0 and not (static(g) and g < 2):
                        act.wait_ge(rec_ready, g - 1)
                    nc.scalar.activation(ex[t % 2][:], s[t % 2][:], ACT.Exp, scale=inv_scale, bias=ntop[:, u, t:t + 1],
                                         accum_out=total[:, u, t:t + 1]).then_inc(ex_ready, 1)

                def head(g, u, ahead, last):
                    for t in range(TB):
                        if t < 3:
                            exps(g, u, t + 1)
                        elif not last:
                            exps(g + 1, 1 - u, 0)
                        if ahead:
                            copy(g + 2, u, t)

                nc.scalar.preload_act_table(ACT.Exp)
                for g in range(2):
                    for t in range(TB):
                        copy(g, g, t)
                exps(0, 0, 0)
                for g in range(2):
                    head(g, g, True, False)
                with act.Fori(1, heads // 2 - 1) as pair:
                    for u in range(2):
                        head(2 * pair + u, u, True, False)
                head(heads - 2, 0, False, False)
                head(heads - 1, 1, False, True)

            @block.vector
            def _(dve):
                def mask(dst, src, b, h, ready):
                    nc.vector.tensor_scalar(dst, src[:, ds(b * S, S)], m.hm[:, ds(h, 1)], None, ALU.mult).then_inc(ready, 1)

                def score(g, u, t):
                    dve.wait_ge(c_ready, TB * g + t + 1)
                    dve.wait_ge(rel_ready[u], 8 * (g - u) + 16)
                    if not (static(g) and TB * g + t < 2):
                        dve.wait_ge(ex_ready, TB * g + t - 1)
                    dve.nop(nofuse=True)
                    nc.vector.tensor_tensor_reduce(s[t % 2][:], c_ps[t % 2][:], rel[u][:, t, :], 1.0, -3.0e38, ALU.add, ALU.max,
                                                   top[:, u, t:t + 1]).then_inc(s_ready, 1)
                    dve.wait_ge(s_ready, TB * g + t + 1)
                    nc.vector.tensor_scalar(ntop[:, u, t:t + 1], top[:, u, t:t + 1], -inv_scale, None, ALU.mult).then_inc(ntop_ready, 1)

                def copy(g, t):
                    dve.wait_ge(t_ready, TB * g + t + 1)
                    if not (static(g) and TB * g + t < 2):
                        dve.wait_ge(pv_ready, TB * g + t - 1)
                    nc.vector.tensor_copy(et[t % 2][:], t_ps[t % 2][:]).then_inc(et_ready, 1)

                def store(g, u, b, h):
                    dve.wait_ge(pv_ready, TB * g + TB)
                    dve.wait_ge(rec_ready, g + 1)
                    nc.vector.tensor_tensor(o_view[:, ds(b * TB, TB), ds(h * HD, HD)], o_ps[u][:],
                                            rec[:, u, :].rearrange("p (t c) -> p t c", c=1).broadcast_to([P, TB, HD]),
                                            ALU.mult).then_inc(o_ready, 1)

                def normed(g, u, at):
                    dve.wait_ge(ex_ready, TB * g + TB)
                    if not (static(g) and g < 1):
                        dve.wait_ge(o_ready, g)
                    nc.vector.reciprocal(rec[:, u, :], total[:, u, :]).then_inc(rec_ready, 1)
                    store(g, u, *at)

                def head(g, u, before, at1, at3, last):
                    for t in range(TB):
                        if t < 3:
                            score(g, u, t + 1)
                        elif not last:
                            score(g + 1, 1 - u, 0)
                        copy(g, t)
                        if t == 0:
                            if before:
                                normed(g - 1, 1 - u, before)
                            if at1:
                                if not (static(g) and g == 0):
                                    dve.wait_ge(c_ready, TB * g)
                                mask(quh[1 - u][:], qu, *at1, quh_ready)
                        if t == 1 and at3:
                            dve.wait_ge(p_ready, TB * (g + 2))
                            mask(qvh[1 - u][:], qv, *at3, qvh_ready)

                mask(qvh[0][:], qv, 0, 0, qvh_ready)
                mask(qvh[1][:], qv, 0, 1, qvh_ready)
                mask(quh[0][:], qu, 0, 0, quh_ready)
                dve.wait_ge(p_ready, TB)
                mask(qvh[0][:], qv, 0, 2, qvh_ready)
                score(0, 0, 0)
                for g in range(2):
                    head(g, g, (0, g - 1) if g else None, (0, g + 1), (0, g + 3), False)
                with dve.Fori(1, heads // 2 - 1) as pair:
                    for u in range(2):
                        g = 2 * pair + u
                        head(g, u, ((g - 1) // H, (g - 1) % H), ((g + 1) // H, (g + 1) % H), (((g + 3) // H) % B, (g + 3) % H), False)
                head(heads - 2, 0, (B - 1, H - 3), (B - 1, H - 1), None, False)
                head(heads - 1, 1, (B - 1, H - 2), None, None, True)
                normed(heads - 1, 1, (B - 1, H - 1))


E = 8
FF = 512
CAP = T // E


def experts(nc, m, tag, a):
    C = FF // P
    with nc.cleanup_on_exit():
        sb, ps, sem = places(nc, tag)
        y = sb("y", [P, NT, P])
        gates = sb("gates", [P, NT, E])
        with nc.cleanup_on_exit():
            wg, b2 = sb("wg", [P, E]), sb("b2", [E, P])
            before, ones = sb("before", [P, P]), sb("ones", [P, P])
            first = sb("first", [P, E])
            lg, d, ex, hit, rank, pick, tot, run, place, kept = (sb(n, [P, NT, E]) for n in (
                "lg", "d", "ex", "hit", "rank", "pick", "tot", "run", "place", "kept"))
            top, total, gate, best = (sb(n, [P, NT]) for n in ("top", "total", "gate", "best"))
            unit = sb("unit", [P, NT])
            gt = sb("gt", [E, T])
            l_ps, n_ps, s_ps = ps("l", [P, NT, E]), ps("n", [P, NT, E]), ps("s", [P, NT, E])
            g_ps = [ps(f"g{u}", [E, S]) for u in range(2)]
            y_ps = [ps(f"y{u}", [P, TB, P]) for u in range(2)]
            loaded, l_ready, step, ex_ready, pick_ready, n_ready, s_ready, gates_ready, g_ready, gt_ready, yp_ready, y_ready = (
                sem(n) for n in ("loaded", "l_ready", "step", "ex_ready", "pick_ready", "n_ready", "s_ready",
                                 "gates_ready", "g_ready", "gt_ready", "yp_ready", "y_ready"))
            ones_ready = sem("ones_ready")
            wide = lambda ap: ap.rearrange("p (t e) -> p t e", e=1).broadcast_to([P, NT, E])
            with nc.Block() as block:
                @block.sync
                def _(sp):
                    for dst, src in ((wg, a["wg"]), (b2, a["b2"]), (before, a["before"]), (first, a["first"])):
                        sp.dma_start(dst[:], src).then_inc(loaded, 16)

                @block.tensor
                def _(pe):
                    pe.wait_ge(loaded, 4 * 16)
                    for n in range(NT):
                        last = nc.tensor.matmul(l_ps[:, n, :], m.xt[:, n * P:(n + 1) * P], wg[:], start=True, stop=True)
                    last.then_inc(l_ready, 1)
                    pe.wait_ge(ones_ready, 1)
                    pe.wait_ge(pick_ready, 1)
                    nc.tensor.matmul(n_ps[:], before[:], pick[:], start=True, stop=True).then_inc(n_ready, 1)
                    nc.tensor.matmul(s_ps[:], ones[:], pick[:], start=True, stop=True).then_inc(s_ready, 1)
                    pe.wait_ge(gates_ready, 1)
                    for b in range(B):
                        if b >= 2:
                            pe.wait_ge(gt_ready, b - 1)
                            pe.wait_ge(y_ready, b - 1)
                        for t in range(TB):
                            last = nc.tensor.transpose(g_ps[b % 2][:, t * P:(t + 1) * P], gates[:, b * TB + t, :], m.ident[:])
                        last.then_inc(g_ready, 1)
                        pe.wait_ge(gt_ready, b + 1)
                        for t in range(TB):
                            n = b * TB + t
                            last = nc.tensor.matmul(y_ps[b % 2][:, t, :], gt[:, n * P:(n + 1) * P], b2[:], start=True, stop=True)
                        last.then_inc(yp_ready, 1)

                @block.scalar
                def _(act):
                    act.wait_ge(step, 2)
                    nc.scalar.activation(ex[:], d[:], ACT.Exp).then_inc(ex_ready, 1)
                    for b in range(B):
                        act.wait_ge(yp_ready, b + 1)
                        nc.scalar.activation(y[:, b * TB:(b + 1) * TB, :], y_ps[b % 2][:], ACT.Copy).then_inc(y_ready, 1)

                @block.vector
                def _(dve):
                    done = [0]

                    def then(ins):
                        done[0] += 1
                        ins.then_inc(step, 1)
                        dve.wait_ge(step, done[0])

                    nc.vector.memset(unit[:], 1.0)
                    dve.wait_ge(l_ready, 1)
                    then(nc.vector.tensor_reduce(top[:], l_ps[:], AX.X, ALU.max))
                    then(nc.vector.tensor_tensor(d[:], l_ps[:], wide(top[:]), ALU.subtract))
                    then(nc.vector.tensor_scalar(hit[:], d[:], 0.0, None, ALU.is_ge))
                    dve.wait_ge(loaded, 4 * 16)
                    then(nc.vector.tensor_tensor(rank[:], hit[:], first[:].rearrange("p (t e) -> p t e", t=1).broadcast_to([P, NT, E]),
                                                 ALU.mult))
                    then(nc.vector.tensor_reduce(best[:], rank[:], AX.X, ALU.max))
                    nc.vector.tensor_tensor(pick[:], rank[:], wide(best[:]), ALU.is_equal).then_inc(pick_ready, 1)
                    dve.wait_ge(ex_ready, 1)
                    then(nc.vector.tensor_reduce(total[:], ex[:], AX.X, ALU.add))
                    then(nc.vector.reciprocal(gate[:], total[:]))
                    dve.wait_ge(s_ready, 1)
                    then(nc.vector.tensor_copy(tot[:], s_ps[:]))
                    for e in range(E):
                        last = nc.vector.tensor_tensor_scan(run[:, :, e], unit[:], tot[:, :, e], 0.0, ALU.mult, ALU.add)
                    then(last)
                    dve.wait_ge(n_ready, 1)
                    then(nc.vector.tensor_tensor(place[:], n_ps[:], run[:], ALU.add))
                    then(nc.vector.tensor_tensor(lg[:], place[:], tot[:], ALU.subtract))
                    then(nc.vector.tensor_scalar(kept[:], lg[:], float(CAP), None, ALU.is_le))
                    then(nc.vector.tensor_tensor(hit[:], kept[:], pick[:], ALU.mult))
                    nc.vector.tensor_tensor(gates[:], hit[:], wide(gate[:]), ALU.mult).then_inc(gates_ready, 1)
                    for b in range(B):
                        dve.wait_ge(g_ready, b + 1)
                        nc.vector.tensor_copy(gt[:, b * S:(b + 1) * S], g_ps[b % 2][:]).then_inc(gt_ready, 1)

                @block.gpsimd
                def _(pool):
                    nc.gpsimd.memset(ones[:], 1.0).then_inc(ones_ready, 1)

        with nc.cleanup_on_exit():
            w1 = [sb(f"w1{u}", [P, FF]) for u in range(2)]
            w2 = [sb(f"w2{u}", [P, C, P]) for u in range(2)]
            b1 = [sb(f"b1{u}", [P, C]) for u in range(2)]
            h = [sb(f"h{c}", [P, S]) for c in range(C)]
            h_ps = [ps(f"h_ps{c}", [P, S]) for c in range(C)]
            e_ps = [ps(f"e{u}", [P, TB, P]) for u in range(2)]
            ld0, ld1, hp_ready, h_act, h_dve, e_ready, y_ready = (
                sem(n) for n in ("ld0", "ld1", "hp_ready", "h_act", "h_dve", "e_ready", "y2_ready"))
            loaded = (ld0, ld1)
            with nc.Block() as block:
                @block.sync
                def _(sp):
                    for i in rounds(sp, E // 2):
                        for u in range(2):
                            e = 2 * i + u
                            if not isinstance(i, int):
                                used = sp.snap(sp.to_reg(B * (e - 1)))
                                sp.wait_ge(e_ready, used)
                            sp.dma_start(w1[u][:], a["w1"][ds(e, 1)].rearrange("e m h -> (e m) h")).then_inc(loaded[u], 16)
                            sp.dma_start(w2[u][:], a["w2"][ds(e, 1)].rearrange("e (c p) m -> p (e c) m", p=P)).then_inc(loaded[u], 16)
                            sp.dma_start(b1[u][:], a["b1"][:, ds(e * C, C)]).then_inc(loaded[u], 16)

                @block.tensor
                def _(pe):
                    for i in rounds(pe, E // 2):
                        for u in range(2):
                            for pair in rounds(pe, B // 2):
                                for v in range(2):
                                    n = (2 * i + u) * B + 2 * pair + v
                                    pe.wait_ge(loaded[u], 48 * i + 48)
                                    pe.wait_ge(h_act, 2 * n)
                                    pe.wait_ge(h_dve, 2 * n)
                                    for c in range(C):
                                        nc.tensor.matmul(h_ps[c][:], w1[u][:, c * P:(c + 1) * P], m.xt[:, ds((2 * pair + v) * S, S)],
                                                         start=True, stop=True).then_inc(hp_ready, 1)
                                    pe.wait_ge(y_ready, TB * 2 * ((2 * i + u) * (B // 2) + pair))
                                    for t in range(TB):
                                        for c in range(C):
                                            if t == 0:
                                                pe.wait_ge(h_act if c % 2 == 0 else h_dve, 2 * n + c // 2 + 1)
                                            last = nc.tensor.matmul(e_ps[v][:, t, :], h[c][:, t * P:(t + 1) * P], w2[u][:, c, :],
                                                                    start=(c == 0), stop=(c == C - 1))
                                    last.then_inc(e_ready, 1)

                @block.scalar
                def _(act):
                    for i in rounds(act, E // 2):
                        for u in range(2):
                            for b in rounds(act, B):
                                n = (2 * i + u) * B + b
                                for c in (0, 2):
                                    act.wait_ge(hp_ready, C * n + c + 1)
                                    act.wait_ge(e_ready, n)
                                    nc.scalar.activation(h[c][:], h_ps[c][:], ACT.Relu, bias=b1[u][:, c:c + 1]).then_inc(h_act, 1)

                @block.vector
                def _(dve):
                    for i in rounds(dve, E // 2):
                        for u in range(2):
                            for pair in rounds(dve, B // 2):
                                for v in range(2):
                                    e, b = 2 * i + u, 2 * pair + v
                                    n = e * B + b
                                    for c in (1, 3):
                                        dve.wait_ge(hp_ready, C * n + c + 1)
                                        dve.wait_ge(e_ready, n)
                                        nc.vector.tensor_scalar(h[c][:], h_ps[c][:], b1[u][:, c:c + 1], 0.0,
                                                                ALU.add, ALU.max).then_inc(h_dve, 1)
                                    dve.wait_ge(e_ready, n + 1)
                                    dve.wait_ge(y_ready, TB * n)
                                    for t in range(TB):
                                        row = y[:, ds(b * TB + t, 1), :].rearrange("p a f -> p (a f)")
                                        nc.vector.scalar_tensor_tensor(
                                            out=row, in0=e_ps[v][:, t, :],
                                            scalar=gates[:, ds(b * TB + t, 1), ds(e, 1)].rearrange("p a f -> p (a f)"),
                                            in1=row, op0=ALU.mult, op1=ALU.add).then_inc(y_ready, 1)
        rows_out(nc, m, tag + "o", y)


def rows_out(nc, m, tag, y):
    with nc.cleanup_on_exit():
        sb, ps, sem = places(nc, tag)
        t_ps = [ps(f"t{u}", [P, S]) for u in range(2)]
        t_ready, z_ready = sem("t_ready"), sem("z_ready")
        with nc.Block() as block:
            @block.tensor
            def _(pe):
                for b in range(B):
                    if b >= 2:
                        pe.wait_ge(z_ready, b - 1)
                    for t in range(TB):
                        last = nc.tensor.transpose(t_ps[b % 2][:, t * P:(t + 1) * P], y[:, b * TB + t, :], m.ident[:])
                    last.then_inc(t_ready, 1)

            @block.vector
            def _(dve):
                for b in range(B):
                    dve.wait_ge(t_ready, b + 1)
                    nc.vector.tensor_tensor(m.zt[:, b * S:(b + 1) * S], t_ps[b % 2][:], m.xt[:, b * S:(b + 1) * S],
                                            ALU.add).then_inc(z_ready, 1)


DECAY = 0.9
SPIKE, WINNERS = 0.5, 4


def rms_norm(nc, m, tag, w_col):
    with nc.cleanup_on_exit():
        sb, ps, sem = places(nc, tag)
        w = sb("w", [P, 1])
        sq, ln, rstd = ([sb(f"{n}{u}", [P, S]) for u in range(2)] for n in ("sq", "ln", "rstd"))
        var_ps = [ps(f"var{u}", [P, S]) for u in range(2)]
        loaded, sq_ready, var_ready, ln_ready, rstd_ready, z_ready = (
            sem(n) for n in ("loaded", "sq_ready", "var_ready", "ln_ready", "rstd_ready", "z_ready"))
        with nc.Block() as block:
            @block.sync
            def _(sp):
                sp.dma_start(w[:], w_col).then_inc(loaded, 16)

            @block.tensor
            def _(pe):
                for b in range(B):
                    pe.wait_ge(sq_ready, b + 1)
                    if b >= 2:
                        pe.wait_ge(ln_ready, b - 1)
                    nc.tensor.matmul(var_ps[b % 2][:], m.mean_w[:], sq[b % 2][:], start=True, stop=True).then_inc(var_ready, 1)

            @block.scalar
            def _(act):
                nc.scalar.preload_act_table_set(LN_EXP)
                for b in range(B + 1):
                    if b < B:
                        if b >= 2:
                            act.wait_ge(var_ready, b - 1)
                        nc.scalar.activation(sq[b % 2][:], m.xt[:, b * S:(b + 1) * S], ACT.Square).then_inc(sq_ready, 1)
                    if b >= 1:
                        act.wait_ge(var_ready, b)
                        if b >= 3:
                            act.wait_ge(rstd_ready, b - 2)
                        nc.scalar.activation(ln[(b - 1) % 2][:], var_ps[(b - 1) % 2][:], ACT.Ln, bias=m.eps[:]).then_inc(ln_ready, 1)
                        act.wait_ge(ln_ready, b)
                        if b >= 3:
                            act.wait_ge(z_ready, b - 2)
                        nc.scalar.activation(rstd[(b - 1) % 2][:], ln[(b - 1) % 2][:], ACT.Exp, scale=-0.5).then_inc(rstd_ready, 1)

            @block.vector
            def _(dve):
                dve.wait_ge(loaded, 16)
                for b in range(B):
                    dve.wait_ge(rstd_ready, b + 1)
                    nc.vector.scalar_tensor_tensor(out=m.zt[:, b * S:(b + 1) * S], in0=m.xt[:, b * S:(b + 1) * S], scalar=w[:],
                                                   in1=rstd[b % 2][:], op0=ALU.mult, op1=ALU.mult).then_inc(z_ready, 1)


def spiking_mix(nc, m, tag, a):
    with nc.cleanup_on_exit():
        sb, ps, sem = places(nc, tag)
        wr, wk, wv = (sb(n, [P, P]) for n in ("wr", "wk", "wv"))
        w_in = sb("w_in", [P, P])
        w_out = sb("w_out", [P, 1])
        dmask = sb("dmask", [P, P])
        hblock = sb("hblock", [P, P])
        hb = sb("hb", [P, S])
        rt = sb("rt", [P, TB, P])
        rin = sb("rin", [P, TB, P])
        kraw, k0, cnt, kw, kout, v = (sb(n, [P, TB, P]) for n in ("kraw", "k0", "cnt", "kw", "kout", "v"))
        more = [sb(f"more{u}", [P, H, HD, HD]) for u in range(2)]
        kt = sb("kt", [P, TB, P])
        rm = [sb(f"rm{u}", [P, H, P]) for u in range(2)]
        am = [sb(f"am{u}", [P, H, P]) for u in range(2)]
        state, su = sb("state", [P, P]), sb("su", [P, P])
        r_ps, t_ps, y_ps, u_ps = ps("r", [P, S]), ps("t", [P, TB, P]), ps("y", [P, P]), ps("u", [P, P])
        k_ps, v_ps = ps("k", [P, TB, P]), ps("v", [P, TB, P])
        a_ps = [ps(f"a{u}", [P, 4, P]) for u in range(2)]
        names = ("loaded", "hb_ready", "r_ready", "k_ready", "v_ready", "rt_ready", "kraw_ready", "vs_ready", "k0_ready", "more_ready",
                 "cnt_ready", "kw_ready", "kout_ready", "rin_ready", "kt_made", "kt_ready", "rm_ready", "a_ready", "am_ready",
                 "u_ready", "su_ready", "state_ready", "y_ready", "ys_ready")
        loaded, hb_ready, r_ready, k_ready, v_ready, rt_ready, kraw_ready, vs_ready, k0_ready, more_ready, cnt_ready, kw_ready, \
            kout_ready, rin_ready, kt_made, kt_ready, rm_ready, a_ready, am_ready, u_ready, su_ready, state_ready, y_ready, \
            ys_ready = (sem(n) for n in names)
        z_view = m.zt[:].rearrange("p (n f) -> p n f", f=P)
        NL = 7
        with nc.Block() as block:
            @block.sync
            def _(sp):
                for dst, src in ((wr, a["Wr"]), (wk, a["Wk"]), (wv, a["Wv"]), (w_in, a["w_in"]), (w_out, a["w_out"]),
                                 (dmask, a["dmask"]), (hblock, a["hblock"])):
                    sp.dma_start(dst[:], src).then_inc(loaded, 16)

            @block.tensor
            def _(pe):
                pe.wait_ge(loaded, NL * 16)
                for b in rounds(pe, B):
                    pe.wait_ge(hb_ready, b + 1)
                    pe.wait_ge(rt_ready, b)
                    nc.tensor.matmul(r_ps[:], wr[:], hb[:], start=True, stop=True).then_inc(r_ready, 1)
                    pe.wait_ge(kraw_ready, b)
                    for t in range(TB):
                        last = nc.tensor.matmul(k_ps[:, t, :], hb[:, t * P:(t + 1) * P], wk[:], start=True, stop=True)
                    last.then_inc(k_ready, 1)
                    pe.wait_ge(vs_ready, b)
                    for t in range(TB):
                        last = nc.tensor.matmul(v_ps[:, t, :], hb[:, t * P:(t + 1) * P], wv[:], start=True, stop=True)
                    last.then_inc(v_ready, 1)
                    pe.wait_ge(kw_ready, b + 1)
                    pe.wait_ge(kt_ready, b)
                    for t in range(TB):
                        last = nc.tensor.transpose(t_ps[:, t, :], kw[:, t, :], m.ident[:])
                    last.then_inc(kt_made, 1)
                    pe.wait_ge(kt_ready, b + 1)
                    pe.wait_ge(vs_ready, b + 1)
                    pe.wait_ge(kout_ready, b + 1)
                    pe.wait_ge(rin_ready, b + 1)
                    for c in range(TB):
                        n = TB * b + c
                        pe.wait_ge(rm_ready, n + 1)
                        for g in range(4):
                            if g < 2:
                                pe.wait_ge(am_ready, 4 * n)
                            else:
                                pe.wait_ge(am_ready, 4 * n + g - 1)
                            nc.tensor.matmul(a_ps[g % 2][:], kt[:, c, :], rm[c % 2][:, 4 * g:4 * g + 4, :],
                                             start=True, stop=True).then_inc(a_ready, 1)
                        if c + 1 < TB:
                            pe.wait_ge(su_ready, (TB - 1) * b + c)
                            nc.tensor.matmul(u_ps[:], kout[:, c, :], v[:, c, :], start=True, stop=True).then_inc(u_ready, 1)
                        pe.wait_ge(ys_ready, n)
                        if c > 0:
                            pe.wait_ge(state_ready, (TB - 1) * b + c)
                            nc.tensor.matmul(y_ps[:], rin[:, c, :], state[:], start=True, stop=False, skip_group_check=True)
                        for h in range(H):
                            if h % 4 == 0:
                                pe.wait_ge(am_ready, 4 * n + h // 4 + 1)
                            last = nc.tensor.matmul(y_ps[:, h * HD:(h + 1) * HD], am[c % 2][:, h, :], v[:, c, h * HD:(h + 1) * HD],
                                                    start=(c == 0 and h == 0), stop=(h == H - 1), skip_group_check=True)
                        last.then_inc(y_ready, 1)

            @block.scalar
            def _(act):
                nc.scalar.preload_act_table(ACT.Sigmoid)
                for b in rounds(act, B):
                    act.wait_ge(k_ready, b + 1)
                    act.wait_ge(kout_ready, b)
                    nc.scalar.activation(kraw[:], k_ps[:], ACT.Copy).then_inc(kraw_ready, 1)
                    act.wait_ge(r_ready, b + 1)
                    act.wait_ge(rm_ready, TB * b)
                    act.wait_ge(rin_ready, b)
                    nc.scalar.activation(rt[:].rearrange("p t q -> p (t q)"), r_ps[:], ACT.Sigmoid).then_inc(rt_ready, 1)
                    act.wait_ge(v_ready, b + 1)
                    act.wait_ge(y_ready, TB * b)
                    nc.scalar.activation(v[:], v_ps[:], ACT.Copy).then_inc(vs_ready, 1)
                    act.wait_ge(kt_made, b + 1)
                    act.wait_ge(a_ready, 4 * TB * b)
                    nc.scalar.activation(kt[:], t_ps[:], ACT.Copy).then_inc(kt_ready, 1)
                    for c in range(TB):
                        n = TB * b + c
                        act.wait_ge(y_ready, n + 1)
                        act.nop(nofuse=True)
                        nc.scalar.activation(z_view[:, ds(n, 1), :].rearrange("p a f -> p (a f)"), y_ps[:],
                                             ACT.Copy).then_inc(ys_ready, 1)

            @block.gpsimd
            def _(pool):
                for b in rounds(pool, B):
                    pool.wait_ge(rt_ready, b + 1)
                    for c in range(TB):
                        if c < 2:
                            pool.wait_ge(a_ready, 4 * TB * b)
                        else:
                            pool.wait_ge(a_ready, 4 * (TB * b + c - 1))
                        nc.gpsimd.tensor_tensor(rm[c % 2][:], rt[:, c, :].rearrange("p (h l) -> p h l", h=1).broadcast_to([P, H, P]),
                                                m.hm[:].rearrange("p (h l) -> p h l", l=1).broadcast_to([P, H, P]),
                                                ALU.mult).then_inc(rm_ready, 1)

            @block.vector
            def _(dve):
                dve.wait_ge(loaded, NL * 16)
                for b in rounds(dve, B):
                    dve.wait_ge(v_ready, b)
                    dve.nop(nofuse=True)
                    nc.vector.tensor_copy(hb[:], m.zt[:, ts(b, S)]).then_inc(hb_ready, 1)
                    dve.wait_ge(kraw_ready, b + 1)
                    nc.vector.scalar_tensor_tensor(out=k0[:], in0=kraw[:], scalar=SPIKE, in1=kraw[:], op0=ALU.is_gt,
                                                   op1=ALU.mult).then_inc(k0_ready, 1)
                    dve.wait_ge(k0_ready, b + 1)
                    for t in range(TB):
                        k4 = k0[:, t, :].rearrange("p (h a c) -> p h a c", h=H, a=1)
                        k4t = k0[:, t, :].rearrange("p (h c a) -> p h c a", h=H, a=1)
                        if t >= 2:
                            dve.wait_ge(cnt_ready, TB * b + t - 1)
                        nc.vector.tensor_tensor(more[t % 2][:], k4.broadcast_to([P, H, HD, HD]), k4t.broadcast_to([P, H, HD, HD]),
                                                ALU.is_gt).then_inc(more_ready, 1)
                        dve.wait_ge(more_ready, TB * b + t + 1)
                        nc.vector.tensor_reduce(cnt[:, t, :], more[t % 2][:].rearrange("p h i j -> p (h i) j"), AX.X,
                                                ALU.add).then_inc(cnt_ready, 1)
                    dve.wait_ge(cnt_ready, TB * b + TB)
                    nc.vector.scalar_tensor_tensor(out=kw[:], in0=cnt[:], scalar=float(WINNERS) - 0.5, in1=k0[:],
                                                   op0=ALU.is_lt, op1=ALU.mult).then_inc(kw_ready, 1)
                    dve.wait_ge(kw_ready, b + 1)
                    nc.vector.tensor_scalar(kout[:], kw[:], w_out[:], None, ALU.mult).then_inc(kout_ready, 1)
                    dve.wait_ge(rt_ready, b + 1)
                    nc.vector.tensor_tensor(rin[:], rt[:], w_in[:].rearrange("p (t l) -> p t l", t=1).broadcast_to([P, TB, P]),
                                            ALU.mult).then_inc(rin_ready, 1)
                    for c in range(TB):
                        n = TB * b + c
                        for g in range(4):
                            dve.wait_ge(a_ready, 4 * n + g + 1)
                            if c < 2:
                                dve.wait_ge(y_ready, TB * b)
                            else:
                                dve.wait_ge(y_ready, n - 1)
                            nc.vector.tensor_tensor(am[c % 2][:, 4 * g:4 * g + 4, :], a_ps[g % 2][:],
                                                    dmask[:].rearrange("p (h l) -> p h l", h=1).broadcast_to([P, 4, P]),
                                                    ALU.mult).then_inc(am_ready, 1)
                        if c + 1 < TB:
                            r = (TB - 1) * b + c
                            dve.wait_ge(u_ready, r + 1)
                            dve.wait_ge(state_ready, r)
                            nc.vector.tensor_tensor(su[:], u_ps[:], hblock[:], ALU.mult).then_inc(su_ready, 1)
                            dve.wait_ge(su_ready, r + 1)
                            dve.wait_ge(y_ready, n + (1 if c else 0))
                            if c == 0:
                                nc.vector.tensor_copy(state[:], su[:]).then_inc(state_ready, 1)
                            else:
                                nc.vector.scalar_tensor_tensor(out=state[:], in0=state[:], scalar=DECAY ** P, in1=su[:],
                                                               op0=ALU.mult, op1=ALU.add).then_inc(state_ready, 1)


def swiglu(nc, m, tag, w1_d, w2_d, w3_d, hidden=4 * P):
    C = hidden // P
    with nc.cleanup_on_exit():
        sb, ps, sem = places(nc, tag)
        w1, w2, w3 = sb("w1", [P, hidden]), sb("w2", [P, hidden]), sb("w3", [P, C, P])
        sg, h = ([sb(f"{n}{u}", [P, S]) for u in range(2)] for n in ("sg", "h"))
        g_ps, u_ps, o_ps = ([ps(f"{n}{u}", [P, S]) for u in range(2)] for n in ("g", "u", "o"))
        loaded, g_ready, u_ready, sg_ready, h_ready, o_ready, o_done, z_ready = (
            sem(n) for n in ("loaded", "g_ready", "u_ready", "sg_ready", "h_ready", "o_ready", "o_done", "z_ready"))
        with nc.Block() as block:
            @block.sync
            def _(sp):
                sp.dma_start(w1[:], w1_d).then_inc(loaded, 16)
                sp.dma_start(w2[:], w2_d).then_inc(loaded, 16)
                sp.dma_start(w3[:], w3_d.rearrange("(c p) m -> p c m", p=P)).then_inc(loaded, 16)

            @block.tensor
            def _(pe):
                pe.wait_ge(loaded, 3 * 16)

                def up(b, c):
                    n = C * b + c
                    if not isinstance(n, int) or n >= 2:
                        pe.wait_ge(sg_ready, n - 1)
                    nc.tensor.matmul(g_ps[c % 2][:], w1[:, c * P:(c + 1) * P], m.zt[:, ts(b, S)], start=True, stop=True).then_inc(g_ready, 1)
                    if not isinstance(n, int) or n >= 2:
                        pe.wait_ge(h_ready, n - 1)
                    nc.tensor.matmul(u_ps[c % 2][:], w2[:, c * P:(c + 1) * P], m.zt[:, ts(b, S)], start=True, stop=True).then_inc(u_ready, 1)

                def batch(b, v, nxt):
                    for c in range(C):
                        if c + 1 < C:
                            up(b, c + 1)
                        elif nxt is not None:
                            up(nxt, 0)
                        pe.wait_ge(h_ready, C * b + c + 1)
                        if c == 0 and not (isinstance(b, int) and b < 2):
                            pe.wait_ge(z_ready, b - 1)
                        nc.tensor.matmul(o_ps[v][:], w3[:, c, :], h[c % 2][:], start=(c == 0), stop=(c == C - 1)).then_inc(o_ready, 1)

                up(0, 0)
                for b in range(B):
                    batch(b, b % 2, b + 1 if b + 1 < B else None)

            @block.scalar
            def _(act):
                nc.scalar.preload_act_table(ACT.Silu)
                for n in range(B * C):
                    act.wait_ge(g_ready, n + 1)
                    if n >= 2:
                        act.wait_ge(h_ready, n - 1)
                    nc.scalar.activation(sg[n % 2][:], g_ps[n % 2][:], ACT.Silu).then_inc(sg_ready, 1)

            @block.vector
            def _(dve):
                for b in range(B):
                    for c in range(C):
                        n = C * b + c
                        dve.wait_ge(sg_ready, n + 1)
                        dve.wait_ge(u_ready, n + 1)
                        if n >= 2:
                            dve.wait_ge(o_ready, n - 1)
                        nc.vector.tensor_tensor(h[c % 2][:], sg[c % 2][:], u_ps[c % 2][:], ALU.mult).then_inc(h_ready, 1)
                    dve.wait_ge(o_ready, C * b + C)
                    nc.vector.tensor_tensor(m.zt[:, b * S:(b + 1) * S], o_ps[b % 2][:], m.xt[:, b * S:(b + 1) * S],
                                            ALU.add).then_inc(z_ready, 1)


def keep_x(nc, m, tag):
    with nc.Block() as block:
        @block.vector
        def _(dve):
            nc.vector.tensor_copy(m.kept[:], m.xt[:])


def add_kept(nc, m, tag):
    with nc.Block() as block:
        @block.vector
        def _(dve):
            nc.vector.tensor_tensor(m.zt[:], m.zt[:], m.kept[:], ALU.add)


def gated_retention_layer(nc, m, tag, a):
    keep_x(nc, m, tag)
    rms_norm(nc, m, tag + "n1", a["n1"])
    spiking_mix(nc, m, tag + "m", a)
    attention_out(nc, m, tag + "o", a["Wo"], a["zero"], a["zero"])
    m.xt, m.zt = m.zt, m.xt
    rms_norm(nc, m, tag + "n2", a["n2"])
    swiglu(nc, m, tag + "s", a["w1"], a["w2"], a["w3"])
    add_kept(nc, m, tag)


DEPTH = 6
DH = 64
INNER = H * DH
W = 32
FT = INNER // P
DI = 341
CH = [(0, P), (P, P), (2 * P, DI - 2 * P)]
TINY = 1e-24
LIFT = 2.0 ** 40
HIDDEN = -1e20


def windowed_layers(nc, m, tag, a):
    keep_x(nc, m, tag)
    with nc.cleanup_on_exit():
        sb, ps, sem = places(nc, tag)
        g = Model()
        g.tab = [sb(f"tab{i}", [P, S]) for i in range(4)]
        g.ltab = [sb(f"ltab{i}", [P, S]) for i in range(4)]
        g.cols = sb("cols", [P, DEPTH * 4])
        g.mask32 = sb("mask32", [P, 2, 2 * P])
        g.mask = sb("mask", [P, 2, 2 * P], BF16)
        g.pair = sb("pair", [P, P])
        g.pair2 = sb("pair2", [P, 2])
        g.consts = sb("consts", [P, 2])
        g.wqkv = sb("wqkv", [P, 3 * INNER])
        g.wrot = sb("wrot", [P, 2 * INNER])
        g.wo = sb("wo", [P, FT, P])
        g.w1 = sb("w1", [P, 2 * DI])
        g.w2 = sb("w2", [P, 3, P])
        g.b1 = sb("b1", [P, 6])
        g.lnb = sb("lnb", [P, 3])
        g.attention_loaded, g.gated_loaded = sem("attention_loaded"), sem("gated_loaded")
        loaded = sem("loaded")
        with nc.Block() as block:
            @block.sync
            def _(sp):
                load_attention(sp, a, g, 0)
                for i in range(4):
                    sp.dma_start(g.tab[i][:], a["tables"][:, i * S:(i + 1) * S]).then_inc(loaded, 16)
                for dst, src in ((g.cols, "cols"), (g.mask32, "mask"), (g.pair, "pair"), (g.pair2, "pair2"), (g.consts, "consts")):
                    sp.dma_start(dst[:], a[src]).then_inc(loaded, 16)
                sp.wait_ge(loaded, 9 * 16)

            @block.vector
            def _(dve):
                dve.wait_ge(loaded, 9 * 16)
                nc.vector.tensor_copy(g.mask[:], g.mask32[:])
        with nc.Fori(0, DEPTH) as layer:
            with nc.cleanup_on_exit():
                windowed_attention(nc, m, tag + "a", a, g, layer)
            with nc.cleanup_on_exit():
                gated_layer(nc, m, tag + "f", a, g, layer)
        with nc.Block() as block:
            @block.sync
            def _(sp):
                sp.wait_ge(g.attention_loaded, ATTENTION_LOADS * 16 * (DEPTH + 1))
    m.xt, m.zt = m.zt, m.xt
    add_kept(nc, m, tag)


ATTENTION_LOADS, GATED_LOADS = 3, 3 + len(CH)


def load_attention(sp, a, g, layer):
    sp.dma_start(g.wqkv[:], a["Wqkv"][ds(layer, 1)].rearrange("l p n -> (l p) n")).then_inc(g.attention_loaded, 16)
    sp.dma_start(g.wrot[:], a["Wrot"][ds(layer, 1)].rearrange("l p n -> (l p) n")).then_inc(g.attention_loaded, 16)
    sp.dma_start(g.wo[:], a["Wo"][ds(layer, 1)].rearrange("l (c p) n -> p (l c) n", p=P)).then_inc(g.attention_loaded, 16)


def load_gated(sp, a, g, layer):
    sp.dma_start(g.w1[:], a["W1"][ds(layer, 1)].rearrange("l p n -> (l p) n")).then_inc(g.gated_loaded, 16)
    sp.dma_start(g.b1[:], a["b1"][:, ds(layer * 6, 6)]).then_inc(g.gated_loaded, 16)
    sp.dma_start(g.lnb[:], a["lnb"][:, ds(layer * 3, 3)]).then_inc(g.gated_loaded, 16)
    for c, (lo, n) in enumerate(CH):
        sp.dma_start(g.w2[0:n, c, :], a["W2"][ds(layer, 1), lo:lo + n, :].rearrange("l p n -> (l p) n")).then_inc(g.gated_loaded, 16)


def windowed_attention(nc, m, tag, a, g, layer):
    sb, ps, sem = places(nc, tag)
    half = P // 2
    wqkv, wrot, wo = g.wqkv, g.wrot, g.wo
    NB = 4
    G, N = NB * FT, NB * FT * TB
    xs = [sb(f"xs{u}", [P, S]) for u in range(NB)]
    v = [sb(f"v{u}", [P, TB, P]) for u in range(2)]
    vev = [sb(f"vev{u}", [P, TB, P]) for u in range(2)]
    sq = [sb(f"sq{i}", [P, S]) for i in range(2)]
    rot = [[sb(f"rot{i}{j}", [P, S]) for j in range(2)] for i in range(2)]
    kraw, nk, lnk, rn = (sb(n, [P, S]) for n in ("kraw", "nk", "lnk", "rn"))
    nq, lnq = sb("nq", [P, TB, 2]), sb("lnq", [P, TB, 2])
    scq = [sb(f"scq{u}", [P, TB, 2]) for u in range(2)]
    qt = [sb(f"qt{u}", [P, S]) for u in range(2)]
    kt = [sb(f"kt{u}", [P, 2, W + S]) for u in range(2)]
    ex = [sb(f"ex{u}", [P, 2, P]) for u in range(2)]
    et = [sb(f"et{u}", [P, 2, P]) for u in range(2)]
    top, ntop = (sb(n, [P, 2, 2]) for n in ("top", "ntop"))
    total, rec = (sb(n, [P, 2, 2 * TB]) for n in ("total", "rec"))
    osb = [sb(f"osb{u}", [P, TB, P]) for u in range(2)]
    ot = sb("ot", [P, FT, S])
    with nc.cleanup_on_exit():
        with nc.Block() as block:
            @block.sync
            def _(sp):
                load_gated(sp, a, g, layer)
                loads = sp.snap(sp.to_reg(ATTENTION_LOADS * 16 * (layer + 1)))
                sp.wait_ge(g.attention_loaded, loads)
                sp.nop(nofuse=True)

            @block.vector
            def _(dve):
                for i in range(4):
                    nc.vector.tensor_scalar(g.ltab[i][:], g.tab[i][:], g.cols[:, ds(layer * 4 + i, 1)], None, ALU.mult)
                for u in range(2):
                    nc.vector.memset(kt[u][:], 0.0)
                    nc.vector.memset(vev[u][half:P, :, :], 0.0)
                for u in range(NB):
                    nc.vector.memset(xs[u][half:P, 0:1], 0.0)

    pr_ps = [ps(f"pr{i}", [P, S]) for i in range(2)]
    n_ps = ps("n", [P, S])
    s_ps = [ps(f"s{u}", [P, S]) for u in range(2)]
    t_ps = [ps(f"t{u}", [P, S]) for u in range(2)]
    o_ps = ps("o", [P, 2 * TB, DH])
    s_view = [s_ps[u][:, 0:2 * P].rearrange("p (e k) -> p e k", e=2) for u in range(2)]
    with nc.Fori(0, B // NB) as round:
      with nc.cleanup_on_exit():
        names = ("xs_ready", "v_made", "v_ready", "vev_ready", "pr_ready", "sq_ready", "rot_ready", "rope_ready",
                 "nq_made", "nq_ready", "lnq_ready", "sc_ready", "nk_made", "nk_ready", "lnk_ready", "rn_ready", "kt_ready",
                 "s_ready", "top_ready", "ntop_ready", "ex_ready", "t_ready", "et_ready", "pv_ready", "rec_ready", "o_ready",
                 "ott_ready", "ot_ready", "z_made", "z_ready")
        xs_ready, v_made, v_ready, vev_ready, pr_ready, sq_ready, rot_ready, rope_ready, nq_made, nq_ready, lnq_ready, \
            sc_ready, nk_made, nk_ready, lnk_ready, rn_ready, kt_ready, s_ready, top_ready, ntop_ready, ex_ready, t_ready, \
            et_ready, pv_ready, rec_ready, o_ready, ott_ready, ot_ready, z_made, z_ready = (sem(n) for n in names)
        with nc.Block() as block:
            @block.tensor
            def _(pe):
                def bank_free(f, i):
                    if i == 1 and f >= 1:
                        pe.wait_ge(v_ready, f)
                    elif i >= 2:
                        pe.wait_ge(rot_ready, 4 * f + i - 1)
                    elif f >= 1:
                        pe.wait_ge(rot_ready, 4 * f)

                def product(f, i):
                    bank_free(f, i)
                    w = wrot if i % 2 else wqkv
                    col = (1 - i // 2) * INNER + (f % FT) * P
                    nc.tensor.matmul(pr_ps[(5 * f + i) % 2][:], w[:, col:col + P], xs[f // FT][:], start=True, stop=True).then_inc(pr_ready, 1)

                def values_product(f):
                    bank_free(f, 4)
                    c = 2 * INNER + (f % FT) * P
                    for t in range(TB):
                        last = nc.tensor.matmul(pr_ps[(5 * f + 4) % 2][:, t * P:(t + 1) * P], xs[f // FT][:, t * P:(t + 1) * P],
                                                wqkv[:, c:c + P], start=True, stop=True)
                    last.then_inc(v_made, 1)

                def norm_k(f):
                    pe.wait_ge(sq_ready, 2 * f + 1)
                    if f >= 1:
                        pe.wait_ge(nq_ready, f)
                    if f >= 4:
                        pe.wait_ge(ot_ready, f - 3)
                    if f > FT + 2:
                        pe.wait_ge(z_ready, (f - 3) // FT)
                    nc.tensor.matmul(n_ps[:], g.pair[:], sq[1][:], start=True, stop=True).then_inc(nk_made, 1)

                def norm_q(f):
                    pe.wait_ge(sq_ready, 2 * f + 2)
                    pe.wait_ge(nk_ready, f + 1)
                    for t in range(TB):
                        last = nc.tensor.matmul(n_ps[:, 2 * t:2 * t + 2], sq[0][:, t * P:(t + 1) * P], g.pair2[:],
                                                start=True, stop=True)
                    last.then_inc(nq_made, 1)

                def scores(n):
                    f, t = n // TB, n % TB
                    if t == 0:
                        pe.wait_ge(rope_ready, 2 * f + 2)
                        pe.wait_ge(kt_ready, 2 * f + 2)
                    if n >= 2:
                        pe.wait_ge(ex_ready, n - 1)
                    q, k, o = qt[f % 2], kt[f % 2], s_view[n % 2]
                    nc.tensor.matmul(o, m.ident_b[:], g.mask[:, min(t, 1), :].rearrange("p (e k) -> p e k", e=2),
                                     start=True, stop=False)
                    at = t * P
                    nc.tensor.matmul(o[0:half, :, 0:half], q[:, at:at + half], k[:, :, W + at:W + at + half], start=False, stop=False)
                    nc.tensor.matmul(o[half:P, :, W:P], q[:, at + half:at + P], k[:, :, W + at + W:W + at + P], start=False, stop=True)
                    nc.tensor.matmul(o[0:half, :, P - W:P], q[:, at:at + half], k[:, :, at:at + W],
                                     start=False, stop=True).then_inc(s_ready, 1)

                def turn(n):
                    pe.wait_ge(ex_ready, n + 1)
                    if n >= 2:
                        pe.wait_ge(et_ready, n - 1)
                    for e in range(2):
                        last = nc.tensor.transpose(t_ps[n % 2][:, e * P:(e + 1) * P], ex[n % 2][:, e, :], m.ident[:])
                    last.then_inc(t_ready, 1)

                def values(n):
                    f, t = n // TB, n % TB
                    pe.wait_ge(et_ready, n + 1)
                    if t == 0:
                        pe.wait_ge(v_ready, f + 1)
                        pe.wait_ge(vev_ready, 2 * f + 2)
                    if t == 0 and f >= 1:
                        pe.wait_ge(o_ready, f)
                    for e in range(2):
                        c = slice(e * DH, (e + 1) * DH)
                        nc.tensor.matmul(o_ps[0:half, 2 * t + e, :], et[n % 2][:, e, 0:half], vev[f % 2][:, t, c], start=True, stop=True)
                        last = nc.tensor.matmul(o_ps[half:P, 2 * t + e, :], et[n % 2][:, e, half:P], v[f % 2][:, t, c], start=True, stop=True)
                    last.then_inc(pv_ready, 1)

                def out_turn(f):
                    pe.wait_ge(o_ready, f + 1)
                    pe.wait_ge(nq_ready, min(f + 4, G))
                    if f >= 1:
                        pe.wait_ge(ot_ready, f)
                    for t in range(TB):
                        last = nc.tensor.transpose(n_ps[:, t * P:(t + 1) * P], osb[f % 2][:, t, :], m.ident[:])
                    last.then_inc(ott_ready, 1)

                def result(i):
                    pe.wait_ge(ot_ready, FT * (i + 1))
                    for f in range(FT):
                        last = nc.tensor.matmul(n_ps[:], wo[:, f, :], ot[:, f, :], start=(f == 0), stop=(f == FT - 1))
                    last.then_inc(z_made, 1)

                pe.wait_ge(xs_ready, 2 * NB)
                for q in range(-2, G):
                    p = q + 2
                    for t in range(TB):
                        n = TB * q + t
                        if n >= 0:
                            turn(n)
                        if n >= 1:
                            values(n - 1)
                        if 0 <= n + 2 < N:
                            scores(n + 2)
                        if t == 0 and q >= 2:
                            out_turn(q - 2)
                        if t == 1 and q >= 2 and (q - 1) % FT == 0:
                            result((q - 1) // FT - 1)
                        if p < G:
                            if t % 2 == 0:
                                product(p, t)
                                product(p, t + 1)
                            elif t == 1:
                                norm_k(p)
                            else:
                                values_product(p)
                                norm_q(p)
                values(N - 1)
                out_turn(G - 2)
                out_turn(G - 1)
                result(NB - 1)

            @block.scalar
            def _(act):
                def squares(f, k):
                    i = 2 * (1 - k)
                    act.wait_ge(pr_ready, 4 * f + i + 1)
                    if f >= 1:
                        act.wait_ge(nk_made if k else nq_made, f)
                    nc.scalar.activation(sq[k][:], pr_ps[(5 * f + i) % 2][:], ACT.Square).then_inc(sq_ready, 1)

                def inverse_q(f):
                    act.wait_ge(nq_ready, f + 1)
                    if f >= 1:
                        act.wait_ge(sc_ready, f)
                    nc.scalar.activation(lnq[:], nq[:], ACT.Ln).then_inc(lnq_ready, 1)
                    act.wait_ge(lnq_ready, f + 1)
                    if f >= 2:
                        act.wait_ge(ex_ready, TB * (f - 1))
                        act.wait_ge(ntop_ready, TB * (f - 1))
                    nc.scalar.activation(scq[f % 2][:], lnq[:], ACT.Exp, scale=-0.5, bias=g.consts[:, 0:1]).then_inc(sc_ready, 1)

                def inverse_k(f):
                    act.wait_ge(nk_ready, f + 1)
                    if f >= 1:
                        act.wait_ge(rn_ready, f)
                    nc.scalar.activation(lnk[:], nk[:], ACT.Ln).then_inc(lnk_ready, 1)
                    act.wait_ge(lnk_ready, f + 1)
                    if f >= 1:
                        act.wait_ge(kt_ready, 2 * f)
                    nc.scalar.activation(rn[:], lnk[:], ACT.Exp, scale=-0.5, bias=g.consts[:, 1:2]).then_inc(rn_ready, 1)

                def exps(n):
                    f, t, u = n // TB, n % TB, n % 2
                    act.wait_ge(ntop_ready, n + 1)
                    if n >= 2:
                        act.wait_ge(t_ready, n - 1)
                    if t == 0 and f >= 2:
                        act.wait_ge(rec_ready, f - 1)
                    for e in range(2):
                        last = nc.scalar.activation(ex[u][:, e, :], s_view[u][:, e, :], ACT.Exp, scale=scq[f % 2][:, t, e:e + 1],
                                                    bias=ntop[:, u, e:e + 1], accum_out=total[:, f % 2, 2 * t + e:2 * t + e + 1])
                    last.then_inc(ex_ready, 1)

                def out_copy(f):
                    act.wait_ge(ott_ready, f + 1)
                    if f >= FT:
                        act.wait_ge(z_made, f // FT)
                    nc.scalar.activation(ot[:, f % FT, :], n_ps[:], ACT.Copy).then_inc(ot_ready, 1)

                nc.scalar.preload_act_table_set(LN_EXP)
                for q in range(-2, G):
                    p = q + 2
                    for t in range(TB):
                        n = TB * q + t
                        if p < G and t % 2:
                            squares(p, 1 if t == 1 else 0)
                        if 0 <= n + 1 < N:
                            exps(n + 1)
                        if t == 0 and q >= 2:
                            out_copy(q - 2)
                        if t == 3 and p < G:
                            inverse_k(p)
                        if t == 1 and 1 <= p <= G:
                            inverse_q(p - 1)
                out_copy(G - 2)
                out_copy(G - 1)

            @block.gpsimd
            def _(pool):
                def keys_and_queries(f):
                    pool.wait_ge(rot_ready, 4 * f + 2)
                    if f >= 1:
                        pool.wait_ge(kt_ready, 2 * f)
                        pool.wait_ge(vev_ready, 2 * f)
                    nc.gpsimd.tensor_tensor(kraw[:], rot[1][0][:], rot[1][1][:], ALU.add).then_inc(rope_ready, 1)
                    pool.wait_ge(rot_ready, 4 * f + 4)
                    pool.wait_ge(rope_ready, 2 * f + 1)
                    if f >= 2:
                        pool.wait_ge(s_ready, TB * (f - 1))
                    nc.gpsimd.tensor_tensor(qt[f % 2][:], rot[0][0][:], rot[0][1][:], ALU.add).then_inc(rope_ready, 1)
                    pool.wait_ge(rn_ready, f + 1)
                    pool.wait_ge(rope_ready, 2 * f + 2)
                    for e in range(2):
                        rows = slice(e * DH, (e + 1) * DH)
                        if e:
                            pool.wait_ge(kt_ready, 2 * f + 1)
                        nc.gpsimd.tensor_tensor(kt[f % 2][rows, e, W:W + S], kraw[rows, :], rn[rows, :], ALU.mult).then_inc(kt_ready, 1)

                for f in range(G):
                    keys_and_queries(f)
                    pool.wait_ge(v_ready, f + 1)
                    pool.wait_ge(kt_ready, 2 * f + 2)
                    if f >= 2:
                        pool.wait_ge(pv_ready, TB * (f - 1))
                    nc.gpsimd.tensor_copy(vev[f % 2][0:half, :, :], v[f % 2][0:half, :, :]).then_inc(vev_ready, 1)
                    pool.wait_ge(vev_ready, 2 * f + 1)
                    nc.gpsimd.tensor_copy(vev[f % 2][P - W:P, 1:TB, :], v[f % 2][P - W:P, 0:TB - 1, :]).then_inc(vev_ready, 1)

            @block.vector
            def _(dve):
                def rotate(f, i):
                    n = 4 * f + i
                    dve.wait_ge(pr_ready, n + 1)
                    if i % 2 == 0:
                        dve.wait_ge(sq_ready, 2 * f + i // 2 + 1)
                    if f >= 1:
                        dve.wait_ge(rope_ready, 2 * f - 1 + i // 2)
                    k = 1 - i // 2
                    nc.vector.tensor_tensor(rot[k][i % 2][:], pr_ps[(5 * f + i) % 2][:], g.ltab[2 * k + i % 2][:], ALU.mult).then_inc(rot_ready, 1)

                def norm_q(f):
                    dve.wait_ge(nq_made, f + 1)
                    if f >= 1:
                        dve.wait_ge(lnq_ready, f)
                    nc.vector.tensor_scalar(nq[:].rearrange("p t e -> p (t e)"), n_ps[:, 0:2 * TB], TINY, LIFT, ALU.max,
                                            ALU.mult).then_inc(nq_ready, 1)

                def norm_k(f):
                    dve.wait_ge(nk_made, f + 1)
                    if f >= 1:
                        dve.wait_ge(lnk_ready, f)
                    nc.vector.tensor_scalar(nk[:], n_ps[:], TINY, LIFT, ALU.max, ALU.mult).then_inc(nk_ready, 1)

                def maximum(n):
                    f, t, u = n // TB, n % TB, n % 2
                    dve.wait_ge(s_ready, n + 1)
                    if n >= 2:
                        dve.wait_ge(ntop_ready, n - 1)
                    nc.vector.tensor_reduce(top[:, u, :], s_view[u], AX.X, ALU.max).then_inc(top_ready, 1)
                    dve.wait_ge(top_ready, n + 1)
                    if t == 0:
                        dve.wait_ge(sc_ready, f + 1)
                    if n >= 2:
                        dve.wait_ge(ex_ready, n - 1)
                    nc.vector.scalar_tensor_tensor(out=ntop[:, u, :], in0=top[:, u, :], scalar=-1.0, in1=scq[f % 2][:, t, :],
                                                   op0=ALU.mult, op1=ALU.mult).then_inc(ntop_ready, 1)

                def copy(n):
                    dve.wait_ge(t_ready, n + 1)
                    if n >= 2:
                        dve.wait_ge(pv_ready, n - 1)
                    nc.vector.tensor_copy(et[n % 2][:].rearrange("p e k -> p (e k)"), t_ps[n % 2][:, 0:2 * P]).then_inc(et_ready, 1)

                def normed(f):
                    dve.wait_ge(ex_ready, TB * f + TB)
                    if f >= 2:
                        dve.wait_ge(o_ready, f - 1)
                    nc.vector.reciprocal(rec[:, f % 2, :], total[:, f % 2, :]).then_inc(rec_ready, 1)
                    dve.wait_ge(rec_ready, f + 1)
                    dve.wait_ge(pv_ready, TB * f + TB)
                    if f >= 2:
                        dve.wait_ge(ott_ready, f - 1)
                    nc.vector.tensor_tensor(osb[f % 2][:].rearrange("p t (e d) -> p (t e) d", e=2), o_ps[:],
                                            rec[:, f % 2, :].rearrange("p (u d) -> p u d", d=1).broadcast_to([P, 2 * TB, DH]),
                                            ALU.mult).then_inc(o_ready, 1)

                def keep_values(f):
                    dve.wait_ge(v_made, f + 1)
                    if f >= 2:
                        dve.wait_ge(pv_ready, TB * (f - 1))
                    src = pr_ps[(5 * f + 4) % 2][:].rearrange("p (t c) -> p t c", t=TB)
                    if f >= 2:
                        dve.wait_ge(vev_ready, 2 * (f - 1))
                    nc.vector.tensor_copy(v[f % 2][:], src).then_inc(v_ready, 1)

                def add(i):
                    at = (round * NB + i) * S
                    dve.wait_ge(z_made, i + 1)
                    nc.vector.tensor_tensor(m.zt[:, ds(at, S)], n_ps[:], m.xt[:, ds(at, S)], ALU.add).then_inc(z_ready, 1)

                for i in range(NB):
                    at = (round * NB + i) * S
                    nc.vector.tensor_copy(xs[i][0:half, :], m.xt[0:half, ds(at, S)]).then_inc(xs_ready, 1)
                    nc.vector.tensor_copy(xs[i][half:P, 1:S], m.xt[half:P, ds(at, S - 1)]).then_inc(xs_ready, 1)
                for q in range(-2, G):
                    p = q + 2
                    for t in range(TB):
                        n = TB * q + t
                        if t == 0 and 1 <= p <= G:
                            norm_q(p - 1)
                        if 0 <= n + 1 < N:
                            maximum(n + 1)
                        if n >= 0:
                            copy(n)
                        if t == 0 and q >= 1:
                            normed(q - 1)
                        if t == 0 and 1 <= p <= G:
                            keep_values(p - 1)
                        if t == 1 and q >= 2 and (q - 1) % FT == 0:
                            add((q - 1) // FT - 1)
                        if p < G:
                            if t % 2:
                                rotate(p, t - 1)
                                rotate(p, t)
                            elif t == 2:
                                norm_k(p)
                normed(G - 1)
                add(NB - 1)


def gated_layer(nc, m, tag, a, g, layer):
    sb, ps, sem = places(nc, tag)
    w1, w2, b1, lnb = g.w1, g.w2, g.b1, g.lnb
    w1g = sb("w1g", [P, 2 * DI])
    bias = sb("bias", [P, 6])
    xn = sb("xn", [P, T])
    b_ps = ps("b", [P, 6])
    half = P // 2
    with nc.Block() as block:
        @block.sync
        def _(sp):
            loads = sp.snap(sp.to_reg(GATED_LOADS * 16 * (layer + 1)))
            sp.wait_ge(g.gated_loaded, loads)
            sp.nop(nofuse=True)
    with nc.cleanup_on_exit():
        bias_made, edge = sem("bias_made"), sem("edge")
        zero_ready = sem("zero_ready")
        with nc.Block() as block:
            @block.sync
            def _(sp):
                load_attention(sp, a, g, (layer + 1) % DEPTH)

            @block.gpsimd
            def _(pool):
                nc.gpsimd.memset(xn[half:P, :].rearrange("p (b s) -> p b s", b=B)[:, :, 0:1], 0.0).then_inc(edge, 1)

            @block.vector
            def _(dve):
                for i in range(B):
                    nc.vector.tensor_copy(xn[half:P, i * S + 1:(i + 1) * S], m.zt[half:P, i * S:(i + 1) * S - 1])
                nc.vector.memset(bias[:], 0.0).then_inc(zero_ready, 1)
                nc.vector.tensor_scalar(w1g[:], w1[:], lnb[:, 0:1], None, ALU.mult)
                dve.wait_ge(bias_made, 1)
                dve.wait_ge(zero_ready, 1)
                for i in range(6):
                    n = CH[i % 3][1]
                    nc.vector.tensor_tensor(bias[0:n, i:i + 1], b_ps[0:n, i:i + 1], b1[0:n, i:i + 1], ALU.add)

            @block.scalar
            def _(act):
                nc.scalar.activation(xn[0:half, :], m.zt[0:half, :], ACT.Copy)

            @block.tensor
            def _(pe):
                for i in range(6):
                    lo, n = CH[i % 3]
                    lo += (i // 3) * DI
                    last = nc.tensor.matmul(b_ps[0:n, i:i + 1], w1[:, lo:lo + n], lnb[:, 1:2], start=True, stop=True)
                last.then_inc(bias_made, 1)
    layer_norm(nc, m, tag + "n", xn, xn)
    with nc.cleanup_on_exit():
        ge, h = ([sb(f"{n}{i}", [P, S]) for i in range(3)] for n in ("ge", "h"))
        g_ps, a_ps = ([ps(f"{n}{i}", [P, S]) for i in range(3)] for n in ("g", "a"))
        o_ps = ps("o", [P, S])
        g_ready, ge_ready, a_ready, h_ready, o_ready, x_ready = (
            sem(n) for n in ("g_ready", "ge_ready", "a_ready", "h_ready", "o_ready", "x_ready"))
        with nc.Block() as block:
            @block.tensor
            def _(pe):
                def up(i, c):
                    lo, n = CH[c]
                    if i:
                        pe.wait_ge(ge_ready, 3 * (i - 1) + c + 1)
                    nc.tensor.matmul(g_ps[c][0:n, :], w1g[:, DI + lo:DI + lo + n], xn[:, i * S:(i + 1) * S],
                                     start=True, stop=True).then_inc(g_ready, 1)
                    if i:
                        pe.wait_ge(h_ready, 3 * (i - 1) + c + 1)
                    nc.tensor.matmul(a_ps[c][0:n, :], w1g[:, lo:lo + n], xn[:, i * S:(i + 1) * S],
                                     start=True, stop=True).then_inc(a_ready, 1)

                for c in range(3):
                    up(0, c)
                for i in range(B):
                    for c in range(3):
                        n = CH[c][1]
                        pe.wait_ge(h_ready, 3 * i + c + 1)
                        if c == 0 and i:
                            pe.wait_ge(x_ready, i)
                        nc.tensor.matmul(o_ps[:], w2[0:n, c, :], h[c][0:n, :], start=(c == 0), stop=(c == 2)).then_inc(o_ready, 1)
                        if i + 1 < B:
                            up(i + 1, c)

            @block.scalar
            def _(act):
                nc.scalar.preload_act_table(ACT.Gelu)
                for i in range(B):
                    for c in range(3):
                        n = CH[c][1]
                        act.wait_ge(g_ready, 3 * i + c + 1)
                        if i:
                            act.wait_ge(h_ready, 3 * (i - 1) + c + 1)
                        nc.scalar.activation(ge[c][0:n, :], g_ps[c][0:n, :], ACT.Gelu, bias=bias[0:n, 3 + c:4 + c]).then_inc(ge_ready, 1)

            @block.vector
            def _(dve):
                for i in range(B):
                    for c in range(3):
                        n = CH[c][1]
                        dve.wait_ge(ge_ready, 3 * i + c + 1)
                        dve.wait_ge(a_ready, 3 * i + c + 1)
                        if i:
                            dve.wait_ge(o_ready, 3 * (i - 1) + c + 1)
                        nc.vector.scalar_tensor_tensor(out=h[c][0:n, :], in0=a_ps[c][0:n, :], scalar=bias[0:n, c:c + 1],
                                                       in1=ge[c][0:n, :], op0=ALU.add, op1=ALU.mult).then_inc(h_ready, 1)
                    dve.wait_ge(o_ready, 3 * i + 3)
                    nc.vector.scalar_tensor_tensor(out=m.xt[:, i * S:(i + 1) * S], in0=o_ps[:], scalar=lnb[:, 2:3],
                                                   in1=m.zt[:, i * S:(i + 1) * S], op0=ALU.add, op1=ALU.add).then_inc(x_ready, 1)


def model(nc, a):
    m = Model()
    m.xt, m.zt, m.kept, m.ident, m.mean_w, m.eps, m.hm = (
        nc.alloc_sbuf_tensor(f"model_{name}", shape, F32) for name, shape in
        (("xt", [P, T]), ("zt", [P, T]), ("kept", [P, T]), ("ident", [P, P]), ("mean_w", [P, P]), ("eps", [P, 1]), ("hm", [P, H])))
    m.ident_b = nc.alloc_sbuf_tensor("model_ident_b", [P, P], BF16)
    scratch = [nc.dram_tensor(f"scratch{u}", [S * (S + 1)], F32).ap() for u in range(2)]
    with nc.cleanup_on_exit():
        loaded = nc.alloc_semaphore("model_loaded")
        with nc.Block() as block:
            @block.sync
            def _(sp):
                for dst, name in ((m.xt, "x"), (m.ident, "ident"), (m.mean_w, "mean_w"), (m.eps, "eps"), (m.hm, "hm")):
                    sp.dma_start(dst[:], a[name]).then_inc(loaded, 16)
                sp.wait_ge(loaded, 5 * 16)

            @block.vector
            def _(dve):
                dve.wait_ge(loaded, 5 * 16)
                nc.vector.tensor_copy(m.ident_b[:], m.ident[:])

    def of(prefix):
        return {name[len(prefix):]: ap for name, ap in a.items() if name.startswith(prefix)}

    relative_attention(nc, m, "l0a", of("L0_attn_"), scratch)
    attention_out(nc, m, "l0o", a["L0_attn_Wo"], a["L0_attn_bv"], a["L0_attn_bo"])
    layer_norm(nc, m, "n0")
    channel_mix(nc, m, "l0f", *(a["L0_ffn_" + n] for n in ("W_r", "W_k", "W_v", "mu_r", "mu_k")))
    layer_norm(nc, m, "n1")
    batch_softmax_attention(nc, m, "l1a", *(a["L1_attn_" + n] for n in ("w_q", "w_k", "w_v", "W_o")), a["zero"])
    layer_norm(nc, m, "n2")
    experts(nc, m, "l1f", of("L1_ffn_"))
    layer_norm(nc, m, "n3")
    linear_attention(nc, m, "l2a", *(a["L2_attn_" + n] for n in ("Wq", "Wk", "Wv", "bq", "bk", "bv")))
    layer_norm(nc, m, "n4")
    windowed_layers(nc, m, "l2f", of("L2_ffn_"))
    layer_norm(nc, m, "n5")
    gated_retention_layer(nc, m, "l3a", {**of("L3_attn_"), "zero": a["zero"]})
    layer_norm(nc, m, "n6")
    channel_mix(nc, m, "l3f", *(a["L3_ffn_" + n] for n in ("W_r", "W_k", "W_v", "mu_r", "mu_k")))
    layer_norm(nc, m, "n7")
    with nc.cleanup_on_exit():
        stored = nc.alloc_semaphore("model_stored")
        with nc.Block() as block:
            @block.sync
            def _(sp):
                sp.dma_start(a["out"], m.xt[:]).then_inc(stored, 16)
                sp.wait_ge(stored, 16)


def shape_constants():
    f = np.float32
    i = np.arange(P)
    c = {"ident": np.eye(P, dtype=f), "mean_w": np.full((P, P), 1 / P, f), "eps": np.full((P, 1), EPS, f),
         "zero": np.zeros((P, 1), f), "hm": (i[:, None] // HD == np.arange(H)[None]).astype(f)}
    inv = (1.0 / 10000.0 ** (2.0 * np.arange(P // 2, dtype=f) / P)).astype(f)
    ang = np.arange(S, dtype=f)[:, None] * inv[None]
    c["L0_attn_feat"] = np.concatenate([np.sin(ang), np.cos(ang)], -1).T
    c["L1_ffn_before"] = np.triu(np.ones((P, P), f))
    c["L1_ffn_first"] = np.broadcast_to(np.arange(E, 0, -1), (P, E))
    half = np.arange(0, DH, 2, dtype=f)
    freqs = np.arange(S, dtype=f)[:, None] * (f(1) / f(10000) ** (half / f(DH))).astype(f)[None]
    freqs = np.concatenate([freqs, freqs], -1)
    base = ((half + f(0.4 * DH)) / f(1.4 * DH)).astype(f)
    power = ((np.arange(S, dtype=f) - f(S // 2)) / f(W // 2)).astype(f)
    scale = (base[None] ** power[:, None]).astype(f)
    scale = np.concatenate([scale, scale], -1)
    cos, sin = np.cos(freqs), np.sin(freqs) * np.where(np.arange(DH) < DH // 2, -1, 1).astype(f)
    c["L2_ffn_tables"] = np.concatenate([np.tile(x.T, (2, 1)) for x in (cos * scale, sin * scale, cos / scale, sin / scale)], 1)
    row, column = i[:, None], np.arange(P)[None]
    own = (column <= row) & (row - column <= W)
    before = (row < P // 2) & (column >= P - W) & (column >= row + P - W)
    c["L2_ffn_mask"] = np.stack([np.tile(np.where(seen, 0, HIDDEN), (1, 2)) for seen in (own, own | before)], 1)
    c["L2_ffn_pair"] = i[:, None] // DH == i[None] // DH
    c["L2_ffn_pair2"] = i[:, None] // DH == np.arange(2)[None]
    c["L2_ffn_consts"] = np.tile([np.log(8) + np.log(LIFT) / 2, np.log(LIFT) / 2], (P, 1))
    c["L3_attn_w_in"] = np.broadcast_to(f(DECAY) ** (i + 1), (P, P))
    c["L3_attn_w_out"] = (f(DECAY) ** (P - 1 - i))[:, None]
    ahead = i[None] - i[:, None]
    c["L3_attn_dmask"] = np.where(ahead >= 0, DECAY ** np.maximum(ahead, 0), 0)
    c["L3_attn_hblock"] = i[:, None] // HD == i[None] // HD
    return {name: np.ascontiguousarray(v, dtype=f) for name, v in c.items()}


def layouts(d):
    a = {n: v for n, v in d.items()}
    a["x"] = a.pop("L0_attn_x").reshape(T, P).T
    for n in ("W_r", "W_k", "W_v"):
        for layer in ("L0_ffn_", "L3_ffn_"):
            a[layer + n] = d[layer + n].T
    for n in ("Wq", "Wk", "Wv"):
        a["L2_attn_" + n] = d["L2_attn_" + n].T
    a["L2_attn_bq"] = np.broadcast_to(d["L2_attn_bq"], (P, P))
    for n in ("bq", "bk", "bv", "bp", "bo", "u", "v"):
        a["L0_attn_" + n] = d["L0_attn_" + n].reshape(P, 1)
    for n in ("L0_ffn_mu_r", "L0_ffn_mu_k", "L3_ffn_mu_r", "L3_ffn_mu_k", "L2_attn_bk", "L2_attn_bv"):
        a[n] = d[n].reshape(P, 1)
    a["L3_attn_n1"], a["L3_attn_n2"] = a.pop("L3_attn_norm1_w").reshape(P, 1), a.pop("L3_attn_norm2_w").reshape(P, 1)
    a["L1_ffn_b1"] = d["L1_ffn_b1"].reshape(E, FF // P, P).transpose(2, 0, 1).reshape(P, E * FF // P)
    other = np.arange(DH) ^ (DH // 2)
    q_k = d["L2_ffn_Wqkv"][:, :, :2 * INNER]
    a["L2_ffn_Wrot"] = q_k.reshape(DEPTH, P, 2 * H, DH)[..., other].reshape(DEPTH, P, 2 * INNER)
    scales = (a.pop("L2_ffn_q_scale"), a.pop("L2_ffn_k_scale"))
    cols = np.stack([np.tile(v[:, o], (1, 2)) for v in scales for o in (slice(None), other)], 1)
    a["L2_ffn_cols"] = cols.transpose(2, 0, 1).reshape(P, DEPTH * 4)
    b1 = np.zeros((DEPTH, 6, P), np.float32)
    for k in range(6):
        lo, n = CH[k % 3]
        b1[:, k, :n] = d["L2_ffn_b1"][:, (k // 3) * DI + lo:(k // 3) * DI + lo + n]
    a["L2_ffn_b1"] = b1.transpose(2, 0, 1).reshape(P, DEPTH * 6)
    lnb = np.stack([a.pop("L2_ffn_" + n) for n in ("ln_g", "ln_b", "b2")], 1)
    a["L2_ffn_lnb"] = lnb.transpose(2, 0, 1).reshape(P, DEPTH * 3)
    return {n: np.ascontiguousarray(v) for n, v in a.items()}


def kernel(**inputs):
    import concourse.bacc as bacc
    from concourse.bass_utils import run_bass_kernel_spmd as run

    arrays = {**layouts({n: np.asarray(v) for n, v in inputs.items()}), **shape_constants()}
    nc = bacc.Bacc("TRN2", target_bir_lowering=False, num_devices=1)
    args = {n: nc.dram_tensor(f"in_{n}", v.shape, mybir.dt.from_np(v.dtype), kind="ExternalInput").ap()
            for n, v in arrays.items()}
    args["out"] = nc.dram_tensor("out", [P, T], F32, kind="ExternalOutput").ap()
    model(nc, args)
    result = run(nc, [{f"in_{n}": v for n, v in arrays.items()}], core_ids=[0]).results[0]["out"]
    return np.ascontiguousarray(result.T).reshape(B, S, P)
```
